# Optimizing a Trainium2 kernel written in Bass

```python
import numpy as np
import jax
import jax.numpy as jnp

def _softmax(x, axis=-1):
    return jax.nn.softmax(x, axis=axis)
def _gelu(x):
    return jax.nn.gelu(x, approximate=True)
def _silu(x):
    return jax.nn.silu(x)
def _sigmoid(x):
    return jax.nn.sigmoid(x)
def _layernorm(x, axis=-1, eps=1e-5):
    m = jnp.mean(x, axis=axis, keepdims=True)
    v = jnp.var(x, axis=axis, keepdims=True)
    return (x - m) / jnp.sqrt(v + eps)
def _scatter_add(tgt, idx, src, axis=0):
    return tgt.at[idx].add(src)
def _segment_sum(src, seg, n):
    return jax.ops.segment_sum(src, seg, n)

kernel_name = 'mk_adj_preln_d1_adj_256_27af99'

def setup_inputs(seed: int = 0):
    np.random.seed(seed)
    _w = jnp.asarray
    def _rec_inputs():
        import jax
        import jax.numpy as jnp
        _gk = jax.random.key(seed)
        x = 7.22e-05 + 1 * jax.random.normal(jax.random.fold_in(_gk, 1), (32, 512, 256), jnp.float32)
        _w = (1.0 + jnp.arange(512, dtype=jnp.float32)) ** -0.5
        _w = _w / _w.mean()
        _pij = jnp.clip(0.015625 * _w[:, None] * _w[None, :], 0.0, 1.0)
        _a = jax.random.uniform(jax.random.fold_in(_gk, 2), (32, 512, 512)) < _pij
        _a = jnp.logical_or(_a, jnp.swapaxes(_a, -1, -2))
        _a = jnp.logical_or(_a, jnp.eye(512, dtype=bool))
        _af = _a.astype(jnp.float32)
        adj = _af
        return x, adj
    x, adj = _rec_inputs()
    def _L0_gnn_setup():
        import jax, jax.numpy as jnp
        import numpy as np
        from jax import lax
        DIM = 256
        EPS = 1e-05

        def _bn(h, g, b, m, v):
            scale = g / jnp.sqrt(v + EPS)
            return h * scale[None, :, None] + (b - m * scale)[None, :, None]

        def _conv1d(h, w, pad):
            return lax.conv_general_dilated(h, w, window_strides=(1,), padding=[(pad, pad)], dimension_numbers=('NCH', 'OIH', 'NCH'))
        key = jax.random.key(seed)
        ks = jax.random.split(key, 16)
        bs, n, d = (16, 2048, DIM)
        s = 0.05
        return {'x': jax.random.normal(ks[0], (bs, n, d), jnp.float32), 'mask': jnp.ones((bs, n, n), jnp.float32), 'w_se': jax.random.normal(ks[1], (3, d), jnp.float32) * s, 'b_se': jnp.zeros((3,), jnp.float32), 'conv1_w': jax.random.normal(ks[2], (d, d, 1), jnp.float32) * s, 'bn1_g': jnp.ones((d,), jnp.float32), 'bn1_b': jnp.zeros((d,), jnp.float32), 'bn1_m': jnp.zeros((d,), jnp.float32), 'bn1_v': jnp.ones((d,), jnp.float32), 'conv2_w': jax.random.normal(ks[3], (d, d, 17), jnp.float32) * s, 'bn2_g': jnp.ones((d,), jnp.float32), 'bn2_b': jnp.zeros((d,), jnp.float32), 'bn2_m': jnp.zeros((d,), jnp.float32), 'bn2_v': jnp.ones((d,), jnp.float32), 'w_msg': jax.random.normal(ks[4], (d, d), jnp.float32) * s, 'b_msg': jnp.zeros((d,), jnp.float32), 'w_ih': jax.random.normal(ks[5], (3 * d, 2 * d), jnp.float32) * s, 'b_ih': jnp.zeros((3 * d,), jnp.float32), 'w_hh': jax.random.normal(ks[6], (3 * d, d), jnp.float32) * s, 'b_hh': jnp.zeros((3 * d,), jnp.float32)}
    _L0_gnn_all = _L0_gnn_setup()
    _L0_gnn_in = {k: v for k, v in _L0_gnn_all.items() if k in ('w_se', 'b_se', 'conv1_w', 'bn1_g', 'bn1_b', 'bn1_m', 'bn1_v', 'conv2_w', 'bn2_g', 'bn2_b', 'bn2_m', 'bn2_v', 'w_msg', 'b_msg', 'w_ih', 'b_ih', 'w_hh', 'b_hh', )}
    del _L0_gnn_all

    return {
        "x": x,
        "adj": adj,
        "L0_gnn_w_se": _L0_gnn_in["w_se"],
        "L0_gnn_b_se": _L0_gnn_in["b_se"],
        "L0_gnn_conv1_w": _L0_gnn_in["conv1_w"],
        "L0_gnn_bn1_g": _L0_gnn_in["bn1_g"],
        "L0_gnn_bn1_b": _L0_gnn_in["bn1_b"],
        "L0_gnn_bn1_m": _L0_gnn_in["bn1_m"],
        "L0_gnn_bn1_v": _L0_gnn_in["bn1_v"],
        "L0_gnn_conv2_w": _L0_gnn_in["conv2_w"],
        "L0_gnn_bn2_g": _L0_gnn_in["bn2_g"],
        "L0_gnn_bn2_b": _L0_gnn_in["bn2_b"],
        "L0_gnn_bn2_m": _L0_gnn_in["bn2_m"],
        "L0_gnn_bn2_v": _L0_gnn_in["bn2_v"],
        "L0_gnn_w_msg": _L0_gnn_in["w_msg"],
        "L0_gnn_b_msg": _L0_gnn_in["b_msg"],
        "L0_gnn_w_ih": _L0_gnn_in["w_ih"],
        "L0_gnn_b_ih": _L0_gnn_in["b_ih"],
        "L0_gnn_w_hh": _L0_gnn_in["w_hh"],
        "L0_gnn_b_hh": _L0_gnn_in["b_hh"],
    }

def reference(x, adj, L0_gnn_w_se, L0_gnn_b_se, L0_gnn_conv1_w, L0_gnn_bn1_g, L0_gnn_bn1_b, L0_gnn_bn1_m, L0_gnn_bn1_v, L0_gnn_conv2_w, L0_gnn_bn2_g, L0_gnn_bn2_b, L0_gnn_bn2_m, L0_gnn_bn2_v, L0_gnn_w_msg, L0_gnn_b_msg, L0_gnn_w_ih, L0_gnn_b_ih, L0_gnn_w_hh, L0_gnn_b_hh):
    import jax
    import jax.numpy as jnp
    def _L0_gnn_ref(x, mask, w_se, b_se, conv1_w, bn1_g, bn1_b, bn1_m, bn1_v, conv2_w, bn2_g, bn2_b, bn2_m, bn2_v, w_msg, b_msg, w_ih, b_ih, w_hh, b_hh):
        import jax, jax.numpy as jnp
        import numpy as np
        from jax import lax
        DIM = 256
        EPS = 1e-05

        def _bn(h, g, b, m, v):
            scale = g / jnp.sqrt(v + EPS)
            return h * scale[None, :, None] + (b - m * scale)[None, :, None]

        def _conv1d(h, w, pad):
            return lax.conv_general_dilated(h, w, window_strides=(1,), padding=[(pad, pad)], dimension_numbers=('NCH', 'OIH', 'NCH'))
        d = x.shape[-1]
        xc = jnp.transpose(x, (0, 2, 1))
        h = _bn(_conv1d(xc, conv1_w, 0), bn1_g, bn1_b, bn1_m, bn1_v)
        h = jax.nn.relu(h)
        h = _bn(_conv1d(h, conv2_w, 8), bn2_g, bn2_b, bn2_m, bn2_v)
        x_conv = jnp.transpose(jax.nn.relu(h + xc), (0, 2, 1))
        s = x @ w_se.T + b_se
        sq = jnp.sum(s * s, axis=-1)
        dist = sq[:, :, None] + sq[:, None, :] - 2.0 * jnp.einsum('bnd,bmd->bnm', s, s)
        A = jnp.exp(-dist) * mask
        msg = jax.nn.relu(x @ w_msg.T + b_msg)
        x_nmp = jnp.einsum('bnm,bmd->bnd', A, msg)
        x_in = jnp.concatenate([x_conv, x_nmp], axis=-1)
        gi = x_in @ w_ih.T + b_ih
        gh = x @ w_hh.T + b_hh
        gi_r, gi_z, gi_n = (gi[..., :d], gi[..., d:2 * d], gi[..., 2 * d:])
        gh_r, gh_z, gh_n = (gh[..., :d], gh[..., d:2 * d], gh[..., 2 * d:])
        r = jax.nn.sigmoid(gi_r + gh_r)
        z = jax.nn.sigmoid(gi_z + gh_z)
        nn_ = jnp.tanh(gi_n + r * gh_n)
        return (1.0 - z) * nn_ + z * x

    h = jnp.maximum(_layernorm(x, axis=-1), 0.0)
    x = x + _L0_gnn_ref(h, adj, L0_gnn_w_se, L0_gnn_b_se, L0_gnn_conv1_w, L0_gnn_bn1_g, L0_gnn_bn1_b, L0_gnn_bn1_m, L0_gnn_bn1_v, L0_gnn_conv2_w, L0_gnn_bn2_g, L0_gnn_bn2_b, L0_gnn_bn2_m, L0_gnn_bn2_v, L0_gnn_w_msg, L0_gnn_b_msg, L0_gnn_w_ih, L0_gnn_b_ih, L0_gnn_w_hh, L0_gnn_b_hh)
    return x


_drawn_inputs = setup_inputs


def setup_inputs(seed=0):
    import zlib

    import numpy as np

    out = dict(_drawn_inputs(seed))
    spreads = {'L0_gnn_b_se': (0.0, 0.8),
     'L0_gnn_bn1_g': (1.0, 0.2),
     'L0_gnn_bn1_b': (0.0, 0.1),
     'L0_gnn_bn1_m': (0.0, 0.1),
     'L0_gnn_bn1_v': (1.0, 0.6),
     'L0_gnn_bn2_g': (1.0, 0.2),
     'L0_gnn_bn2_b': (0.0, 0.526),
     'L0_gnn_bn2_m': (0.0, 0.425),
     'L0_gnn_bn2_v': (1.0, 0.6),
     'L0_gnn_b_msg': (0.0, 0.1),
     'L0_gnn_b_ih': (0.0, 0.295),
     'L0_gnn_b_hh': (0.0, 0.413)}
    factors = {}
    for name, (base, spread) in spreads.items():
        noise = np.random.default_rng([zlib.crc32(name.encode()), seed]).standard_normal(out[name].shape)
        drawn = base * np.exp(spread * noise) if base else spread * noise
        out[name] = jnp.asarray(drawn.astype(out[name].dtype))
    for name, factor in factors.items():
        out[name] = (out[name] * factor).astype(out[name].dtype)
    return out
```

```python
from contextlib import ExitStack

import concourse.bass as bass
import numpy as np
from concourse import mybir

DT = mybir.dt
F32, F16, F32R, I32 = DT.float32, DT.float16, DT.float32r, DT.int32
ALU = mybir.AluOpType
ACT = mybir.ActivationFunctionType
AX = mybir.AxisListType

P = 128
B, N, D = 32, 512, 256
KD = D // P
NB = N // P
EPS = 1e-5
H_TOP = 11
H_SCALE = float(2 ** H_TOP)
TAPS, PAD = 17, 8
G = 4
NGROUP = B // G
Q = N // 4
QW = (N + 2 * PAD) // 4
CW = KD * G * QW
W_TOP = 14
W2_TOP = 12
Y_TOP = 12
TINY = 1e-18
EXPO = 0x7F800000
PTAPS = [5, 5, 4, 5, 5, 4, 4, 4, 4]
NPROD = len(PTAPS)
TAP0 = [sum(PTAPS[:p]) for p in range(NPROD)]
NTAP = sum(PTAPS)
EV = NPROD * KD
SUMS = 10
S_ROWS = [0, 3, 6, 64, 67, 70, 73]
SQ = 32


def distance_rows():
    t = np.zeros((P, 6), np.float32)
    ar, br, cr, al, bl, cl = range(6)
    t[0:3, ar] = 1
    t[3:6, ar], t[3:6, br] = -1, 1
    t[6:9, ar] = 1
    t[0:6, al] = 2
    t[6:9, al], t[6:9, bl] = -2, 2
    t[64:67, ar] = 1
    t[67:70, ar], t[67:70, br] = -1, 1
    t[64:70, cl] = -1
    t[70:73, al] = -1
    t[73:76, al], t[73:76, bl] = 1, -1
    t[70:76, cr] = 1
    return t


def count(index, per, k=0):
    base, off = index
    return base * per + (off * per + k)


def wait(eng, sem, value):
    if isinstance(value, int) and value <= 0:
        return
    eng.wait_ge(sem, value)


def tap_source(raw, fa, s4, p):
    last = (raw[:, :, TAPS - 1:TAPS], 1)
    ph = lambda c: (raw[:, :, c:c + 13:4], 4)
    return {
        0: [(s4[:, :, 0:4], 4), last],
        1: [(fa[:, :, 0:7:2], 4), last],
        2: [(fa[:, :, 1:8:2], 4)],
        3: [(s4[:, :, 4:8], 4), last],
        4: [ph(0), last],
        5: [ph(2)],
        6: [(s4[:, :, 8:12], 4)],
        7: [ph(1)],
        8: [ph(3)],
    }[p]


def rsqrt_step(eng, link, out, root, value, tmp):
    link(eng.reciprocal(out, root))
    link(eng.tensor_tensor(tmp, out, out, ALU.mult))
    link(eng.tensor_tensor(tmp, tmp, value, ALU.mult))
    link(eng.tensor_scalar(tmp, tmp, -0.5, 1.5, ALU.mult, ALU.add))
    link(eng.tensor_tensor(out, out, tmp, ALU.mult))


def power_scale(eng, link, biggest, power, scale, inverse, top):
    link(eng.tensor_scalar(biggest, biggest, TINY, None, ALU.max))
    link(eng.tensor_scalar(power.bitcast(I32), biggest.bitcast(I32), EXPO, None, ALU.bitwise_and))
    link(eng.reciprocal(scale, power))
    link(eng.tensor_scalar(scale, scale, float(2.0 ** top), None, ALU.mult))
    link(eng.tensor_scalar(inverse, power, float(2.0 ** -top), None, ALU.mult))


def convolution_phase(nc, io, scratch, shared):
    ident, h_scratch = shared["ident"], shared["h_scratch"]
    by_group = scratch.rearrange("(r g) k p n -> r k p g n", g=G)
    h_by_batch = h_scratch.rearrange("b k p n -> b p k n")
    ctx = ExitStack()
    with ctx:
        sb = lambda name, shape, dt=F32: ctx.enter_context(nc.sbuf_tensor(name, shape, dt))
        sem = lambda name: ctx.enter_context(nc.semaphore(name))
        w2h = sb("w2h", [P, NTAP, KD, D], F16)
        w2l = sb("w2l", [P, NTAP, KD, D], F16)
        w1h = sb("w1h", [P, KD, D], F16)
        w1l = sb("w1l", [P, KD, D], F16)
        conv1_scale = sb("conv1_scale", [P, KD])
        conv1_bias = sb("conv1_bias", [P, KD])
        conv2_scale = sb("conv2_scale", [P, KD])
        conv2_bias = sb("conv2_bias", [P, KD])

        with ExitStack() as tmp:
            tb = lambda name, shape, dt=F32: tmp.enter_context(nc.sbuf_tensor(name, shape, dt))
            raw2 = [tb(f"raw2_{o}", [P, D, TAPS]) for o in range(KD)]
            fa = tb("fa", [P, D, 8])
            s4 = tb("s4", [P, D, 12])
            raw1 = tb("raw1", [P, KD, D])
            sq_junk = tb("sq_junk", [P, D])
            vec = tb("vec", [P, 8, KD])
            ones = tb("ones", [P, P])
            diag = tb("diag", [P, P])
            names = "work1 norm2 norm w1max w1pow w1scale w1inv w2max w2pow w2scale w2inv bound"
            small = {n: tb(n, [P, KD]) for n in names.split()}
            veps = tb("veps2", [P, 2, KD])
            root = tb("root2", [P, 2, KD])
            bn = tb("bn2", [P, 2, KD])
            work = tb("work2", [P, 2, KD])
            ymax, ypow, yscale, yinv = (tb(n, [P, 1]) for n in ("ymax", "ypow", "yscale", "yinv"))
            bank = [tmp.enter_context(nc.psum_tensor(f"wt{i}", [P, 4, P], F32)) for i in range(4)]
            bound_row = tmp.enter_context(nc.psum_tensor("bound_row", [P, KD, P], F32))
            names = ("vec_in raw1_in raw2_in0 raw2_in1 id_in dve_step act_step veps_ready root_ready "
                     "w1_scaled w2_scaled sums_ready bound_ready norm_ready "
                     "diag_ready row_ready turned high_ready rest_ready")
            s = {n: tmp.enter_context(nc.semaphore(n)) for n in names.split()}
            units = []
            for ob in range(KD):
                for ib in range(KD):
                    for p in range(NPROD):
                        units.append((ob, ib, p))
            block = tmp.enter_context(nc.Block())

            def unit_taps(ob, ib, p):
                out, t = [], TAP0[p]
                for view, n in tap_source(raw2[ob], fa, s4, p):
                    for k in range(n):
                        out.append((t, view[:, ib * P:(ib + 1) * P, k]))
                        t += 1
                return out

            chunks = []
            for ob, ib, p in units:
                taps = list(range(TAP0[p], TAP0[p] + PTAPS[p]))
                chunks.append((ob, ib, p, 0, 4))
                if len(taps) == 5:
                    chunks.append((ob, ib, p, 4, 1))

            @block.sync
            def _(sp):
                sp.dma_start(ident[:, :], io["ident"]).then_inc(s["id_in"], 16)
                sp.dma_start(raw1[:, :, :], io["conv1_w"].rearrange("(ob p) i k -> p ob (i k)", p=P)).then_inc(s["raw1_in"], 16)
                for ob in range(KD):
                    src = io["conv2_w"][ob * P:(ob + 1) * P, :, :]
                    sp.dma_start(raw2[ob][:, :, :], src).then_inc(s[f"raw2_in{ob}"], 16)

            @block.gpsimd
            def _(pool):
                with nc.allow_non_contiguous_dma(reason="256-element vectors"):
                    for j, n in enumerate(("bn1_g", "bn1_b", "bn1_m", "bn1_v", "bn2_g", "bn2_b", "bn2_m", "bn2_v")):
                        pool.dma_start(vec[:, j, :], io[n].rearrange("(k p) -> p k", p=P)).then_inc(s["vec_in"], 16)

            @block.scalar
            def _(act):
                act.wait_ge(s["raw1_in"], 16)
                act.wait_ge(s["w1_scaled"], 1)
                for ob in range(KD):
                    if ob:
                        act.wait_ge(s["act_step"], ob)
                    nc.scalar.activation(sq_junk[:, :], raw1[:, ob, :], ACT.Square,
                                         accum_out=small["norm2"][:, ob:ob + 1]).then_inc(s["act_step"], 1)
                act.wait_ge(s["act_step"], KD)
                nc.scalar.activation(small["norm"][:, :], small["norm2"][:, :], ACT.Sqrt).then_inc(s["norm_ready"], 1)
                act.wait_ge(s["veps_ready"], 1)
                nc.scalar.activation(root[:, :, :], veps[:, :, :], ACT.Sqrt).then_inc(s["root_ready"], 1)
                for ob in range(KD):
                    u = ob
                    act.wait_ge(s["turned"], u + 1)
                    nc.scalar.activation(w1h[:, :, ob * P:(ob + 1) * P], bank[u % 4][:, 0:KD, :],
                                         ACT.Copy).then_inc(s["high_ready"], 1)
                for c, (ob, ib, p, t, n) in enumerate(chunks):
                    u = KD + c
                    act.wait_ge(s["turned"], u + 1)
                    tap = TAP0[p] + t
                    nc.scalar.activation(w2h[:, tap:tap + n, ib, ob * P:(ob + 1) * P], bank[u % 4][:, 0:n, :],
                                         ACT.Copy).then_inc(s["high_ready"], 1)

            @block.vector
            def _(dve):
                steps = [0]

                def link(ins):
                    steps[0] += 1
                    ins.then_inc(s["dve_step"], 1)
                    dve.wait_ge(s["dve_step"], steps[0])

                v = nc.vector
                link(v.memset(ones[:, :], 1.0))
                dve.wait_ge(s["vec_in"], 8 * 16)
                vt = vec[:, :, :].rearrange("p (a c) k -> p a c k", a=2)
                link(v.tensor_scalar(veps[:, :, :], vt[:, :, 3, :], EPS, None, ALU.add))
                v.tensor_copy(work[:, :, :], veps[:, :, :]).then_inc(s["veps_ready"], 1)
                dve.wait_ge(s["raw1_in"], 16)
                link(v.tensor_reduce(small["w1max"][:, :], raw1[:, :, :], AX.X, ALU.max, apply_absolute_value=True))
                power_scale(v, link, small["w1max"][:, :], small["w1pow"][:, :], small["w1scale"][:, :],
                            small["w1inv"][:, :], W_TOP)
                for ob in range(KD):
                    ins = v.tensor_scalar(raw1[:, ob, :], raw1[:, ob, :], small["w1scale"][:, ob:ob + 1], None, ALU.mult)
                    if ob < KD - 1:
                        link(ins)
                    else:
                        ins.then_inc(s["w1_scaled"], 1)
                dve.wait_ge(s["root_ready"], 1)
                rsqrt_step(v, link, bn[:, :, :], root[:, :, :], veps[:, :, :], work[:, :, :])
                link(v.tensor_tensor(bn[:, :, :], bn[:, :, :], vt[:, :, 0, :], ALU.mult))
                link(v.tensor_tensor(work[:, :, :], vt[:, :, 2, :], bn[:, :, :], ALU.mult))
                link(v.tensor_tensor(veps[:, :, :], vt[:, :, 1, :], work[:, :, :], ALU.subtract))
                link(v.tensor_copy(conv2_bias[:, :], veps[:, 1, :]))
                dve.wait_ge(s["norm_ready"], 1)
                bound, t1 = small["bound"], small["work1"]
                link(v.tensor_tensor(bound[:, :], small["norm"][:, :], small["w1inv"][:, :], ALU.mult))
                link(v.scalar_tensor_tensor(out=t1[:, :], in0=bn[:, 0, :], scalar=-1.0, in1=bn[:, 0, :],
                                            op0=ALU.mult, op1=ALU.max))
                link(v.scalar_tensor_tensor(out=bound[:, :], in0=bound[:, :], scalar=16.25, in1=t1[:, :],
                                            op0=ALU.mult, op1=ALU.mult))
                link(v.scalar_tensor_tensor(out=t1[:, :], in0=veps[:, 0, :], scalar=-1.0, in1=veps[:, 0, :],
                                            op0=ALU.mult, op1=ALU.max))
                link(v.tensor_tensor(bound[:, :], bound[:, :], t1[:, :], ALU.add))
                for ob in range(KD):
                    if ob:
                        dve.wait_ge(s["row_ready"], ob)
                    v.tensor_scalar(diag[:, :], ident[:, :], bound[:, ob:ob + 1], None, ALU.mult)\
                        .then_inc(s["diag_ready"], 1)
                dve.wait_ge(s["row_ready"], KD)
                link(v.tensor_reduce(ymax[:, :], bound_row[:, :, :], AX.XY, ALU.max))
                power_scale(v, link, ymax[:, :], ypow[:, :], yscale[:, :], yinv[:, :], Y_TOP)
                link(v.tensor_scalar(conv1_bias[:, :], veps[:, 0, :], yscale[:, 0:1], None, ALU.mult))
                link(v.tensor_tensor(t1[:, :], bn[:, 0, :], small["w1inv"][:, :], ALU.mult))
                link(v.tensor_scalar(conv1_scale[:, :], t1[:, :], yscale[:, 0:1], float(2.0 ** -H_TOP),
                                     ALU.mult, ALU.mult))

                def rests(lo, hi):
                    for u in range(lo, hi):
                        dve.wait_ge(s["high_ready"], u + 1)
                        if u < KD:
                            o, h = w1l[:, :, u * P:(u + 1) * P], w1h[:, :, u * P:(u + 1) * P]
                            n = KD
                        else:
                            ob, ib, p, t, n = chunks[u - KD]
                            tap = TAP0[p] + t
                            o = w2l[:, tap:tap + n, ib, ob * P:(ob + 1) * P]
                            h = w2h[:, tap:tap + n, ib, ob * P:(ob + 1) * P]
                        v.tensor_tensor(o, bank[u % 4][:, 0:n, :], h, ALU.subtract).then_inc(s["rest_ready"], 1)

                rests(0, KD)
                half = len(chunks) // KD
                for ob in range(KD):
                    dve.wait_ge(s[f"raw2_in{ob}"], 16)
                    r2 = raw2[ob]
                    m = small["w2max"][:, ob:ob + 1]
                    link(v.tensor_reduce(m, r2[:, :, :], AX.XY, ALU.max, apply_absolute_value=True))
                    power_scale(v, link, m, small["w2pow"][:, ob:ob + 1], small["w2scale"][:, ob:ob + 1],
                                small["w2inv"][:, ob:ob + 1], W2_TOP)
                    link(v.tensor_scalar(r2[:, :, :], r2[:, :, :], small["w2scale"][:, ob:ob + 1], None, ALU.mult))
                    link(v.tensor_tensor(fa[:, :, :], r2[:, :, 0:15:2], r2[:, :, 1:16:2], ALU.add))
                    v.tensor_tensor(s4[:, :, 4:8], r2[:, :, 0:13:4], r2[:, :, 2:15:4], ALU.add)
                    v.tensor_tensor(s4[:, :, 8:12], r2[:, :, 1:14:4], r2[:, :, 3:16:4], ALU.add)
                    v.tensor_tensor(s4[:, :, 0:4], fa[:, :, 0:7:2], fa[:, :, 1:8:2], ALU.add).then_inc(s["sums_ready"], 1)
                    rests(KD + ob * half, KD + (ob + 1) * half)
                link(v.tensor_tensor(t1[:, :], bn[:, 1, :], small["w2inv"][:, :], ALU.mult))
                link(v.tensor_scalar(conv2_scale[:, :], t1[:, :], yinv[:, 0:1], None, ALU.mult))

            @block.tensor
            def _(pe):
                def room(u):
                    if u >= 4:
                        pe.wait_ge(s["rest_ready"], u - 3)

                pe.wait_ge(s["id_in"], 16)
                pe.wait_ge(s["w1_scaled"], 1)
                for ob in range(KD):
                    for ib in range(KD):
                        last = nc.tensor.transpose(bank[ob][:, ib, :], raw1[:, ob, ib * P:(ib + 1) * P], ident[:, :])
                    last.then_inc(s["turned"], 1)
                for ob in range(KD):
                    pe.wait_ge(s["diag_ready"], ob + 1)
                    nc.tensor.matmul(bound_row[:, ob, :], ones[:, :], diag[:, :], start=True, stop=True)\
                        .then_inc(s["row_ready"], 1)
                now = -1
                for c, (ob, ib, p, t, n) in enumerate(chunks):
                    if ob != now:
                        pe.wait_ge(s["sums_ready"], ob + 1)
                        now = ob
                    room(KD + c)
                    for j, (_, src) in enumerate(unit_taps(ob, ib, p)[t:t + n]):
                        last = nc.tensor.transpose(bank[(KD + c) % 4][:, j, :], src, ident[:, :])
                    last.then_inc(s["turned"], 1)

        xa = [sb(f"xa{i}", [P, NB, D]) for i in range(2)]
        bst = sb("bst", [P, NB, 6])
        mv = sb("mv", [P, NB, 2])
        ve = sb("ve", [P, NB])
        rt = sb("rt", [P, NB])
        r0 = sb("r0", [P, NB])
        nt = sb("nt", [P, NB])
        ln = [sb(f"ln{i}", [P, 2, NB]) for i in range(2)]
        h32 = sb("h32", [P, KD, N])
        hh = sb("hh", [P, KD, N], F16)
        hl = sb("hl", [P, KD, N], F16)
        y1 = sb("y1", [P, 4, KD, G, QW])
        mix = sb("mix", [P, CW])
        da = sb("da", [P, CW])
        db = sb("db", [P, CW])
        ch = sb("ch", [P, NPROD, KD, G, QW], F16)
        cl = sb("cl", [P, NPROD, KD, G, QW], F16)
        sa, ga2, ga3, ha, hb = (sb(n, [P, KD, G, Q]) for n in ("sa", "ga2", "ga3", "ha", "hb"))
        co = sb("co", [P, KD, G, N])
        turn = [ctx.enter_context(nc.psum_tensor(f"turn{i}", [P, NB, P], F32)) for i in range(KD)]
        c1p = [ctx.enter_context(nc.psum_tensor(f"c1p{i}", [P, Q, 4], F32)) for i in range(KD)]
        kp = [ctx.enter_context(nc.psum_tensor(f"kp{i}", [P, G, Q], F32)) for i in range(3)]
        x_in = [sem(f"x_in{i}") for i in range(2)]
        loading, aggregating = sem("loading"), sem("aggregating")
        pad_ready, bst_ready, mv_ready, ve_ready, rt_ready, ln_step, ln_ready = map(sem, (
            "pad_ready", "bst_ready", "mv_ready", "ve_ready", "rt_ready", "ln_step", "ln_ready"))
        hrow_ready, turn_ready, h32_ready, hh_ready, hl_ready = map(sem, (
            "hrow_ready", "turn_ready", "h32_ready", "hh_ready", "hl_ready"))
        c1_ready, y1_ready, diff_ready, ch_ready, cl_ready = map(sem, (
            "c1_ready", "y1_ready", "diff_ready", "ch_ready", "cl_ready"))
        prod_ready, taken, fin_ready = map(sem, ("prod_ready", "taken", "fin_ready"))
        stored = [sem(f"stored{i}") for i in range(KD)]
        h_stored = sem("h_stored")
        flat = lambda c: y1[:, c, :, :, :].rearrange("p k g w -> p (k g w)")
        cflat = lambda t, p: t[:, p, :, :, :].rearrange("p k g w -> p (k g w)")
        whole, here, shifted = slice(0, CW), slice(0, CW - 1), slice(1, CW)
        D_OF = {1: 0, 2: 1, 3: 3, 4: 4, 5: 5, 6: 7, 7: 8, 8: 9}
        SRC = {1: mix, 2: mix, 3: db, 4: mix, 5: mix, 6: db, 7: mix, 8: mix}
        SHORT = {2, 5, 6, 7, 8}
        span = lambda p: here if p in SHORT else whole
        src_of = lambda p: (flat(3) if p == 0 else SRC[p][:, :])[:, span(p)]

        block = ctx.enter_context(nc.Block())

        @block.sync
        def _(sp):
            def loads(n):
                for q in range(G):
                    wait(sp, turn_ready, count(n, KD * G, KD * (q - 1)))
                    sp.sem_inc(loading, 1)
                    base, off = n
                    sp.dma_start(xa[q % 2][:, :, :],
                                 io["x"][base * G + (off * G + q), :, :].rearrange("(j p) d -> p j d", p=P))\
                        .then_inc(x_in[q % 2], 16)
            loads((0, 0))
            loads((0, 1))
            with sp.Fori(1, NGROUP - 1) as g:
                loads((g, 1))

        @block.gpsimd
        def _(pool):
            def rest(n, p):
                pool.wait_ge(ch_ready, count(n, NPROD, p + 1))
                nc.gpsimd.tensor_tensor(cflat(cl, p)[:, span(p)], src_of(p), cflat(ch, p)[:, span(p)], ALU.subtract)\
                    .then_inc(cl_ready, 1)

            def group(n):
                for p in range(NPROD):
                    rest(n, p)
            group((0, 0))
            group((0, 1))
            with pool.Fori(1, NGROUP - 1) as g:
                group((g, 1))

        @block.scalar
        def _(act):
            def layernorm(n, q):
                act.wait_ge(ve_ready, count(n, G, q + 1))
                nc.scalar.activation(rt[:, :], ve[:, :], ACT.Sqrt).then_inc(rt_ready, 1)
                act.wait_ge(ln_ready, count(n, G, q + 1))
                for j in range(NB):
                    nc.scalar.activation(xa[q % 2][:, j, :], xa[q % 2][:, j, :], ACT.Relu,
                                         bias=ln[q % 2][:, 1, j:j + 1], scale=ln[q % 2][:, 0, j:j + 1])\
                        .then_inc(hrow_ready, 1)

            def h_out(n, q):
                wait(act, hl_ready, count(n, G, q))
                wait(act, h_stored, count(n, 16 * G, 16 * q))
                for c in range(KD):
                    act.wait_ge(turn_ready, count(n, KD * G, KD * q + c + 1))
                    nc.scalar.activation(h32[:, c, :], turn[c][:, :, :].rearrange("p j r -> p (j r)"), ACT.Copy)\
                        .then_inc(h32_ready, 1)
                act.wait_ge(h32_ready, count(n, KD * G, KD * (q + 1)))
                base, off = n
                act.dma_start(h_by_batch[base * G + (off * G + q), :, :, :], h32[:, :, :]).then_inc(h_stored, 16)

            def y_out(n, q):
                if q == 0:
                    wait(act, diff_ready, count(n, SUMS))
                    wait(act, cl_ready, count(n, NPROD, -NPROD + 1))
                for ob in range(KD):
                    act.wait_ge(c1_ready, count(n, KD * G, KD * q + ob + 1))
                    nc.scalar.activation(y1[:, :, ob, q, 2:2 + Q], c1p[ob][:, :, :].rearrange("p r c -> p c r"),
                                         ACT.Relu, bias=conv1_bias[:, ob:ob + 1], scale=conv1_scale[:, ob:ob + 1])\
                        .then_inc(y1_ready, 1)

            def high(n, p):
                wait(act, prod_ready, count(n, EV, -EV + KD * (p + 1)))
                if p == 0:
                    act.wait_ge(y1_ready, count(n, KD * G, KD * G))
                else:
                    act.wait_ge(diff_ready, count(n, SUMS, D_OF[p] + 1))
                nc.scalar.activation(cflat(ch, p)[:, span(p)], src_of(p), ACT.Copy).then_inc(ch_ready, 1)

            def finish(g):
                for ob in range(KD):
                    act.wait_ge(taken, count(g, EV, EV - KD + ob + 1))
                    nc.scalar.activation(co[:, ob, :, :], co[:, ob, :, :], ACT.Identity,
                                         bias=conv2_bias[:, ob:ob + 1], scale=conv2_scale[:, ob:ob + 1])\
                        .then_inc(fin_ready, 1)
                base, off = g
                for ob in range(KD):
                    act.wait_ge(fin_ready, count(g, KD, ob + 1))
                    act.dma_start(by_group[base + off, ob, :, :, :], co[:, ob, :, :]).then_inc(stored[ob], 16)

            def ahead(n):
                layernorm(n, 0)
                layernorm(n, 1)
                h_out(n, 0)
                y_out(n, 0)
                h_out(n, 1)
                layernorm(n, 2)
                y_out(n, 1)
                h_out(n, 2)
                layernorm(n, 3)
                y_out(n, 2)
                h_out(n, 3)
                y_out(n, 3)
                for p in range(NPROD - 1):
                    high(n, p)

            ahead((0, 0))
            high((0, 0), NPROD - 1)

            def both(g, n):
                ahead(n)
                finish(g)
                high(n, NPROD - 1)
            both((0, 0), (0, 1))
            with act.Fori(1, NGROUP - 1) as g:
                both((g, 0), (g, 1))
            finish((0, NGROUP - 1))
            for ob in range(KD):
                act.wait_ge(stored[ob], 16 * NGROUP)
            act.wait_ge(h_stored, 16 * B)

        @block.vector
        def _(dve):
            v = nc.vector
            v.memset(y1[:, :, :, :, :], 0.0).then_inc(pad_ready, 1)
            dve.wait_ge(pad_ready, 1)

            LN_STEPS = 6

            def layernorm(n, q):
                dve.wait_ge(x_in[q % 2], count(n, 2 * 16, 16 * (q // 2 + 1)))
                for j in range(NB):
                    v.bn_stats(bst[:, j, :], xa[q % 2][:, j, :]).then_inc(bst_ready, 1)
                dve.wait_ge(bst_ready, count(n, NB * G, NB * (q + 1)))
                dve.sem_inc(aggregating, 1)
                for j in range(NB):
                    v.bn_aggr(mv[:, j, :], bst[:, j, :]).then_inc(mv_ready, 1)
                dve.wait_ge(mv_ready, count(n, NB * G, NB * (q + 1)))
                v.tensor_scalar(ve[:, :], mv[:, :, 1], EPS, None, ALU.add).then_inc(ve_ready, 1)
                dve.wait_ge(rt_ready, count(n, G, q + 1))
                wait(dve, hrow_ready, count(n, NB * G, NB * (q - 1)))
                k = [0]

                def step(ins):
                    k[0] += 1
                    ins.then_inc(ln_step, 1)
                    dve.wait_ge(ln_step, count(n, LN_STEPS * G, LN_STEPS * q + k[0]))
                rsqrt_step(v, step, r0[:, :], rt[:, :], ve[:, :], nt[:, :])
                step(v.tensor_scalar(ln[q % 2][:, 0, :], r0[:, :], H_SCALE, None, ALU.mult))
                v.scalar_tensor_tensor(out=ln[q % 2][:, 1, :], in0=mv[:, :, 0], scalar=-1.0,
                                       in1=ln[q % 2][:, 0, :], op0=ALU.mult, op1=ALU.mult).then_inc(ln_ready, 1)

            def split(n, q):
                dve.wait_ge(h32_ready, count(n, KD * G, KD * (q + 1)))
                wait(dve, c1_ready, count(n, KD * G, KD * q))
                v.tensor_copy(hh[:, :, :], h32[:, :, :]).then_inc(hh_ready, 1)
                dve.wait_ge(hh_ready, count(n, G, q + 1))
                v.tensor_tensor(hl[:, :, :], h32[:, :, :], hh[:, :, :], ALU.subtract).then_inc(hl_ready, 1)

            def take(g, m):
                p, ob = divmod(m, KD)
                dve.wait_ge(prod_ready, count(g, EV, m + 1))
                wait(dve, taken, count(g, EV, m - 1))
                if p == 4:
                    wait(dve, stored[ob], count(g, 16))
                bank = kp[m % 3][:, :, :]
                o4 = co[:, ob, :, :].rearrange("p g (r c) -> p c g r", c=4)
                if p == 0:
                    last = v.tensor_copy(sa[:, ob, :, :], bank)
                elif p == 1:
                    last = v.tensor_tensor(ga2[:, ob, :, :], bank, sa[:, ob, :, :], ALU.add)
                elif p == 2:
                    last = v.tensor_tensor(ga3[:, ob, :, :], bank, sa[:, ob, :, :], ALU.add)
                elif p in (3, 6):
                    v.tensor_tensor(ha[:, ob, :, :], bank, ga2[:, ob, :, :], ALU.add)
                    last = v.tensor_tensor(hb[:, ob, :, :], bank, ga3[:, ob, :, :], ALU.add)
                else:
                    phase, addend = {4: (0, ha), 5: (2, hb), 7: (1, ha), 8: (3, hb)}[p]
                    last = v.tensor_tensor(o4[:, phase, :, :], bank, addend[:, ob, :, :], ALU.add)
                last.then_inc(taken, 1)

            def difference(n, d):
                q0, q1, q2, q3 = (flat(c) for c in range(4))
                a, b = da[:, :], db[:, :]
                if d == 0:
                    dve.wait_ge(y1_ready, count(n, KD * G, KD * G))
                else:
                    dve.wait_ge(diff_ready, count(n, SUMS, d))
                free = {0: -1, 1: 1, 3: 6 - NPROD, 4: 2, 5: 4, 7: 3, 8: 5, 9: 7}
                if d in free:
                    wait(dve, cl_ready, count(n, NPROD, free[d] + 1))
                w, h, f = whole, here, shifted
                out, x, y = [
                    (mix[:, w], q1[:, w], q3[:, w]),
                    (mix[:, h], q1[:, f], q3[:, h]),
                    (da[:, w], q0[:, w], q1[:, w]),
                    (db[:, w], q2[:, w], q3[:, w]),
                    (mix[:, w], a[:, w], b[:, w]),
                    (mix[:, h], a[:, f], b[:, h]),
                    (da[:, w], q2[:, w], q1[:, w]),
                    (db[:, h], q0[:, f], q3[:, h]),
                    (mix[:, h], a[:, h], b[:, h]),
                    (mix[:, h], a[:, f], b[:, h]),
                ][d]
                v.tensor_tensor(out, x, y, ALU.subtract).then_inc(diff_ready, 1)

            def both(g, n):
                def banks(p):
                    if g is not None:
                        take(g, KD * p)
                        take(g, KD * p + 1)

                def bank(m):
                    if g is not None:
                        take(g, m)

                if n is None:
                    for p in range(NPROD):
                        banks(p)
                    return
                layernorm(n, 0)
                banks(0)
                layernorm(n, 1)
                banks(1)
                banks(2)
                split(n, 0)
                banks(3)
                layernorm(n, 2)
                split(n, 1)
                banks(4)
                layernorm(n, 3)
                split(n, 2)
                banks(5)
                split(n, 3)
                banks(6)
                for d in range(4):
                    difference(n, d)
                bank(14)
                difference(n, 4)
                bank(15)
                difference(n, 5)
                difference(n, 6)
                difference(n, 7)
                bank(16)
                difference(n, 8)
                bank(17)
                difference(n, 9)

            both(None, (0, 0))
            both((0, 0), (0, 1))
            with dve.Fori(1, NGROUP - 1) as g:
                both((g, 0), (g, 1))
            both((0, NGROUP - 1), None)

        @block.tensor
        def _(pe):
            def turn_h(n, q):
                pe.wait_ge(hrow_ready, count(n, NB * G, NB * (q + 1)))
                for c in range(KD):
                    wait(pe, h32_ready, count(n, KD * G, KD * (q - 1) + c + 1))
                    for j in range(NB):
                        last = nc.tensor.transpose(turn[c][:, j, :], xa[q % 2][:, j, c * P:(c + 1) * P], ident[:, :])
                    last.then_inc(turn_ready, 1)

            def conv1(n, q):
                pe.wait_ge(hl_ready, count(n, G, q + 1))
                for ob in range(KD):
                    wait(pe, y1_ready, count(n, KD * G, KD * (q - 1) + ob + 1))
                    pairs = [(w, h, k) for k in range(KD) for w, h in ((w1h, hh), (w1h, hl), (w1l, hh))]
                    for i, (w, h, k) in enumerate(pairs):
                        last = nc.tensor.matmul(c1p[ob][:, :, :].rearrange("p r c -> p (r c)"),
                                                w[:, k, ob * P:(ob + 1) * P], h[:, k, :],
                                                start=(i == 0), stop=(i == len(pairs) - 1))
                    last.then_inc(c1_ready, 1)

            def product(g, p):
                pe.wait_ge(cl_ready, count(g, NPROD, p + 1))
                for ob in range(KD):
                    m = KD * p + ob
                    wait(pe, taken, count(g, EV, m - 2))
                    steps = [(w, c, t, k) for t in range(PTAPS[p]) for k in range(KD)
                             for w, c in ((w2h, ch), (w2h, cl), (w2l, ch))]
                    for i, (w, c, t, k) in enumerate(steps):
                        last = nc.tensor.matmul(kp[m % 3][:, :, :], w[:, TAP0[p] + t, k, ob * P:(ob + 1) * P],
                                                c[:, p, k, :, t:t + Q], start=(i == 0), stop=(i == len(steps) - 1))
                    last.then_inc(prod_ready, 1)

            def both(g, n):
                def prod(p):
                    if g is not None:
                        product(g, p)
                if n is None:
                    for p in range(NPROD):
                        prod(p)
                    return
                prod(0)
                prod(1)
                prod(2)
                turn_h(n, 0)
                for q in range(G):
                    prod(3 + q)
                    conv1(n, q)
                    if q + 1 < G:
                        turn_h(n, q + 1)
                prod(7)
                prod(8)

            both(None, (0, 0))
            both((0, 0), (0, 1))
            with pe.Fori(1, NGROUP - 1) as g:
                both((g, 0), (g, 1))
            both((0, NGROUP - 1), None)


def gate_phase(nc, io, scratch, shared, out):
    ident, h_scratch = shared["ident"], shared["h_scratch"]
    ctx = ExitStack()
    with ctx:
        sb = lambda name, shape, dt=F32: ctx.enter_context(nc.sbuf_tensor(name, shape, dt))
        sem = lambda name: ctx.enter_context(nc.semaphore(name))
        KI = 2 * KD
        NHH = 3 * D // P
        whh = sb("whh", [P, KD, 3 * D], F16)
        whl = sb("whl", [P, KD, 3 * D], F16)
        wih = sb("wih", [P, KI, 3 * D], F32R)
        wil = sb("wil", [P, KI, 3 * D], F32R)
        wmh = sb("wmh", [P, KD, D], F16)
        wml = sb("wml", [P, KD, D], F16)
        wsh = sb("wsh", [P, KD, P], F16)
        wsl = sb("wsl", [P, KD, P], F16)
        gate_inv = sb("gate_inv", [P, NHH])
        gate_half = sb("gate_half", [P, NHH])
        gate_bias = sb("gate_bias", [P, NHH])
        hn_bias = sb("hn_bias", [P, KD])
        s_inv = sb("s_inv", [P, 1])
        s_bias = sb("s_bias", [P, 1])
        msg_inv = sb("msg_inv", [P, 2, D])
        msg_bias = sb("msg_bias", [P, 2, D])
        rows = sb("rows", [P, 6])

        with ExitStack() as tmp:
            tb = lambda name, shape, dt=F32: tmp.enter_context(nc.sbuf_tensor(name, shape, dt))
            raw_hh = tb("raw_hh", [P, NHH, D])
            raw_ih = tb("raw_ih", [P, NHH, 2 * D])
            raw_m = tb("raw_m", [P, KD, D])
            raw_s = tb("raw_s", [P, D])
            vih, vhh = tb("vih", [P, NHH]), tb("vhh", [P, NHH])
            ones, diag = tb("ones2", [P, P]), tb("diag2", [P, P])
            NS = NHH + KD + 1
            wmax, wpow, wscale, winv = (tb(n, [P, NS]) for n in ("wmax", "wpow", "wscale", "winv"))
            kscale = tb("kscale", [P, NHH])
            bank = [tmp.enter_context(nc.psum_tensor(f"wg{i}", [P, 4, P], F32)) for i in range(4)]
            inv_row = tmp.enter_context(nc.psum_tensor("inv_row", [P, KD, P], F32))
            names = ("w_in s_cleared s_in v_in step2 scaled2 turned2 high2 rest2 diag2_ready row2_ready")
            s = {n: tmp.enter_context(nc.semaphore(n + "_g")) for n in names.split()}
            chunks = []
            for o in range(NHH):
                chunks.append([(raw_hh[:, o, k * P:(k + 1) * P]) for k in range(KD)]
                              + [None, whh[:, :, o * P:(o + 1) * P], whl[:, :, o * P:(o + 1) * P]])
            for o in range(KD):
                chunks.append([(raw_m[:, o, k * P:(k + 1) * P]) for k in range(KD)]
                              + [None, wmh[:, :, o * P:(o + 1) * P], wml[:, :, o * P:(o + 1) * P]])
            chunks.append([(raw_s[:, k * P:(k + 1) * P]) for k in range(KD)] + [None, wsh[:, :, :], wsl[:, :, :]])
            for o in range(NHH):
                chunks.append([(raw_ih[:, o, k * P:(k + 1) * P]) for k in range(KI)]
                              + [None, wih[:, :, o * P:(o + 1) * P], wil[:, :, o * P:(o + 1) * P]])
            block = tmp.enter_context(nc.Block())

            @block.sync
            def _(sp):
                sp.dma_start(raw_hh[:, :, :], io["w_hh"].rearrange("(o p) i -> p o i", p=P)).then_inc(s["w_in"], 16)
                sp.dma_start(raw_ih[:, :, :], io["w_ih"].rearrange("(o p) i -> p o i", p=P)).then_inc(s["w_in"], 16)
                sp.dma_start(raw_m[:, :, :], io["w_msg"].rearrange("(o p) i -> p o i", p=P)).then_inc(s["w_in"], 16)
                sp.dma_start(rows[:, :], io["rows"]).then_inc(s["w_in"], 16)
                sp.wait_ge(s["s_cleared"], 2)
                for r in S_ROWS:
                    sp.dma_start(raw_s[r:r + 3, :], io["w_se"]).then_inc(s["s_in"], 16)

            @block.gpsimd
            def _(pool):
                with nc.allow_non_contiguous_dma(reason="small vectors"):
                    pool.dma_start(vih[:, :], io["b_ih"].rearrange("(k p) -> p k", p=P)).then_inc(s["v_in"], 16)
                    pool.dma_start(vhh[:, :], io["b_hh"].rearrange("(k p) -> p k", p=P)).then_inc(s["v_in"], 16)
                    for c in range(2):
                        pool.dma_start(msg_bias[:, c, :], io["b_msg"].partition_broadcast(P)).then_inc(s["v_in"], 16)
                    pool.wait_ge(s["s_cleared"], 2)
                    for r in S_ROWS:
                        pool.dma_start(s_bias[r:r + 3, :], io["b_se"].rearrange("(p a) -> p a", a=1))\
                            .then_inc(s["v_in"], 16)
                pool.wait_ge(s["v_in"], 16 * (4 + len(S_ROWS)))

            @block.scalar
            def _(act):
                for u, chunk in enumerate(chunks):
                    n, high = len(chunk) - 3, chunk[-2]
                    act.wait_ge(s["turned2"], u + 1)
                    nc.scalar.activation(high, bank[u % 4][:, 0:n, :], ACT.Copy).then_inc(s["high2"], 1)

            @block.vector
            def _(dve):
                v = nc.vector
                steps = [0]

                def link(ins):
                    steps[0] += 1
                    ins.then_inc(s["step2"], 1)
                    dve.wait_ge(s["step2"], steps[0])
                v.memset(raw_s[:, :], 0.0).then_inc(s["s_cleared"], 1)
                v.memset(s_bias[:, :], 0.0).then_inc(s["s_cleared"], 1)
                link(v.memset(ones[:, :], 1.0))
                dve.wait_ge(s["w_in"], 4 * 16)
                dve.wait_ge(s["s_in"], 16 * len(S_ROWS))
                dve.wait_ge(s["v_in"], 16 * (4 + len(S_ROWS)))
                v.tensor_reduce(wmax[:, 0:NHH], raw_hh[:, :, :], AX.X, ALU.max, apply_absolute_value=True)
                v.tensor_reduce(wmax[:, NHH:NHH + KD], raw_m[:, :, :], AX.X, ALU.max, apply_absolute_value=True)
                link(v.tensor_reduce(wmax[:, NS - 1:NS], raw_s[:, :], AX.X, ALU.max, apply_absolute_value=True))
                power_scale(v, link, wmax[:, :], wpow[:, :], wscale[:, :], winv[:, :], W_TOP)
                v.tensor_scalar(kscale[:, :], wscale[:, 0:NHH], H_SCALE, None, ALU.mult)
                link(v.tensor_scalar(winv[:, :], winv[:, :], 1.0 / H_SCALE, None, ALU.mult))
                v.tensor_copy(gate_inv[:, :], winv[:, 0:NHH])
                v.tensor_scalar(gate_half[:, :], winv[:, 0:NHH], 0.5, None, ALU.mult)
                link(v.tensor_copy(s_inv[:, :], winv[:, NS - 1:NS]))
                for o in range(NHH):
                    v.tensor_scalar(raw_hh[:, o, :], raw_hh[:, o, :], wscale[:, o:o + 1], None, ALU.mult)
                for o in range(KD):
                    v.tensor_scalar(raw_m[:, o, :], raw_m[:, o, :], wscale[:, NHH + o:NHH + o + 1], None, ALU.mult)
                v.tensor_scalar(raw_s[:, :], raw_s[:, :], wscale[:, NS - 1:NS], None, ALU.mult).then_inc(s["scaled2"], 1)
                for o in range(NHH):
                    last = v.tensor_scalar(raw_ih[:, o, :], raw_ih[:, o, :], kscale[:, o:o + 1], None, ALU.mult)
                last.then_inc(s["scaled2"], 1)
                link(v.tensor_tensor(gate_bias[:, 0:4], vih[:, 0:4], vhh[:, 0:4], ALU.add))
                v.tensor_scalar(gate_bias[:, 0:4], gate_bias[:, 0:4], 0.5, None, ALU.mult)
                v.tensor_copy(gate_bias[:, 4:6], vih[:, 4:6])
                v.tensor_scalar(hn_bias[:, :], vhh[:, 4:6], 0.5, None, ALU.mult)
                for o in range(KD):
                    if o:
                        dve.wait_ge(s["row2_ready"], o)
                    v.tensor_scalar(diag[:, :], ident[:, :], winv[:, NHH + o:NHH + o + 1], None, ALU.mult)\
                        .then_inc(s["diag2_ready"], 1)
                dve.wait_ge(s["row2_ready"], KD)
                for c in range(2):
                    v.tensor_copy(msg_inv[:, c, :], inv_row[:, :, :].rearrange("p k o -> p (k o)"))
                for u, chunk in enumerate(chunks):
                    n, high, rest = len(chunk) - 3, chunk[-2], chunk[-1]
                    dve.wait_ge(s["high2"], u + 1)
                    if high.dtype == F32R:
                        high = high.bitcast(F32)
                    v.tensor_tensor(rest, bank[u % 4][:, 0:n, :], high, ALU.subtract).then_inc(s["rest2"], 1)

            @block.tensor
            def _(pe):
                pe.wait_ge(s["scaled2"], 1)
                for o in range(KD):
                    pe.wait_ge(s["diag2_ready"], o + 1)
                    nc.tensor.matmul(inv_row[:, o, :], ones[:, :], diag[:, :], start=True, stop=True)\
                        .then_inc(s["row2_ready"], 1)
                pe.wait_ge(s["scaled2"], 2)
                for u, chunk in enumerate(chunks):
                    if u >= 4:
                        pe.wait_ge(s["rest2"], u - 3)
                    for j, src in enumerate(chunk[:-3]):
                        last = nc.tensor.transpose(bank[u % 4][:, j, :], src, ident[:, :])
                    last.then_inc(s["turned2"], 1)

        two = range(2)
        h_next = sb("h_next", [P, KD, N])
        adj_t = [sb(f"adj_t{i}", [P, N // SQ, SQ, NB]) for i in two]
        mask_t = sb("mask_t", [P, NB, N])
        xc_t = [sb(f"xc_t{i}", [P, KD, N]) for i in two]
        out_t = [sb(f"out_t{i}", [P, NB, D]) for i in two]
        hs = [sb(f"hs{i}", [P, KD, N]) for i in two]
        hh = [sb(f"hh2{i}", [P, KD, N], F16) for i in two]
        hl = [sb(f"hl2{i}", [P, KD, N], F16) for i in two]
        sf, lin_right, lin_left = sb("sf", [P, N]), sb("lin_right", [P, N]), sb("lin_left", [P, N])
        shi = sb("shi", [P, N], F32R)
        s_right, s_left = sb("s_right", [P, N], F32R), sb("s_left", [P, N], F32R)
        mg = [sb(f"mg{i}", [P, 2, D]) for i in two]
        mh = sb("mh", [P, NB, D], F32R)
        ml = sb("ml", [P, NB, D], F32R)
        ex = [sb(f"ex{i}", [P, N]) for i in two]
        ah = [sb(f"ah{i}", [P, N], F32R) for i in two]
        al = [sb(f"al{i}", [P, N], F32R) for i in two]
        ch = [sb(f"ch2{i}", [P, KD, N], F32R) for i in two]
        cl = [sb(f"cl2{i}", [P, KD, N], F32R) for i in two]
        nh = sb("nh", [P, KD, N], F32R)
        nl = sb("nl", [P, KD, N], F32R)
        rg, zg, gh, nn = (sb(n, [P, N]) for n in ("rg", "zg", "gh", "nn"))
        zg = [zg, sb("zg1", [P, N])]
        oo = [sb(f"oo{i}", [P, N]) for i in two]
        pg = [ctx.enter_context(nc.psum_tensor(f"pg{i}", [P, N], F32)) for i in range(3)]
        px = [ctx.enter_context(nc.psum_tensor(f"px{i}", [P, N], F32)) for i in range(KD)]
        pu = [ctx.enter_context(nc.psum_tensor(f"pu{i}", [P, N], F32)) for i in range(3)]
        x_in, adj_in, xc_in, out_st = ([sem(f"{n}{i}") for i in two] for n in ("xt_in", "adj_in", "xc_in", "out_st"))
        moving, h_in = sem("moving"), sem("h_in")
        hs_ready, hh_ready, hl_ready = map(sem, ("hs_ready", "hh2_ready", "hl2_ready"))
        (s_ready, sf_ready, shi_ready, sr_lin, s_right_ready, sl_lin, s_left_ready) = map(sem, (
            "s_ready", "sf_ready", "shi_ready", "sr_lin", "s_right_ready", "sl_lin", "s_left_ready"))
        (m_ready, m_scaled, m_biased, mh_ready, ml_ready) = map(sem, (
            "m_ready", "m_scaled", "m_biased", "mh_ready", "ml_ready"))
        (dist_ready, ex_ready, mask_ready, a_ready, ah_ready, al_ready, x_step) = map(sem, (
            "dist_ready", "ex_ready", "mask_ready", "a_ready", "ah_ready", "al_ready", "x_step"))
        (nmp_h, nmp_l, ct_ready, ch_ready, cl_ready) = map(sem, ("nmp_h", "nmp_l", "ct_ready", "ch2_ready", "cl2_ready"))
        (gate_ready, act_gate, u_ready, v_ready, n_ready, d_ready, w_ready, o_ready, ot_ready, out_ready) = map(sem, (
            "gate_ready", "act_gate", "u_ready", "v_ready", "n_ready", "d_ready", "w_ready", "o_ready",
            "ot_ready", "out_ready"))
        R0, HN0, Z0, IN0, R1, HN1, Z1, IN1 = range(8)
        BANK = {R0: 0, HN0: 1, Z0: 2, IN0: 0, R1: 1, HN1: 2, Z1: 0, IN1: 1}
        block = ctx.enter_context(nc.Block())
        nxt = lambda b, k=1: (b[0], b[1] + k)
        par = lambda b: b[1] % 2

        def index(b):
            return b[0] + b[1]

        def index_known(b):
            return b[0] + b[1] if isinstance(b[0], int) else None

        PREV = {R0: (Z1, -1), HN0: (IN1, -1), Z0: (HN1, -1), IN0: (R0, 0), R1: (HN0, 0), HN1: (Z0, 0),
                Z1: (IN0, 0), IN1: (R1, 0)}
        ACT_ORDER = {R0: 1, HN0: 2, Z0: 3, R1: 4, HN1: 5, Z1: 6}

        def bank_free(eng, b, k):
            prev, back = PREV[k]
            if prev in ACT_ORDER:
                wait(eng, act_gate, count(nxt(b, back), 6, ACT_ORDER[prev]))
            else:
                wait(eng, v_ready, count(nxt(b, back), 2, 1 if prev == IN0 else 2))

        def run(eng, both):
            both(None, None, (0, 0))
            both(None, (0, 0), (0, 1))
            both((0, 0), (0, 1), (0, 2))
            with eng.Fori(1, B // 2 - 1) as pair:
                b = pair * 2
                both((b, -1), (b, 0), (b, 1))
                both((b, 0), (b, 1), (b, 2))
            both((0, B - 3), (0, B - 2), (0, B - 1))
            both((0, B - 2), (0, B - 1), None)
            both((0, B - 1), None, None)

        def arrived(eng, sems, b, parts=1):
            base, off = b
            if isinstance(base, int):
                eng.wait_ge(sems[par(b)], 16 * parts * ((base + off) // 2 + 1))
            else:
                eng.wait_ge(sems[par(b)], base * (8 * parts) + 16 * parts * (off // 2 + 1))

        @block.sync
        def _(sp):
            def loads(b):
                i, k = par(b), index(b)
                wait(sp, hl_ready, count(b, 1))
                sp.sem_inc(moving, 1)
                wait(sp, hs_ready, count(b, 1))
                sp.sem_inc(moving, 1)
                sp.dma_start(h_next[:, :, :], h_scratch[k, :, :, :].rearrange("k p n -> p k n")).then_inc(h_in, 16)
                wait(sp, mask_ready, count(nxt(b, -1), NB))
                sp.sem_inc(moving, 1)
                for a in range(NB):
                    sp.dma_start(adj_t[i][a * SQ:(a + 1) * SQ, :, :, :],
                                 io["adj"][k, :, a * P:(a + 1) * P].rearrange("(b c) (r j) -> c b r j", c=SQ, r=SQ))\
                        .then_inc(adj_in[i], 16)
                wait(sp, cl_ready, count(nxt(b, -1), 1))
                sp.sem_inc(moving, 1)
                sp.dma_start(xc_t[i][:, :, :], scratch[k, :, :, :].rearrange("k p n -> p k n")).then_inc(xc_in[i], 16)

            def residual(b):
                if index_known(b) is None or index_known(b) >= 2:
                    arrived(sp, out_st, nxt(b, -2))
                    sp.sem_inc(moving, 1)
                sp.dma_start(out_t[par(b)][:, :, :], io["x"][index(b), :, :].rearrange("(j p) d -> p j d", p=P))\
                    .then_inc(x_in[par(b)], 16)

            def store(p):
                sp.wait_ge(out_ready, count(p, 2, 2))
                sp.sem_inc(moving, 1)
                sp.dma_start(out[index(p), :, :].rearrange("(j p) d -> p j d", p=P), out_t[par(p)][:, :, :])\
                    .then_inc(out_st[par(p)], 16)

            def both(p, b, n):
                if p is not None:
                    store(p)
                if n is not None:
                    residual(n)
                    if index_known(n) != B - 1:
                        loads(nxt(n))

            loads((0, 0))
            run(sp, both)
            for i in two:
                sp.wait_ge(out_st[i], 16 * (B // 2))

        @block.gpsimd
        def _(pool):
            def ahead(n):
                for m in range(NB):
                    pool.wait_ge(ah_ready, count(n, NB, m + 1))
                    nc.gpsimd.tensor_tensor(al[m % 2][:, :], ex[m % 2][:, :], ah[m % 2][:, :].bitcast(F32), ALU.subtract)\
                        .then_inc(al_ready, 1)
            ahead((0, 0))
            ahead((0, 1))
            ahead((0, 2))
            with pool.Fori(1, B // 2 - 1) as pair:
                ahead((pair * 2, 1))
                ahead((pair * 2, 2))
            ahead((0, B - 1))

        @block.scalar
        def _(act):
            A = nc.scalar.activation

            def tanh_n(b, f):
                act.wait_ge(v_ready, count(b, 2, f + 1))
                A(nn[:, :], nn[:, :], ACT.Tanh, bias=gate_bias[:, 4 + f:5 + f]).then_inc(n_ready, 1)

            def h_high(n):
                act.wait_ge(h_in, count(n, 16, 16))
                wait(act, gate_ready, count(nxt(n, -1), 8))
                A(hh[par(n)][:, :, :], h_next[:, :, :], ACT.Copy).then_inc(hh_ready, 1)

            def h_keep(n):
                wait(act, d_ready, count(nxt(n, -1), 2))
                A(hs[par(n)][:, :, :], h_next[:, :, :], ACT.Copy).then_inc(hs_ready, 1)

            def gate(b, k):
                f = 1 if k in (R1, HN1, Z1) else 0
                act.wait_ge(gate_ready, count(b, 8, k + 1))
                if k in (R0, R1):
                    wait(act, u_ready, count(b, 2, f))
                    A(rg[:, :], pg[BANK[k]][:, :], ACT.Tanh, bias=gate_bias[:, f:f + 1],
                      scale=gate_half[:, f:f + 1]).then_inc(act_gate, 1)
                elif k in (Z0, Z1):
                    wait(act, w_ready, count(nxt(b, -1), 2, f + 1))
                    A(zg[f][:, :], pg[BANK[k]][:, :], ACT.Tanh, bias=gate_bias[:, 2 + f:3 + f],
                      scale=gate_half[:, 2 + f:3 + f]).then_inc(act_gate, 1)
                else:
                    wait(act, v_ready, count(b, 2, f))
                    A(gh[:, :], pg[BANK[k]][:, :], ACT.Identity, bias=hn_bias[:, f:f + 1],
                      scale=gate_half[:, 4 + f:5 + f]).then_inc(act_gate, 1)

            def s_out(n):
                act.wait_ge(s_ready, count(n, 1, 1))
                wait(act, s_left_ready, count(n, 1))
                A(sf[0:64, :], pu[0][0:64, :], ACT.Identity, bias=s_bias[0:64, :], scale=s_inv[0:64, :])
                A(sf[64:128, :], pu[0][64:128, :], ACT.Square, bias=s_bias[64:128, :], scale=s_inv[64:128, :])\
                    .then_inc(sf_ready, 1)
                act.wait_ge(sf_ready, count(n, 1, 1))
                A(lin_right[:, :], sf[:, :], ACT.Identity, bias=rows[:, 2:3], scale=rows[:, 1:2]).then_inc(sr_lin, 1)
                A(lin_left[:, :], sf[:, :], ACT.Identity, bias=rows[:, 5:6], scale=rows[:, 4:5]).then_inc(sl_lin, 1)

            def messages(n):
                for m in range(2):
                    act.wait_ge(m_biased, count(n, 2, m + 1))
                    if m == 0:
                        wait(act, x_step, count(n, NB))
                    A(mh[:, 2 * m:2 * m + 2, :], mg[m][:, :, :], ACT.Relu).then_inc(mh_ready, 1)

            def exps(n, m):
                act.wait_ge(dist_ready, count(n, NB, m + 1))
                wait(act, al_ready, count(n, NB, m - 1))
                A(ex[m % 2][:, :], pu[m % 2][:, :], ACT.Exp).then_inc(ex_ready, 1)

            def mask_high(n, m):
                act.wait_ge(a_ready, count(n, NB, m + 1))
                wait(act, x_step, count(n, NB, m - 1))
                A(ah[m % 2][:, :], ex[m % 2][:, :], ACT.Copy).then_inc(ah_ready, 1)

            def conv_high(n):
                act.wait_ge(ct_ready, count(n, 1, 1))
                wait(act, gate_ready, count(nxt(n, -1), 8))
                A(ch[par(n)][:, :, :], xc_t[par(n)][:, :, :], ACT.Relu).then_inc(ch_ready, 1)

            def message_high(b):
                for c in range(KD):
                    act.wait_ge(x_step, count(b, NB, NB))
                    if c == 0:
                        wait(act, gate_ready, count(b, 8))
                    A(nh[:, c, :], px[c][:, :], ACT.Copy).then_inc(nmp_h, 1)

            def both(p, b, n):
                if b is not None:
                    message_high(b)
                if p is not None:
                    tanh_n(p, 1)
                if n is not None:
                    h_high(n)
                if b is not None:
                    gate(b, R0)
                if n is not None:
                    h_keep(n)
                if b is not None:
                    gate(b, HN0)
                    gate(b, Z0)
                if n is not None:
                    s_out(n)
                    messages(n)
                if b is not None:
                    tanh_n(b, 0)
                if n is not None:
                    exps(n, 0)
                    mask_high(n, 0)
                if b is not None:
                    gate(b, R1)
                if n is not None:
                    exps(n, 1)
                    mask_high(n, 1)
                if b is not None:
                    gate(b, HN1)
                if n is not None:
                    exps(n, 2)
                    mask_high(n, 2)
                if b is not None:
                    gate(b, Z1)
                if n is not None:
                    exps(n, 3)
                    mask_high(n, 3)
                    conv_high(n)

            run(act, both)

        @block.vector
        def _(dve):
            v = nc.vector

            def message_split(b):
                for c in range(KD):
                    dve.wait_ge(nmp_h, count(b, KD, c + 1))
                    v.tensor_tensor(nl[:, c, :], px[c][:, :], nh[:, c, :].bitcast(F32), ALU.subtract).then_inc(nmp_l, 1)

            def gate_mul(b, f):
                dve.wait_ge(act_gate, count(b, 6, 2 + 3 * f))
                v.scalar_tensor_tensor(out=gh[:, :], in0=rg[:, :], scalar=1.0, in1=gh[:, :],
                                       op0=ALU.add, op1=ALU.mult).then_inc(u_ready, 1)

            def gate_add(b, f):
                dve.wait_ge(gate_ready, count(b, 8, IN0 + 1 + 4 * f))
                dve.wait_ge(u_ready, count(b, 2, f + 1))
                v.scalar_tensor_tensor(out=nn[:, :], in0=pg[BANK[IN1 if f else IN0]][:, :],
                                       scalar=gate_inv[:, 4 + f:5 + f], in1=gh[:, :],
                                       op0=ALU.mult, op1=ALU.add).then_inc(v_ready, 1)

            def gate_end(b, f):
                o = oo[f][:, :]
                dve.wait_ge(n_ready, count(b, 2, f + 1))
                wait(dve, ot_ready, count(nxt(b, -1), 2, f + 1))
                v.scalar_tensor_tensor(out=o, in0=hs[par(b)][:, f, :], scalar=1.0 / H_SCALE, in1=nn[:, :],
                                       op0=ALU.mult, op1=ALU.subtract).then_inc(d_ready, 1)
                dve.wait_ge(act_gate, count(b, 6, 3 + 3 * f))
                dve.wait_ge(d_ready, count(b, 2, f + 1))
                v.scalar_tensor_tensor(out=o, in0=zg[f][:, :], scalar=1.0, in1=o, op0=ALU.add, op1=ALU.mult)\
                    .then_inc(w_ready, 1)
                dve.wait_ge(w_ready, count(b, 2, f + 1))
                v.scalar_tensor_tensor(out=o, in0=o, scalar=0.5, in1=nn[:, :], op0=ALU.mult, op1=ALU.add)\
                    .then_inc(o_ready, 1)

            def out_add(b, f):
                t = out_t[par(b)][:, :, f * P:(f + 1) * P]
                dve.wait_ge(ot_ready, count(b, 2, f + 1))
                arrived(dve, x_in, b)
                v.tensor_tensor(t, pu[2][:, :].rearrange("p (j c) -> p j c", c=P), t, ALU.add).then_inc(out_ready, 1)

            def h_rest(n):
                i = par(n)
                dve.wait_ge(hh_ready, count(n, 1, 1))
                v.tensor_tensor(hl[i][:, :, :], h_next[:, :, :], hh[i][:, :, :], ALU.subtract).then_inc(hl_ready, 1)

            def mask_turn(n, j):
                if j == 0:
                    arrived(dve, adj_in, n, NB)
                wait(dve, a_ready, count(n, NB, j + 1 - NB))
                v.transpose(mask_t[:, j, :], adj_t[par(n)][:, :, :, j]).then_inc(mask_ready, 1)

            def s_split(n):
                dve.wait_ge(sf_ready, count(n, 1, 1))
                v.tensor_copy(shi[:, :], sf[:, :]).then_inc(shi_ready, 1)
                dve.wait_ge(shi_ready, count(n, 1, 1))
                for dst, col, part, lin, done in ((s_right, 0, lin_right, sr_lin, s_right_ready),
                                                  (s_left, 3, lin_left, sl_lin, s_left_ready)):
                    dve.wait_ge(lin, count(n, 1, 1))
                    wait(dve, dist_ready, count(n, NB))
                    v.scalar_tensor_tensor(out=dst[:, :], in0=shi[:, :].bitcast(F32), scalar=rows[:, col:col + 1],
                                           in1=part[:, :], op0=ALU.mult, op1=ALU.add).then_inc(done, 1)

            def message_scale(n):
                for m in range(2):
                    dve.wait_ge(m_ready, count(n, 2, m + 1))
                    wait(dve, ml_ready, count(nxt(n, -1), 2, m + 1))
                    v.tensor_tensor(mg[m][:, :, :], pu[1 + m][:, :].rearrange("p (a d) -> p a d", d=D),
                                    msg_inv[:, :, :], ALU.mult).then_inc(m_scaled, 1)
                    dve.wait_ge(m_scaled, count(n, 2, m + 1))
                    v.tensor_tensor(mg[m][:, :, :], mg[m][:, :, :], msg_bias[:, :, :], ALU.add).then_inc(m_biased, 1)

            def message_rest(n):
                for m in range(2):
                    dve.wait_ge(mh_ready, count(n, 2, m + 1))
                    v.scalar_tensor_tensor(out=ml[:, 2 * m:2 * m + 2, :].rearrange("p a d -> p (a d)"),
                                           in0=mg[m][:, :, :].rearrange("p a d -> p (a d)"), scalar=0.0,
                                           in1=mh[:, 2 * m:2 * m + 2, :].bitcast(F32).rearrange("p a d -> p (a d)"),
                                           op0=ALU.max, op1=ALU.subtract).then_inc(ml_ready, 1)

            def mask(n, m):
                dve.wait_ge(mask_ready, count(n, NB, m + 1))
                dve.wait_ge(ex_ready, count(n, NB, m + 1))
                v.tensor_tensor(ex[m % 2][:, :], ex[m % 2][:, :], mask_t[:, m, :], ALU.mult).then_inc(a_ready, 1)

            def conv_sum(n):
                i = par(n)
                arrived(dve, xc_in, n)
                dve.wait_ge(hs_ready, count(n, 1, 1))
                v.scalar_tensor_tensor(out=xc_t[i][:, :, :].rearrange("p k n -> p (k n)"),
                                       in0=hs[i][:, :, :].rearrange("p k n -> p (k n)"), scalar=1.0 / H_SCALE,
                                       in1=xc_t[i][:, :, :].rearrange("p k n -> p (k n)"),
                                       op0=ALU.mult, op1=ALU.add).then_inc(ct_ready, 1)

            def conv_rest(n):
                i = par(n)
                dve.wait_ge(ch_ready, count(n, 1, 1))
                v.scalar_tensor_tensor(out=cl[i][:, :, :].rearrange("p k n -> p (k n)"),
                                       in0=xc_t[i][:, :, :].rearrange("p k n -> p (k n)"), scalar=0.0,
                                       in1=ch[i][:, :, :].bitcast(F32).rearrange("p k n -> p (k n)"),
                                       op0=ALU.max, op1=ALU.subtract).then_inc(cl_ready, 1)

            def both(p, b, n):
                if b is not None:
                    conv_rest(b)
                    message_split(b)
                if p is not None:
                    gate_end(p, 1)
                if n is not None:
                    h_rest(n)
                if p is not None:
                    out_add(p, 1)
                if n is not None:
                    for j in range(NB):
                        mask_turn(n, j)
                if b is not None:
                    gate_mul(b, 0)
                if n is not None:
                    s_split(n)
                    message_scale(n)
                if b is not None:
                    gate_add(b, 0)
                if n is not None:
                    message_rest(n)
                    mask(n, 0)
                if b is not None:
                    gate_end(b, 0)
                if n is not None:
                    mask(n, 1)
                if b is not None:
                    out_add(b, 0)
                    gate_mul(b, 1)
                if n is not None:
                    conv_sum(n)
                    mask(n, 2)
                    mask(n, 3)
                if b is not None:
                    gate_add(b, 1)

            run(dve, both)

        @block.tensor
        def _(pe):
            mm = nc.tensor.matmul

            def of_block(t, j):
                return t[:, j::NB]

            def turn_out(b, f, n):
                pe.wait_ge(o_ready, count(b, 2, f + 1))
                wait(pe, out_ready, count(b, 2, f))
                if f == 0 and n is not None:
                    pe.wait_ge(m_scaled, count(n, 2, 2))
                for j in range(NB):
                    last = nc.tensor.transpose(pu[2][:, j * P:(j + 1) * P], oo[f][:, j * P:(j + 1) * P], ident[:, :])
                last.then_inc(ot_ready, 1)

            def gate(b, k):
                i = par(b)
                f = 1 if k >= R1 else 0
                o = {R0: 0, R1: 1, Z0: 2, Z1: 3, HN0: 4, HN1: 5, IN0: 4, IN1: 5}[k]
                cols = slice(o * P, (o + 1) * P)
                bank = pg[BANK[k]][:, :]
                steps = []
                if k not in (IN0, IN1):
                    steps += [(w[:, c, cols], h[i][:, c, :]) for c in range(KD)
                              for w, h in ((whh, hh), (whh, hl), (whl, hh))]
                if k not in (HN0, HN1):
                    steps += [(w[:, c, cols], t[:, c, :]) for c in range(KD)
                              for w, t in ((wih, ch[i]), (wih, cl[i]), (wil, ch[i]))]
                    message = len(steps)
                    steps += [(w[:, KD + c, cols], t[:, c, :]) for c in range(KD)
                              for w, t in ((wih, nh), (wih, nl), (wil, nh))]
                bank_free(pe, b, k)
                for j, (w, t) in enumerate(steps):
                    if k == R0 and j == 3 * KD:
                        pe.wait_ge(cl_ready, count(b, 1, 1))
                    if k == R0 and j >= message and (j - message) % 3 == 0:
                        pe.wait_ge(nmp_l, count(b, KD, (j - message) // 3 + 1))
                    last = mm(bank, w, t, start=(j == 0), stop=(j == len(steps) - 1))
                last.then_inc(gate_ready, 1)

            def distance_rows_mm(n):
                i = par(n)
                pe.wait_ge(hl_ready, count(n, 1, 1))
                wait(pe, ex_ready, count(n, NB))
                steps = [(w[:, c, :], h[i][:, c, :]) for c in range(KD) for w, h in ((wsh, hh), (wsh, hl), (wsl, hh))]
                for j, (w, t) in enumerate(steps):
                    last = mm(pu[0][:, :], w, t, start=(j == 0), stop=(j == len(steps) - 1))
                last.then_inc(s_ready, 1)

            def messages(n):
                i = par(n)
                for m in range(NB):
                    if m == 2:
                        wait(pe, out_ready, count(nxt(n, -1), 2))
                    steps = [(of_block(h[i][:, c, :], m), w[:, c, :]) for c in range(KD)
                             for h, w in ((hh, wmh), (hh, wml), (hl, wmh))]
                    for j, (h, w) in enumerate(steps):
                        last = mm(pu[1 + m // 2][:, (m % 2) * D:(m % 2 + 1) * D], h, w,
                                  start=(j == 0), stop=(j == len(steps) - 1))
                    if m % 2:
                        last.then_inc(m_ready, 1)

            def distance(n, m):
                if m == 0:
                    pe.wait_ge(s_left_ready, count(n, 1, 1))
                elif m == 1:
                    pe.wait_ge(m_scaled, count(n, 2, 1))
                else:
                    pe.wait_ge(ex_ready, count(n, NB, m - 1))
                mm(pu[m % 2][:, :], of_block(s_left, m), s_right[:, :], start=True, stop=True).then_inc(dist_ready, 1)

            def aggregate(n, m):
                if m == 0:
                    pe.wait_ge(ml_ready, count(n, 2, 2))
                    wait(pe, nmp_l, count(n, KD))
                pe.wait_ge(al_ready, count(n, NB, m + 1))
                for c in range(KD):
                    cols = slice(c * P, (c + 1) * P)
                    for j, (w, t) in enumerate(((mh, ah), (mh, al), (ml, ah))):
                        last = mm(px[c][:, :], w[:, m, cols], t[m % 2][:, :],
                                  start=(m == 0 and j == 0), stop=(m == NB - 1 and j == 2))
                last.then_inc(x_step, 1)

            def both(p, b, n):
                if b is not None:
                    gate(b, R0)
                if b is not None:
                    gate(b, HN0)
                if p is not None:
                    turn_out(p, 1, n)
                if b is not None:
                    gate(b, Z0)
                if n is not None:
                    distance_rows_mm(n)
                    messages(n)
                if b is not None:
                    gate(b, IN0)
                if n is not None:
                    distance(n, 0)
                if b is not None:
                    gate(b, R1)
                if n is not None:
                    distance(n, 1)
                if b is not None:
                    gate(b, HN1)
                if n is not None:
                    aggregate(n, 0)
                if b is not None:
                    turn_out(b, 0, n)
                if n is not None:
                    distance(n, 2)
                if b is not None:
                    gate(b, Z1)
                if n is not None:
                    aggregate(n, 1)
                    distance(n, 3)
                if b is not None:
                    gate(b, IN1)
                if n is not None:
                    aggregate(n, 2)
                    aggregate(n, 3)

            run(pe, both)


_NAMES = {
    "x": "x", "adj": "adj", "L0_gnn_w_se": "w_se", "L0_gnn_b_se": "b_se", "L0_gnn_conv1_w": "conv1_w",
    "L0_gnn_bn1_g": "bn1_g", "L0_gnn_bn1_b": "bn1_b", "L0_gnn_bn1_m": "bn1_m", "L0_gnn_bn1_v": "bn1_v",
    "L0_gnn_conv2_w": "conv2_w", "L0_gnn_bn2_g": "bn2_g", "L0_gnn_bn2_b": "bn2_b", "L0_gnn_bn2_m": "bn2_m",
    "L0_gnn_bn2_v": "bn2_v", "L0_gnn_w_msg": "w_msg", "L0_gnn_b_msg": "b_msg", "L0_gnn_w_ih": "w_ih",
    "L0_gnn_b_ih": "b_ih", "L0_gnn_w_hh": "w_hh", "L0_gnn_b_hh": "b_hh",
}


def build(nc, io, out):
    scratch = nc.dram_tensor("conv_scratch", (B, KD, P, N), F32, kind="Internal").ap()
    with ExitStack() as ctx:
        shared = {
            "ident": ctx.enter_context(nc.sbuf_tensor("ident", [P, P], F32)),
            "h_scratch": nc.dram_tensor("h_scratch", (B, KD, P, N), F32, kind="Internal").ap(),
        }
        convolution_phase(nc, io, scratch, shared)
        gate_phase(nc, io, scratch, shared, out)


def kernel(**inputs):
    import concourse.bacc as bacc
    from concourse.bass_utils import run_bass_kernel_spmd

    nc = bacc.Bacc("TRN2", target_bir_lowering=False, num_devices=1)
    arrays = {f"in_{short}": np.ascontiguousarray(inputs[name]) for name, short in _NAMES.items()}
    arrays["in_ident"] = np.eye(P, dtype=np.float32)
    arrays["in_rows"] = distance_rows()
    io = {name[3:]: nc.dram_tensor(name, a.shape, mybir.dt.from_np(a.dtype), kind="ExternalInput").ap()
          for name, a in arrays.items()}
    out = nc.dram_tensor("out_y", (B, N, D), F32, kind="ExternalOutput").ap()
    build(nc, io, out)
    result = run_bass_kernel_spmd(nc, [arrays], core_ids=[0])
    return result.results[0]["out_y"]
```

```python
from contextlib import ExitStack

import concourse.bass as bass
import numpy as np
from concourse import mybir

DT = mybir.dt
F32, F16, F32R, I32 = DT.float32, DT.float16, DT.float32r, DT.int32
ALU = mybir.AluOpType
ACT = mybir.ActivationFunctionType
AX = mybir.AxisListType

P = 128
B, N, D = 32, 512, 256
KD = D // P
NB = N // P
EPS = 1e-5
H_TOP = 11
H_SCALE = float(2 ** H_TOP)
TAPS, PAD = 17, 8
G = 4
NGROUP = B // G
Q = N // 4
QW = (N + 2 * PAD) // 4
CW = KD * G * QW
W_TOP = 14
W2_TOP = 12
Y_TOP = 12
TINY = 1e-18
EXPO = 0x7F800000
PTAPS = [5, 5, 4, 5, 5, 4, 4, 4, 4]
NPROD = len(PTAPS)
TAP0 = [sum(PTAPS[:p]) for p in range(NPROD)]
NTAP = sum(PTAPS)
EV = NPROD * KD
SUMS = 10
RAW_AFTER = 3
S_ROWS = [0, 3, 6, 64, 67, 70, 73]
KI = 2 * KD
NHH = 3 * D // P
SQ = 32
CHUNK = KD * SQ


def distance_rows():
    t = np.zeros((P, 6), np.float32)
    ar, br, cr, al, bl, cl = range(6)
    t[0:3, ar] = 1
    t[3:6, ar], t[3:6, br] = -1, 1
    t[6:9, ar] = 1
    t[0:6, al] = 2
    t[6:9, al], t[6:9, bl] = -2, 2
    t[64:67, ar] = 1
    t[67:70, ar], t[67:70, br] = -1, 1
    t[64:70, cl] = -1
    t[70:73, al] = -1
    t[73:76, al], t[73:76, bl] = 1, -1
    t[70:76, cr] = 1
    return t


def carve(room, start, shape, dtype=F32):
    size = int(np.prod(shape)) // (2 if dtype == F16 else 1)
    names = "abcde"[:len(shape)]
    flat = room[:, start:start + size]
    if dtype != F32:
        flat = flat.bitcast(dtype)
    form = f"p ({' '.join(names)}) -> p {' '.join(names)}"
    return flat.rearrange(form, **dict(zip(names, shape))), start + size


def allocate(nc, ctx, parts):
    return {name: ctx.enter_context(nc.sbuf_tensor(name, [P, *shape], dtype)) for name, shape, dtype in parts}


INPUT_SIDE = [
    ("y1", (4, KD, G, QW), F32),
    ("mix", (CW,), F32),
    ("da", (CW,), F32), ("db", (CW,), F32),
    ("xa0", (NB, D), F32), ("xa1", (NB, D), F32),
    ("h32", (KD, N), F32), ("hh", (KD, N), F16), ("hl", (KD, N), F16),
    ("w1h", (KD, D), F16), ("w1l", (KD, D), F16),
]
GATE_WEIGHTS = [
    ("wih", (KI, 3 * D), F32R), ("wil", (KI, 3 * D), F32R),
    ("whh", (KD, 3 * D), F16), ("whl", (KD, 3 * D), F16),
    ("wmh", (KD, D), F16), ("wml", (KD, D), F16),
    ("wsh", (KD, P), F16), ("wsl", (KD, P), F16),
    ("raw_ih", (NHH, 2 * D), F32),
]
words = lambda parts: sum(int(np.prod(shape)) // (2 if dtype == F16 else 1) for _, shape, dtype in parts)
ROOM_LEFT = words(INPUT_SIDE) - words(GATE_WEIGHTS)
assert ROOM_LEFT >= 0


def count(index, per, k=0):
    base, off = index
    return base * per + (off * per + k)


def wait(eng, sem, value):
    if isinstance(value, int) and value <= 0:
        return
    eng.wait_ge(sem, value)


def tap_source(raw, fa, s4, p):
    last = (raw[:, :, TAPS - 1:TAPS], 1)
    ph = lambda c: (raw[:, :, c:c + 13:4], 4)
    return {
        0: [(s4[0], 4), last],
        1: [(fa[:, :, 0:7:2], 4), last],
        2: [(fa[:, :, 1:8:2], 4)],
        3: [(s4[1], 4), last],
        4: [ph(0), last],
        5: [ph(2)],
        6: [(s4[2], 4)],
        7: [ph(1)],
        8: [ph(3)],
    }[p]


def rsqrt_step(eng, link, out, root, value, tmp):
    link(eng.reciprocal(out, root))
    link(eng.tensor_tensor(tmp, out, out, ALU.mult))
    link(eng.tensor_tensor(tmp, tmp, value, ALU.mult))
    link(eng.tensor_scalar(tmp, tmp, -0.5, 1.5, ALU.mult, ALU.add))
    link(eng.tensor_tensor(out, out, tmp, ALU.mult))


def power_scale(eng, link, biggest, power, scale, inverse, top):
    link(eng.tensor_scalar(biggest, biggest, TINY, None, ALU.max))
    link(eng.tensor_scalar(power.bitcast(I32), biggest.bitcast(I32), EXPO, None, ALU.bitwise_and))
    link(eng.reciprocal(scale, power))
    link(eng.tensor_scalar(scale, scale, float(2.0 ** top), None, ALU.mult))
    link(eng.tensor_scalar(inverse, power, float(2.0 ** -top), None, ALU.mult))


def convolution_phase(nc, io, scratch, shared):
    ident, h_scratch = shared["ident"], shared["h_scratch"]
    by_group = scratch.rearrange("(r g) k p n -> r k p g n", g=G)
    h_by_batch = h_scratch.rearrange("b k p n -> b p k n")
    ctx = ExitStack()
    with ctx:
        sb = lambda name, shape, dt=F32: ctx.enter_context(nc.sbuf_tensor(name, shape, dt))
        sem = lambda name: ctx.enter_context(nc.semaphore(name))
        w2h = sb("w2h", [P, NTAP, KD, D], F16)
        w2l = sb("w2l", [P, NTAP, KD, D], F16)
        side = shared["input_side"]
        y1, mix, da, db, h32, hh, hl, w1h, w1l = (side[n] for n in "y1 mix da db h32 hh hl w1h w1l".split())
        xa = [side["xa0"], side["xa1"]]
        conv1_scale = sb("conv1_scale", [P, KD])
        conv1_bias = sb("conv1_bias", [P, KD])
        conv2_scale = sb("conv2_scale", [P, KD])
        conv2_bias = sb("conv2_bias", [P, KD])

        bst = sb("bst", [P, NB, 6])
        mv = sb("mv", [P, NB, 2])
        ve = sb("ve", [P, NB])
        rt = sb("rt", [P, NB])
        r0 = sb("r0", [P, NB])
        nt = sb("nt", [P, NB])
        ln = [sb(f"ln{i}", [P, 2, NB]) for i in range(2)]
        turn = [ctx.enter_context(nc.psum_tensor(f"turn{i}", [P, NB, P], F32)) for i in range(KD)]
        c1p = [ctx.enter_context(nc.psum_tensor(f"c1p{i}", [P, Q, 4], F32)) for i in range(KD)]
        x_in = [sem(f"x_in{i}") for i in range(2)]
        loading, aggregating = sem("loading"), sem("aggregating")
        pad_ready, bst_ready, mv_ready, ve_ready, rt_ready, ln_step, ln_ready = map(sem, (
            "pad_ready", "bst_ready", "mv_ready", "ve_ready", "rt_ready", "ln_step", "ln_ready"))
        hrow_ready, turn_ready, h32_ready, hh_ready, hl_ready = map(sem, (
            "hrow_ready", "turn_ready", "h32_ready", "hh_ready", "hl_ready"))
        c1_ready, y1_ready, diff_ready, ch_ready, cl_ready = map(sem, (
            "c1_ready", "y1_ready", "diff_ready", "ch_ready", "cl_ready"))
        h_stored = sem("h_stored")

        def sp_load(sp, n, q):
            wait(sp, turn_ready, count(n, KD * G, KD * (q - 1)))
            sp.sem_inc(loading, 1)
            base, off = n
            sp.dma_start(xa[q % 2][:, :, :],
                         io["x"][base * G + (off * G + q), :, :].rearrange("(j p) d -> p j d", p=P))\
                .then_inc(x_in[q % 2], 16)

        def act_layernorm(act, n, q):
            act.wait_ge(ve_ready, count(n, G, q + 1))
            nc.scalar.activation(rt[:, :], ve[:, :], ACT.Sqrt).then_inc(rt_ready, 1)
            act.wait_ge(ln_ready, count(n, G, q + 1))
            for j in range(NB):
                nc.scalar.activation(xa[q % 2][:, j, :], xa[q % 2][:, j, :], ACT.Relu,
                                     bias=ln[q % 2][:, 1, j:j + 1], scale=ln[q % 2][:, 0, j:j + 1])\
                    .then_inc(hrow_ready, 1)

        def act_h_out(act, n, q):
            wait(act, hl_ready, count(n, G, q))
            wait(act, h_stored, count(n, 16 * G, 16 * q))
            for c in range(KD):
                act.wait_ge(turn_ready, count(n, KD * G, KD * q + c + 1))
                nc.scalar.activation(h32[:, c, :], turn[c][:, :, :].rearrange("p j r -> p (j r)"), ACT.Copy)\
                    .then_inc(h32_ready, 1)
            act.wait_ge(h32_ready, count(n, KD * G, KD * (q + 1)))
            base, off = n
            act.dma_start(h_by_batch[base * G + (off * G + q), :, :, :], h32[:, :, :]).then_inc(h_stored, 16)

        def act_y_out(act, n, q):
            if q == 0:
                wait(act, diff_ready, count(n, SUMS))
                wait(act, cl_ready, count(n, NPROD, -NPROD + 1))
            for ob in range(KD):
                act.wait_ge(c1_ready, count(n, KD * G, KD * q + ob + 1))
                nc.scalar.activation(y1[:, :, ob, q, 2:2 + Q], c1p[ob][:, :, :].rearrange("p r c -> p c r"),
                                     ACT.Relu, bias=conv1_bias[:, ob:ob + 1], scale=conv1_scale[:, ob:ob + 1])\
                    .then_inc(y1_ready, 1)

        LN_STEPS = 6

        def dve_layernorm(dve, n, q):
            dve.wait_ge(x_in[q % 2], count(n, 2 * 16, 16 * (q // 2 + 1)))
            for j in range(NB):
                nc.vector.bn_stats(bst[:, j, :], xa[q % 2][:, j, :]).then_inc(bst_ready, 1)
            dve.wait_ge(bst_ready, count(n, NB * G, NB * (q + 1)))
            dve.sem_inc(aggregating, 1)
            for j in range(NB):
                nc.vector.bn_aggr(mv[:, j, :], bst[:, j, :]).then_inc(mv_ready, 1)
            dve.wait_ge(mv_ready, count(n, NB * G, NB * (q + 1)))
            nc.vector.tensor_scalar(ve[:, :], mv[:, :, 1], EPS, None, ALU.add).then_inc(ve_ready, 1)
            dve.wait_ge(rt_ready, count(n, G, q + 1))
            wait(dve, hrow_ready, count(n, NB * G, NB * (q - 1)))
            k = [0]

            def step(ins):
                k[0] += 1
                ins.then_inc(ln_step, 1)
                dve.wait_ge(ln_step, count(n, LN_STEPS * G, LN_STEPS * q + k[0]))
            rsqrt_step(nc.vector, step, r0[:, :], rt[:, :], ve[:, :], nt[:, :])
            step(nc.vector.tensor_scalar(ln[q % 2][:, 0, :], r0[:, :], H_SCALE, None, ALU.mult))
            nc.vector.scalar_tensor_tensor(out=ln[q % 2][:, 1, :], in0=mv[:, :, 0], scalar=-1.0,
                                   in1=ln[q % 2][:, 0, :], op0=ALU.mult, op1=ALU.mult).then_inc(ln_ready, 1)

        def dve_split(dve, n, q):
            dve.wait_ge(h32_ready, count(n, KD * G, KD * (q + 1)))
            wait(dve, c1_ready, count(n, KD * G, KD * q))
            nc.vector.tensor_copy(hh[:, :, :], h32[:, :, :]).then_inc(hh_ready, 1)
            dve.wait_ge(hh_ready, count(n, G, q + 1))
            nc.vector.tensor_tensor(hl[:, :, :], h32[:, :, :], hh[:, :, :], ALU.subtract).then_inc(hl_ready, 1)

        def pe_turn(pe, n, q):
            pe.wait_ge(hrow_ready, count(n, NB * G, NB * (q + 1)))
            for c in range(KD):
                wait(pe, h32_ready, count(n, KD * G, KD * (q - 1) + c + 1))
                for j in range(NB):
                    last = nc.tensor.transpose(turn[c][:, j, :], xa[q % 2][:, j, c * P:(c + 1) * P], ident[:, :])
                last.then_inc(turn_ready, 1)

        def pe_conv1(pe, n, q):
            pe.wait_ge(hl_ready, count(n, G, q + 1))
            for ob in range(KD):
                wait(pe, y1_ready, count(n, KD * G, KD * (q - 1) + ob + 1))
                pairs = [(w, h, k) for k in range(KD) for w, h in ((w1h, hh), (w1h, hl), (w1l, hh))]
                for i, (w, h, k) in enumerate(pairs):
                    last = nc.tensor.matmul(c1p[ob][:, :, :].rearrange("p r c -> p (r c)"),
                                            w[:, k, ob * P:(ob + 1) * P], h[:, k, :],
                                            start=(i == 0), stop=(i == len(pairs) - 1))
                last.then_inc(c1_ready, 1)

        with ExitStack() as tmp:
            tb = lambda name, shape, dt=F32: tmp.enter_context(nc.sbuf_tensor(name, shape, dt))
            raw2 = [tb(f"raw2_{o}", [P, D, TAPS]) for o in range(KD)]
            fa = [tb(f"fa{o}", [P, D, 8]) for o in range(KD)]
            s4 = [[tb(f"sums{i}", [P, D, 4])[:, :, :] for i in range(3)],
                  [t[:, 0:4 * D].rearrange("p (o t) -> p o t", t=4) for t in (mix, da, db)]]
            raw1 = tb("raw1", [P, KD, D])
            sq_junk = tb("sq_junk", [P, D])
            vec = tb("vec", [P, 8, KD])
            ones = tb("ones", [P, P])
            diag = tb("diag", [P, P])
            names = "work1 norm2 norm w1max w1pow w1scale w1inv w2max w2pow w2scale w2inv bound"
            small = {n: tb(n, [P, KD]) for n in names.split()}
            veps = tb("veps2", [P, 2, KD])
            root = tb("root2", [P, 2, KD])
            bn = tb("bn2", [P, 2, KD])
            work = tb("work2", [P, 2, KD])
            ymax, ypow, yscale, yinv = (tb(n, [P, 1]) for n in ("ymax", "ypow", "yscale", "yinv"))
            bank = [tmp.enter_context(nc.psum_tensor(f"wt{i}", [P, 4, P], F32)) for i in range(4)]
            bound_row = c1p[1][:, :, :].rearrange("p r c -> p (r c)").rearrange("p (k c) -> p k c", c=P)[:, 0:KD, :]
            names = ("ones_ready vec_in raw1_in raw2_in0 raw2_in1 id_in dve_step act_step veps_ready root_ready "
                     "w1_scaled w2_power w2_scaled sums_ready0 sums_ready1 sum_step norm_ready "
                     "diag_ready row_ready turned high_ready rest_ready")
            s = {n: tmp.enter_context(nc.semaphore(n)) for n in names.split()}
            PLAIN = (4, 5, 7, 8)
            units = [(ob, ib, p) for ob in range(KD)
                     for products in (PLAIN, [p for p in range(NPROD) if p not in PLAIN])
                     for ib in range(KD) for p in products]

            def unit_taps(ob, ib, p):
                out, t = [], TAP0[p]
                for view, n in tap_source(raw2[ob], fa[ob], s4[ob], p):
                    for k in range(n):
                        out.append((t, view[:, ib * P:(ib + 1) * P, k]))
                        t += 1
                return out

            chunks = []
            for ob, ib, p in units:
                taps = list(range(TAP0[p], TAP0[p] + PTAPS[p]))
                chunks.append((ob, ib, p, 0, 4))
                if len(taps) == 5:
                    chunks.append((ob, ib, p, 4, 1))
            half = KD + len(chunks) // KD
            cut = [KD + (half - KD) * q // G for q in range(G + 1)]
            every = KD + len(chunks)

            def sums(pool, g, ob):
                r2, f = raw2[ob], fa[ob]
                g.tensor_tensor(f[:, :, :], r2[:, :, 0:15:2], r2[:, :, 1:16:2], ALU.add).then_inc(s["sum_step"], 1)
                g.tensor_tensor(s4[ob][1], r2[:, :, 0:13:4], r2[:, :, 2:15:4], ALU.add)
                g.tensor_tensor(s4[ob][2], r2[:, :, 1:14:4], r2[:, :, 3:16:4], ALU.add)
                pool.wait_ge(s["sum_step"], ob + 1)
                return g.tensor_tensor(s4[ob][0], f[:, :, 0:7:2], f[:, :, 1:8:2], ALU.add)

            block = tmp.enter_context(nc.Block())

            @block.sync
            def _(sp):
                sp.dma_start(ident[:, :], io["ident"]).then_inc(s["id_in"], 16)
                sp.dma_start(raw1[:, :, :], io["conv1_w"].rearrange("(ob p) i k -> p ob (i k)", p=P)).then_inc(s["raw1_in"], 16)
                sp_load(sp, (0, 0), 0)
                sp_load(sp, (0, 0), 1)
                for ob in range(KD):
                    src = io["conv2_w"][ob * P:(ob + 1) * P, :, :]
                    sp.dma_start(raw2[ob][:, :, :], src).then_inc(s[f"raw2_in{ob}"], 16)
                sp_load(sp, (0, 0), 2)
                sp_load(sp, (0, 0), 3)

            @block.gpsimd
            def _(pool):
                with nc.allow_non_contiguous_dma(reason="256-element vectors"):
                    for j, n in enumerate(("bn1_g", "bn1_b", "bn1_m", "bn1_v", "bn2_g", "bn2_b", "bn2_m", "bn2_v")):
                        pool.dma_start(vec[:, j, :], io[n].rearrange("(k p) -> p k", p=P)).then_inc(s["vec_in"], 16)

                for ob in range(KD):
                    pool.wait_ge(s["w2_scaled"], ob + 1)
                    sums(pool, nc.gpsimd, ob).then_inc(s[f"sums_ready{ob}"], 1)

            @block.scalar
            def _(act):
                act.wait_ge(s["raw1_in"], 16)
                act.wait_ge(s["w1_scaled"], 1)
                for ob in range(KD):
                    if ob:
                        act.wait_ge(s["act_step"], ob)
                    nc.scalar.activation(sq_junk[:, :], raw1[:, ob, :], ACT.Square,
                                         accum_out=small["norm2"][:, ob:ob + 1]).then_inc(s["act_step"], 1)
                act.wait_ge(s["act_step"], KD)
                nc.scalar.activation(small["norm"][:, :], small["norm2"][:, :], ACT.Sqrt).then_inc(s["norm_ready"], 1)

                def highs(lo, hi):
                    for u in range(lo, hi):
                        act.wait_ge(s["turned"], u + 1)
                        if u < KD:
                            n, high = KD, w1h[:, :, u * P:(u + 1) * P]
                        else:
                            ob, ib, p, t, n = chunks[u - KD]
                            high = w2h[:, TAP0[p] + t:TAP0[p] + t + n, ib, ob * P:(ob + 1) * P]
                        nc.scalar.activation(high, bank[u % 4][:, 0:n, :], ACT.Copy).then_inc(s["high_ready"], 1)

                def scale_rows(ob):
                    act.wait_ge(s["w2_power"], ob + 1)
                    nc.scalar.activation(raw2[ob][:, :, :], raw2[ob][:, :, :], ACT.Copy,
                                         scale=small["w2scale"][:, ob:ob + 1]).then_inc(s["w2_scaled"], 1)

                g0 = (0, 0)
                highs(0, KD)
                act_layernorm(act, g0, 0)
                act_layernorm(act, g0, 1)
                scale_rows(0)
                act.wait_ge(s["veps_ready"], 1)
                nc.scalar.activation(root[:, :, :], veps[:, :, :], ACT.Sqrt).then_inc(s["root_ready"], 1)
                act_h_out(act, g0, 0)
                highs(cut[0], cut[1])
                act_h_out(act, g0, 1)
                scale_rows(1)
                act_layernorm(act, g0, 2)
                act_y_out(act, g0, 0)
                highs(cut[1], cut[2])
                act_h_out(act, g0, 2)
                act_layernorm(act, g0, 3)
                act_y_out(act, g0, 1)
                highs(cut[2], cut[3])
                act_h_out(act, g0, 3)
                act_y_out(act, g0, 2)
                highs(cut[3], cut[4])
                act_y_out(act, g0, 3)
                highs(half, every)

            @block.vector
            def _(dve):
                steps = [0]

                def link(ins):
                    steps[0] += 1
                    ins.then_inc(s["dve_step"], 1)
                    dve.wait_ge(s["dve_step"], steps[0])

                v = nc.vector
                v.memset(ones[:, :], 1.0).then_inc(s["ones_ready"], 1)
                v.memset(y1[:, :, :, :, :], 0.0).then_inc(pad_ready, 1)
                dve.wait_ge(pad_ready, 1)
                dve.wait_ge(s["raw1_in"], 16)
                link(v.tensor_reduce(small["w1max"][:, :], raw1[:, :, :], AX.X, ALU.max, apply_absolute_value=True))
                power_scale(v, link, small["w1max"][:, :], small["w1pow"][:, :], small["w1scale"][:, :],
                            small["w1inv"][:, :], W_TOP)
                for ob in range(KD):
                    ins = v.tensor_scalar(raw1[:, ob, :], raw1[:, ob, :], small["w1scale"][:, ob:ob + 1], None, ALU.mult)
                    if ob < KD - 1:
                        link(ins)
                    else:
                        ins.then_inc(s["w1_scaled"], 1)
                def rests(lo, hi):
                    for u in range(lo, hi):
                        dve.wait_ge(s["high_ready"], u + 1)
                        if u < KD:
                            o, h = w1l[:, :, u * P:(u + 1) * P], w1h[:, :, u * P:(u + 1) * P]
                            n = KD
                        else:
                            ob, ib, p, t, n = chunks[u - KD]
                            tap = TAP0[p] + t
                            o = w2l[:, tap:tap + n, ib, ob * P:(ob + 1) * P]
                            h = w2h[:, tap:tap + n, ib, ob * P:(ob + 1) * P]
                        v.tensor_tensor(o, bank[u % 4][:, 0:n, :], h, ALU.subtract).then_inc(s["rest_ready"], 1)

                def row_power(ob):
                    dve.wait_ge(s[f"raw2_in{ob}"], 16)
                    m = small["w2max"][:, ob:ob + 1]
                    link(v.tensor_reduce(m, raw2[ob][:, :, :], AX.XY, ALU.max, apply_absolute_value=True))
                    power_scale(v, link, m, small["w2pow"][:, ob:ob + 1], small["w2scale"][:, ob:ob + 1],
                                small["w2inv"][:, ob:ob + 1], W2_TOP)
                    dve.sem_inc(s["w2_power"], 1)

                g0 = (0, 0)
                dve_layernorm(dve, g0, 0)
                dve_layernorm(dve, g0, 1)
                row_power(0)
                dve.wait_ge(s["vec_in"], 8 * 16)
                vt = vec[:, :, :].rearrange("p (a c) k -> p a c k", a=2)
                link(v.tensor_scalar(veps[:, :, :], vt[:, :, 3, :], EPS, None, ALU.add))
                v.tensor_copy(work[:, :, :], veps[:, :, :]).then_inc(s["veps_ready"], 1)
                dve.wait_ge(s["root_ready"], 1)
                rsqrt_step(v, link, bn[:, :, :], root[:, :, :], veps[:, :, :], work[:, :, :])
                link(v.tensor_tensor(bn[:, :, :], bn[:, :, :], vt[:, :, 0, :], ALU.mult))
                link(v.tensor_tensor(work[:, :, :], vt[:, :, 2, :], bn[:, :, :], ALU.mult))
                link(v.tensor_tensor(veps[:, :, :], vt[:, :, 1, :], work[:, :, :], ALU.subtract))
                link(v.tensor_copy(conv2_bias[:, :], veps[:, 1, :]))
                dve.wait_ge(s["norm_ready"], 1)
                bound, t1 = small["bound"], small["work1"]
                link(v.tensor_tensor(bound[:, :], small["norm"][:, :], small["w1inv"][:, :], ALU.mult))
                link(v.scalar_tensor_tensor(out=t1[:, :], in0=bn[:, 0, :], scalar=-1.0, in1=bn[:, 0, :],
                                            op0=ALU.mult, op1=ALU.max))
                link(v.scalar_tensor_tensor(out=bound[:, :], in0=bound[:, :], scalar=16.25, in1=t1[:, :],
                                            op0=ALU.mult, op1=ALU.mult))
                link(v.scalar_tensor_tensor(out=t1[:, :], in0=veps[:, 0, :], scalar=-1.0, in1=veps[:, 0, :],
                                            op0=ALU.mult, op1=ALU.max))
                link(v.tensor_tensor(bound[:, :], bound[:, :], t1[:, :], ALU.add))
                for ob in range(KD):
                    if ob:
                        dve.wait_ge(s["row_ready"], ob)
                    v.tensor_scalar(diag[:, :], ident[:, :], bound[:, ob:ob + 1], None, ALU.mult)\
                        .then_inc(s["diag_ready"], 1)
                dve.wait_ge(s["row_ready"], KD)
                link(v.tensor_reduce(ymax[:, :], bound_row[:, :, :], AX.XY, ALU.max))
                power_scale(v, link, ymax[:, :], ypow[:, :], yscale[:, :], yinv[:, :], Y_TOP)
                link(v.tensor_scalar(conv1_bias[:, :], veps[:, 0, :], yscale[:, 0:1], None, ALU.mult))
                link(v.tensor_tensor(t1[:, :], bn[:, 0, :], small["w1inv"][:, :], ALU.mult))
                link(v.tensor_scalar(conv1_scale[:, :], t1[:, :], yscale[:, 0:1], float(2.0 ** -H_TOP),
                                     ALU.mult, ALU.mult))

                rests(0, KD)
                dve_split(dve, g0, 0)
                row_power(1)
                rests(cut[0], cut[1])
                dve_layernorm(dve, g0, 2)
                dve_split(dve, g0, 1)
                rests(cut[1], cut[2])
                dve_layernorm(dve, g0, 3)
                dve_split(dve, g0, 2)
                rests(cut[2], cut[3])
                dve_split(dve, g0, 3)
                rests(cut[3], every)
                link(v.tensor_tensor(t1[:, :], bn[:, 1, :], small["w2inv"][:, :], ALU.mult))
                link(v.tensor_scalar(conv2_scale[:, :], t1[:, :], yinv[:, 0:1], None, ALU.mult))

            @block.tensor
            def _(pe):
                def room(u):
                    if u >= 4:
                        pe.wait_ge(s["rest_ready"], u - 3)

                pe.wait_ge(s["id_in"], 16)
                pe.wait_ge(s["w1_scaled"], 1)
                for ob in range(KD):
                    for ib in range(KD):
                        last = nc.tensor.transpose(bank[ob][:, ib, :], raw1[:, ob, ib * P:(ib + 1) * P], ident[:, :])
                    last.then_inc(s["turned"], 1)
                for ob in range(KD):
                    pe.wait_ge(s["diag_ready"], ob + 1)
                    nc.tensor.matmul(bound_row[:, ob, :], ones[:, :], diag[:, :], start=True, stop=True)\
                        .then_inc(s["row_ready"], 1)

                def turns(lo, hi):
                    for u in range(lo, hi):
                        ob, ib, p, t, n = chunks[u - KD]
                        pe.wait_ge(s["w2_scaled"], ob + 1)
                        if p not in PLAIN:
                            pe.wait_ge(s[f"sums_ready{ob}"], 1)
                        room(u)
                        for j, (_, src) in enumerate(unit_taps(ob, ib, p)[t:t + n]):
                            last = nc.tensor.transpose(bank[u % 4][:, j, :], src, ident[:, :])
                        last.then_inc(s["turned"], 1)

                g0 = (0, 0)
                pe_turn(pe, g0, 0)
                for q in range(G):
                    if q + 1 < G:
                        pe_turn(pe, g0, q + 1)
                    turns(cut[q], cut[q + 1])
                    pe_conv1(pe, g0, q)
                turns(half, every)

        parts = [sb(n, [P, NPROD * CW // 2]) for n in ("ch", "cl")]
        ch, cl = (carve(t, 0, (NPROD, KD, G, QW), F16)[0] for t in parts)
        raw_hh, end = carve(parts[0], 0, (NHH, D))
        assert end <= RAW_AFTER * CW // 2
        raw_m, end = carve(parts[1], 0, (KD, D))
        raw_s, end = carve(parts[1], end, (D,))
        g_ones, end = carve(parts[1], end, (P,))
        g_diag, end = carve(parts[1], end, (P,))
        assert end <= RAW_AFTER * CW // 2
        sa, ga2, ga3, ha, hb = (sb(n, [P, KD, G, Q]) for n in ("sa", "ga2", "ga3", "ha", "hb"))
        co = sb("co", [P, KD, G, N])
        kp = [ctx.enter_context(nc.psum_tensor(f"kp{i}", [P, G, Q], F32)) for i in range(3)]
        prod_ready, taken, fin_ready = map(sem, ("prod_ready", "taken", "fin_ready"))
        stored = [sem(f"stored{i}") for i in range(KD)]
        flat = lambda c: y1[:, c, :, :, :].rearrange("p k g w -> p (k g w)")
        cflat = lambda t, p: t[:, p, :, :, :].rearrange("p k g w -> p (k g w)")
        whole, here, shifted = slice(0, CW), slice(0, CW - 1), slice(1, CW)
        D_OF = {1: 0, 2: 1, 3: 3, 4: 4, 5: 5, 6: 7, 7: 8, 8: 9}
        SRC = {1: mix, 2: mix, 3: db, 4: mix, 5: mix, 6: db, 7: mix, 8: mix}
        SHORT = {2, 5, 6, 7, 8}
        span = lambda p: here if p in SHORT else whole
        src_of = lambda p: (flat(3) if p == 0 else SRC[p][:, :])[:, span(p)]

        gw = shared["gates"]
        raw_ih = gw["raw_ih"]
        vih, vhh = sb("vih", [P, NHH]), sb("vhh", [P, NHH])
        NS = NHH + KD + 1
        wmax, wpow, wscale, winv = (sb(n, [P, NS]) for n in ("wmax", "wpow", "wscale", "winv"))
        kscale = sb("kscale", [P, NHH])
        (small_in, big_in, s_cleared, s_in, v_in, g_step, g_scaled, g_turned, g_high, g_rest, g_diag_ready,
         g_row_ready) = map(sem, ("small_in", "big_in", "s_cleared", "s_in", "v_in", "g_step", "g_scaled",
                                  "g_turned", "g_high", "g_rest", "g_diag_ready", "g_row_ready"))
        chunks = []
        paired = [slice(k, D, KD) for k in range(KD)]
        plain = [slice(D + k * P, D + (k + 1) * P) for k in range(KD)]
        for raw, blocks, inputs, high, rest in ((raw_hh, NHH, paired, gw["whh"], gw["whl"]),
                                                (raw_m, KD, paired, gw["wmh"], gw["wml"]),
                                                (raw_ih, NHH, paired + plain, gw["wih"], gw["wil"])):
            for o in range(blocks):
                cols = slice(o * P, (o + 1) * P)
                chunks.append(([raw[:, o, i] for i in inputs], high[:, :, cols], rest[:, :, cols]))
        chunks.append(([raw_s[:, i] for i in paired], gw["wsh"][:, :, :], gw["wsl"][:, :, :]))
        cut = [0, 4, 8, 12, len(chunks)]
        c1_rows = [b[:, :, :].rearrange("p r c -> p (r c)").rearrange("p (k c) -> p k c", c=P) for b in c1p]
        g_bank = [turn[0][:, :, :], turn[1][:, :, :]] + c1_rows
        inv_row = g_bank[3]
        GATE_STEPS = 11

        block = ctx.enter_context(nc.Block())

        @block.sync
        def _(sp):
            def gate_loads():
                sp.wait_ge(cl_ready, NPROD * NGROUP)
                sp.wait_ge(h_stored, 16 * B)
                pairs = lambda w: w.rearrange("(g p f) i -> p g (f i)", p=P, f=KD)
                sp.dma_start(raw_ih[:, :, :].rearrange("p (g f) i -> p g (f i)", f=KD), pairs(io["w_ih"])).then_inc(big_in, 16)
                sp.wait_ge(prod_ready, EV * (NGROUP - 1) + KD * RAW_AFTER)
                sp.dma_start(raw_hh[:, :, :].rearrange("p (g f) i -> p g (f i)", f=KD), pairs(io["w_hh"])).then_inc(small_in, 16)
                sp.dma_start(raw_m[:, :, :], io["w_msg"].rearrange("(o p) i -> p o i", p=P)).then_inc(small_in, 16)
                sp.dma_start(gw["rows"][:, :], io["rows"]).then_inc(small_in, 16)
                sp.wait_ge(s_cleared, 2)
                for r in S_ROWS:
                    sp.dma_start(raw_s[r:r + 3, :], io["w_se"]).then_inc(s_in, 16)

            def loads(n):
                for q in range(G):
                    sp_load(sp, n, q)
            loads((0, 1))
            with sp.Fori(1, NGROUP - 1) as g:
                loads((g, 1))
            gate_loads()

        @block.gpsimd
        def _(pool):
            def rest(n, p):
                pool.wait_ge(ch_ready, count(n, NPROD, p + 1))
                nc.gpsimd.tensor_tensor(cflat(cl, p)[:, span(p)], src_of(p), cflat(ch, p)[:, span(p)], ALU.subtract)\
                    .then_inc(cl_ready, 1)

            def group(n):
                for p in range(NPROD):
                    rest(n, p)
            group((0, 0))
            group((0, 1))
            with pool.Fori(1, NGROUP - 1) as g:
                group((g, 1))
            with nc.allow_non_contiguous_dma(reason="small vectors"):
                for vector, name in ((vih, "b_ih"), (vhh, "b_hh")):
                    pool.dma_start(vector[:, :].rearrange("p (g f) -> p g f", f=KD),
                                   io[name].rearrange("(g p f) -> p g f", p=P, f=KD)).then_inc(v_in, 16)
                for c in range(2):
                    pool.dma_start(gw["msg_bias"][:, c, :], io["b_msg"].partition_broadcast(P)).then_inc(v_in, 16)
                pool.wait_ge(s_cleared, 2)
                for r in S_ROWS:
                    pool.dma_start(gw["s_bias"][r:r + 3, :], io["b_se"].rearrange("(p a) -> p a", a=1)).then_inc(v_in, 16)

        @block.scalar
        def _(act):
            def high(n, p):
                wait(act, prod_ready, count(n, EV, -EV + KD * (p + 1)))
                if p == 0:
                    act.wait_ge(y1_ready, count(n, KD * G, KD * G))
                else:
                    act.wait_ge(diff_ready, count(n, SUMS, D_OF[p] + 1))
                nc.scalar.activation(cflat(ch, p)[:, span(p)], src_of(p), ACT.Copy).then_inc(ch_ready, 1)

            def finish(g):
                for ob in range(KD):
                    act.wait_ge(taken, count(g, EV, EV - KD + ob + 1))
                    nc.scalar.activation(co[:, ob, :, :], co[:, ob, :, :], ACT.Identity,
                                         bias=conv2_bias[:, ob:ob + 1], scale=conv2_scale[:, ob:ob + 1])\
                        .then_inc(fin_ready, 1)
                base, off = g
                for ob in range(KD):
                    act.wait_ge(fin_ready, count(g, KD, ob + 1))
                    act.dma_start(by_group[base + off, ob, :, :, :], co[:, ob, :, :]).then_inc(stored[ob], 16)

            def ahead(n):
                act_layernorm(act, n, 0)
                act_layernorm(act, n, 1)
                act_h_out(act, n, 0)
                act_y_out(act, n, 0)
                act_h_out(act, n, 1)
                act_layernorm(act, n, 2)
                act_y_out(act, n, 1)
                act_h_out(act, n, 2)
                act_layernorm(act, n, 3)
                act_y_out(act, n, 2)
                act_h_out(act, n, 3)
                act_y_out(act, n, 3)
                for p in range(NPROD - 1):
                    high(n, p)

            def gate_highs(lo, hi):
                for u in range(lo, hi):
                    sources, high_part, _ = chunks[u]
                    act.wait_ge(g_turned, u + 1)
                    nc.scalar.activation(high_part, g_bank[u % 4][:, 0:len(sources), :], ACT.Copy).then_inc(g_high, 1)

            for p in range(NPROD):
                high((0, 0), p)

            def both(g, n):
                ahead(n)
                finish(g)
                high(n, NPROD - 1)
            both((0, 0), (0, 1))
            with act.Fori(1, NGROUP - 1) as g:
                both((g, 0), (g, 1))
            for part in range(len(cut) - 1):
                gate_highs(cut[part], cut[part + 1])
            finish((0, NGROUP - 1))
            for ob in range(KD):
                act.wait_ge(stored[ob], 16 * NGROUP)
            act.wait_ge(h_stored, 16 * B)

        @block.vector
        def _(dve):
            v = nc.vector
            def take(g, m):
                p, ob = divmod(m, KD)
                dve.wait_ge(prod_ready, count(g, EV, m + 1))
                wait(dve, taken, count(g, EV, m - 1))
                if p == 4:
                    wait(dve, stored[ob], count(g, 16))
                bank = kp[m % 3][:, :, :]
                o4 = co[:, ob, :, :].rearrange("p g (r c) -> p c g r", c=4)
                if p == 0:
                    last = v.tensor_copy(sa[:, ob, :, :], bank)
                elif p == 1:
                    last = v.tensor_tensor(ga2[:, ob, :, :], bank, sa[:, ob, :, :], ALU.add)
                elif p == 2:
                    last = v.tensor_tensor(ga3[:, ob, :, :], bank, sa[:, ob, :, :], ALU.add)
                elif p in (3, 6):
                    v.tensor_tensor(ha[:, ob, :, :], bank, ga2[:, ob, :, :], ALU.add)
                    last = v.tensor_tensor(hb[:, ob, :, :], bank, ga3[:, ob, :, :], ALU.add)
                else:
                    phase, addend = {4: (0, ha), 5: (2, hb), 7: (1, ha), 8: (3, hb)}[p]
                    last = v.tensor_tensor(o4[:, phase, :, :], bank, addend[:, ob, :, :], ALU.add)
                last.then_inc(taken, 1)

            def difference(n, d):
                q0, q1, q2, q3 = (flat(c) for c in range(4))
                a, b = da[:, :], db[:, :]
                if d == 0:
                    dve.wait_ge(y1_ready, count(n, KD * G, KD * G))
                else:
                    dve.wait_ge(diff_ready, count(n, SUMS, d))
                free = {0: -1, 1: 1, 3: 6 - NPROD, 4: 2, 5: 4, 7: 3, 8: 5, 9: 7}
                if d in free:
                    wait(dve, cl_ready, count(n, NPROD, free[d] + 1))
                w, h, f = whole, here, shifted
                out, x, y = [
                    (mix[:, w], q1[:, w], q3[:, w]),
                    (mix[:, h], q1[:, f], q3[:, h]),
                    (da[:, w], q0[:, w], q1[:, w]),
                    (db[:, w], q2[:, w], q3[:, w]),
                    (mix[:, w], a[:, w], b[:, w]),
                    (mix[:, h], a[:, f], b[:, h]),
                    (da[:, w], q2[:, w], q1[:, w]),
                    (db[:, h], q0[:, f], q3[:, h]),
                    (mix[:, h], a[:, h], b[:, h]),
                    (mix[:, h], a[:, f], b[:, h]),
                ][d]
                v.tensor_tensor(out, x, y, ALU.subtract).then_inc(diff_ready, 1)

            steps = [0]

            def link(ins):
                steps[0] += 1
                ins.then_inc(g_step, 1)
                dve.wait_ge(g_step, steps[0])

            def gate_clear():
                v.memset(raw_s[:, :], 0.0).then_inc(s_cleared, 1)
                v.memset(gw["s_bias"][:, :], 0.0).then_inc(s_cleared, 1)
                link(v.memset(g_ones[:, :], 1.0))

            def gate_scales():
                dve.wait_ge(small_in, 3 * 16)
                dve.wait_ge(s_in, 16 * len(S_ROWS))
                v.tensor_reduce(wmax[:, 0:NHH], raw_hh[:, :, :], AX.X, ALU.max, apply_absolute_value=True)
                v.tensor_reduce(wmax[:, NHH:NHH + KD], raw_m[:, :, :], AX.X, ALU.max, apply_absolute_value=True)
                link(v.tensor_reduce(wmax[:, NS - 1:NS], raw_s[:, :], AX.X, ALU.max, apply_absolute_value=True))
                power_scale(v, link, wmax[:, :], wpow[:, :], wscale[:, :], winv[:, :], W_TOP)
                v.tensor_scalar(kscale[:, :], wscale[:, 0:NHH], H_SCALE, None, ALU.mult)
                link(v.tensor_scalar(winv[:, :], winv[:, :], 1.0 / H_SCALE, None, ALU.mult))
                v.tensor_copy(gw["gate_inv"][:, :], winv[:, 0:NHH])
                v.tensor_scalar(gw["gate_half"][:, :], winv[:, 0:NHH], 0.5, None, ALU.mult)
                link(v.tensor_copy(gw["s_inv"][:, :], winv[:, NS - 1:NS]))

            def gate_scaled():
                for o in range(NHH):
                    v.tensor_scalar(raw_hh[:, o, :], raw_hh[:, o, :], wscale[:, o:o + 1], None, ALU.mult)
                for o in range(KD):
                    v.tensor_scalar(raw_m[:, o, :], raw_m[:, o, :], wscale[:, NHH + o:NHH + o + 1], None, ALU.mult)
                v.tensor_scalar(raw_s[:, :], raw_s[:, :], wscale[:, NS - 1:NS], None, ALU.mult).then_inc(g_scaled, 1)
                dve.wait_ge(big_in, 16)
                for o in range(NHH):
                    last = v.tensor_scalar(raw_ih[:, o, :], raw_ih[:, o, :], kscale[:, o:o + 1], None, ALU.mult)
                last.then_inc(g_scaled, 1)

            def gate_biases():
                gate_bias, hn_bias = gw["gate_bias"], gw["hn_bias"]
                dve.wait_ge(v_in, 16 * (4 + len(S_ROWS)))
                link(v.tensor_tensor(gate_bias[:, 0:4], vih[:, 0:4], vhh[:, 0:4], ALU.add))
                v.tensor_scalar(gate_bias[:, 0:4], gate_bias[:, 0:4], 0.5, None, ALU.mult)
                v.tensor_copy(gate_bias[:, 4:6], vih[:, 4:6])
                v.tensor_scalar(hn_bias[:, :], vhh[:, 4:6], 0.5, None, ALU.mult)
                for o in range(KD):
                    if o:
                        dve.wait_ge(g_row_ready, o)
                    v.tensor_scalar(g_diag[:, :], ident[:, :], winv[:, NHH + o:NHH + o + 1], None, ALU.mult)\
                        .then_inc(g_diag_ready, 1)
                dve.wait_ge(g_row_ready, KD)
                for c in range(2):
                    last = v.tensor_copy(gw["msg_inv"][:, c, :], inv_row[:, 0:KD, :].rearrange("p k o -> p (k o)"))
                link(last)

            def gate_rests(lo, hi):
                for u in range(lo, hi):
                    sources, high_part, rest_part = chunks[u]
                    if high_part.dtype == F32R:
                        high_part = high_part.bitcast(F32)
                    dve.wait_ge(g_high, u + 1)
                    v.tensor_tensor(rest_part, g_bank[u % 4][:, 0:len(sources), :], high_part, ALU.subtract)\
                        .then_inc(g_rest, 1)

            def both(g, n):
                def banks(p):
                    take(g, KD * p)
                    take(g, KD * p + 1)

                if n is None:
                    for p in range(RAW_AFTER):
                        banks(p)
                    gate_clear()
                    gate_scales()
                    banks(3)
                    gate_scaled()
                    banks(4)
                    gate_biases()
                    for part in range(4):
                        gate_rests(cut[part], cut[part + 1])
                        banks(5 + part)
                    return
                dve_layernorm(dve, n, 0)
                banks(0)
                dve_layernorm(dve, n, 1)
                banks(1)
                banks(2)
                dve_split(dve, n, 0)
                banks(3)
                dve_layernorm(dve, n, 2)
                dve_split(dve, n, 1)
                banks(4)
                dve_layernorm(dve, n, 3)
                dve_split(dve, n, 2)
                banks(5)
                dve_split(dve, n, 3)
                banks(6)
                for d in range(4):
                    difference(n, d)
                take(g, 14)
                difference(n, 4)
                take(g, 15)
                difference(n, 5)
                difference(n, 6)
                difference(n, 7)
                take(g, 16)
                difference(n, 8)
                take(g, 17)
                difference(n, 9)

            for d in range(SUMS):
                difference((0, 0), d)
            both((0, 0), (0, 1))
            with dve.Fori(1, NGROUP - 1) as g:
                both((g, 0), (g, 1))
            both((0, NGROUP - 1), None)

        @block.tensor
        def _(pe):
            def product(g, p):
                pe.wait_ge(cl_ready, count(g, NPROD, p + 1))
                for ob in range(KD):
                    m = KD * p + ob
                    wait(pe, taken, count(g, EV, m - 2))
                    steps = [(w, c, t, k) for t in range(PTAPS[p]) for k in range(KD)
                             for w, c in ((w2h, ch), (w2h, cl), (w2l, ch))]
                    for i, (w, c, t, k) in enumerate(steps):
                        last = nc.tensor.matmul(kp[m % 3][:, :, :], w[:, TAP0[p] + t, k, ob * P:(ob + 1) * P],
                                                c[:, p, k, :, t:t + Q], start=(i == 0), stop=(i == len(steps) - 1))
                    last.then_inc(prod_ready, 1)

            def gate_rows():
                pe.wait_ge(y1_ready, KD * G * NGROUP)
                for o in range(KD):
                    pe.wait_ge(g_diag_ready, o + 1)
                    nc.tensor.matmul(inv_row[:, o, :], g_ones[:, :], g_diag[:, :], start=True, stop=True)\
                        .then_inc(g_row_ready, 1)

            def gate_turns(lo, hi):
                if lo == 0:
                    pe.wait_ge(g_scaled, 2)
                    pe.wait_ge(h32_ready, KD * G * NGROUP)
                for u in range(lo, hi):
                    if u == 3:
                        pe.wait_ge(g_step, GATE_STEPS)
                    if u >= 4:
                        pe.wait_ge(g_rest, u - 3)
                    for j, source in enumerate(chunks[u][0]):
                        last = nc.tensor.transpose(g_bank[u % 4][:, j, :], source, ident[:, :])
                    last.then_inc(g_turned, 1)

            def both(g, n):
                if n is None:
                    for p in range(5):
                        product(g, p)
                    gate_rows()
                    for part in range(4):
                        gate_turns(cut[part], cut[part + 1])
                        product(g, 5 + part)
                    return
                for p in range(3):
                    product(g, p)
                pe_turn(pe, n, 0)
                for q in range(G):
                    product(g, 3 + q)
                    pe_conv1(pe, n, q)
                    if q + 1 < G:
                        pe_turn(pe, n, q + 1)
                product(g, 7)
                product(g, 8)

            both((0, 0), (0, 1))
            with pe.Fori(1, NGROUP - 1) as g:
                both((g, 0), (g, 1))
            both((0, NGROUP - 1), None)


def gate_constants(nc, ctx):
    sb = lambda name, shape, dt=F32: ctx.enter_context(nc.sbuf_tensor(name, shape, dt))
    g = allocate(nc, ctx, GATE_WEIGHTS)
    sb("room_left", [P, ROOM_LEFT])
    g.update({
        "gate_inv": sb("gate_inv", [P, NHH]),
        "gate_half": sb("gate_half", [P, NHH]),
        "gate_bias": sb("gate_bias", [P, NHH]),
        "hn_bias": sb("hn_bias", [P, KD]),
        "s_inv": sb("s_inv", [P, 1]),
        "s_bias": sb("s_bias", [P, 1]),
        "msg_inv": sb("msg_inv", [P, 2, D]),
        "msg_bias": sb("msg_bias", [P, 2, D]),
        "rows": sb("rows", [P, 6]),
    })
    return g


def gate_phase(nc, io, scratch, shared, out):
    ident, h_scratch = shared["ident"], shared["h_scratch"]
    ctx = ExitStack()
    with ctx:
        sb = lambda name, shape, dt=F32: ctx.enter_context(nc.sbuf_tensor(name, shape, dt))
        sem = lambda name: ctx.enter_context(nc.semaphore(name))
        g = shared["gates"]
        whh, whl, wih, wil, wmh, wml, wsh, wsl, gate_inv, gate_half, gate_bias, hn_bias, s_inv, s_bias, msg_inv, \
            msg_bias, rows = (g[n] for n in "whh whl wih wil wmh wml wsh wsl gate_inv gate_half gate_bias hn_bias "
                              "s_inv s_bias msg_inv msg_bias rows".split())
        two = range(2)
        h_next = sb("h_next", [P, KD, N])
        adj_t = [sb(f"adj_t{i}", [P, N // SQ, SQ, NB]) for i in two]
        mask_t = sb("mask_t", [P, NB, N])
        xc_t = [sb(f"xc_t{i}", [P, KD, N]) for i in two]
        out_t = [sb(f"out_t{i}", [P, N // SQ, CHUNK]) for i in two]
        turned = [sb(f"turned{i}", [P, N]) for i in two]
        hs = [sb(f"hs{i}", [P, KD, N]) for i in two]
        hh = [sb(f"hh2{i}", [P, KD, N], F16) for i in two]
        hl = [sb(f"hl2{i}", [P, KD, N], F16) for i in two]
        sf, lin_right, lin_left = sb("sf", [P, N]), sb("lin_right", [P, N]), sb("lin_left", [P, N])
        shi = sb("shi", [P, N], F32R)
        s_right, s_left = sb("s_right", [P, N], F32R), sb("s_left", [P, N], F32R)
        mg = [sb(f"mg{i}", [P, 2, D]) for i in two]
        mh = sb("mh", [P, NB, D], F32R)
        ml = sb("ml", [P, NB, D], F32R)
        ex = [sb(f"ex{i}", [P, N]) for i in two]
        ah = [sb(f"ah{i}", [P, N], F32R) for i in two]
        al = [sb(f"al{i}", [P, N], F32R) for i in two]
        ch = [sb(f"ch2{i}", [P, KD, N], F32R) for i in two]
        cl = [sb(f"cl2{i}", [P, KD, N], F32R) for i in two]
        nh = sb("nh", [P, KD, N], F32R)
        nl = sb("nl", [P, KD, N], F32R)
        rg, zg, gh, nn = (sb(n, [P, N]) for n in ("rg", "zg", "gh", "nn"))
        zg = [zg, sb("zg1", [P, N])]
        oo = [sb(f"oo{i}", [P, N]) for i in two]
        pg = [ctx.enter_context(nc.psum_tensor(f"pg{i}", [P, N], F32)) for i in range(3)]
        px = [ctx.enter_context(nc.psum_tensor(f"px{i}", [P, N], F32)) for i in range(KD)]
        pu = [ctx.enter_context(nc.psum_tensor(f"pu{i}", [P, N], F32)) for i in range(3)]
        x_in, adj_in, xc_in, out_st = ([sem(f"{n}{i}") for i in two] for n in ("xt_in", "adj_in", "xc_in", "out_st"))
        moving, h_in = sem("moving"), sem("h_in")
        hs_ready, hh_ready, hl_ready = map(sem, ("hs_ready", "hh2_ready", "hl2_ready"))
        (s_ready, sf_ready, shi_ready, sr_lin, s_right_ready, sl_lin, s_left_ready) = map(sem, (
            "s_ready", "sf_ready", "shi_ready", "sr_lin", "s_right_ready", "sl_lin", "s_left_ready"))
        (m_ready, m_scaled, m_biased, mh_ready, ml_ready) = map(sem, (
            "m_ready", "m_scaled", "m_biased", "mh_ready", "ml_ready"))
        (dist_ready, ex_ready, mask_ready, a_ready, ah_ready, al_ready, x_step) = map(sem, (
            "dist_ready", "ex_ready", "mask_ready", "a_ready", "ah_ready", "al_ready", "x_step"))
        (nmp_h, nmp_l, ct_ready, ch_ready, cl_ready) = map(sem, ("nmp_h", "nmp_l", "ct_ready", "ch2_ready", "cl2_ready"))
        (gate_ready, act_gate, u_ready, v_ready, n_ready, d_ready, w_ready, o_ready, ot_ready, out_ready) = map(sem, (
            "gate_ready", "act_gate", "u_ready", "v_ready", "n_ready", "d_ready", "w_ready", "o_ready",
            "ot_ready", "out_ready"))
        R0, HN0, Z0, IN0, R1, HN1, Z1, IN1 = range(8)
        BANK = {R0: 0, HN0: 1, Z0: 2, IN0: 0, R1: 1, HN1: 2, Z1: 0, IN1: 1}
        block = ctx.enter_context(nc.Block())
        nxt = lambda b, k=1: (b[0], b[1] + k)
        par = lambda b: b[1] % 2

        def index(b):
            return b[0] + b[1]

        def index_known(b):
            return b[0] + b[1] if isinstance(b[0], int) else None

        PREV = {R0: (Z1, -1), HN0: (IN1, -1), Z0: (HN1, -1), IN0: (R0, 0), R1: (HN0, 0), HN1: (Z0, 0),
                Z1: (IN0, 0), IN1: (R1, 0)}
        ACT_ORDER = {R0: 1, HN0: 2, Z0: 3, R1: 4, HN1: 5, Z1: 6}

        def bank_free(eng, b, k):
            prev, back = PREV[k]
            if prev in ACT_ORDER:
                wait(eng, act_gate, count(nxt(b, back), 6, ACT_ORDER[prev]))
            else:
                wait(eng, v_ready, count(nxt(b, back), 2, 1 if prev == IN0 else 2))

        def run(eng, both):
            both(None, None, (0, 0))
            both(None, (0, 0), (0, 1))
            both((0, 0), (0, 1), (0, 2))
            with eng.Fori(1, B // 2 - 1) as pair:
                b = pair * 2
                both((b, -1), (b, 0), (b, 1))
                both((b, 0), (b, 1), (b, 2))
            both((0, B - 3), (0, B - 2), (0, B - 1))
            both((0, B - 2), (0, B - 1), None)
            both((0, B - 1), None, None)

        def arrived(eng, sems, b, parts=1):
            base, off = b
            if isinstance(base, int):
                eng.wait_ge(sems[par(b)], 16 * parts * ((base + off) // 2 + 1))
            else:
                eng.wait_ge(sems[par(b)], base * (8 * parts) + 16 * parts * (off // 2 + 1))

        @block.sync
        def _(sp):
            paired = lambda t, k: t[k, :, :, :].rearrange("k q n -> (k q) n").rearrange("(p f) n -> p f n", f=KD)
            groups = [(slice(a * SQ, (a + 1) * SQ), slice(a * CHUNK, (a + 1) * CHUNK)) for a in range(NB)]

            def loads(b):
                i, k = par(b), index(b)
                wait(sp, hl_ready, count(b, 1))
                sp.sem_inc(moving, 1)
                wait(sp, hs_ready, count(b, 1))
                sp.sem_inc(moving, 1)
                sp.dma_start(h_next[:, :, :], paired(h_scratch, k)).then_inc(h_in, 16)
                wait(sp, mask_ready, count(nxt(b, -1), NB))
                sp.sem_inc(moving, 1)
                for a in range(NB):
                    sp.dma_start(adj_t[i][a * SQ:(a + 1) * SQ, :, :, :],
                                 io["adj"][k, :, a * P:(a + 1) * P].rearrange("(b c) (r j) -> c b r j", c=SQ, r=SQ))\
                        .then_inc(adj_in[i], 16)
                wait(sp, cl_ready, count(nxt(b, -1), 1))
                sp.sem_inc(moving, 1)
                sp.dma_start(xc_t[i][:, :, :], paired(scratch, k)).then_inc(xc_in[i], 16)

            def residual(b):
                if index_known(b) is None or index_known(b) >= 2:
                    arrived(sp, out_st, nxt(b, -2), NB)
                    sp.sem_inc(moving, 1)
                for parts, features in groups:
                    sp.dma_start(out_t[par(b)][parts, :, :],
                                 io["x"][index(b), :, features].rearrange("(b c) w -> c b w", c=SQ))\
                        .then_inc(x_in[par(b)], 16)

            def store(p):
                sp.wait_ge(out_ready, count(p, 2, 2))
                sp.sem_inc(moving, 1)
                for parts, features in groups:
                    sp.dma_start(out[index(p), :, features].rearrange("(b c) w -> c b w", c=SQ),
                                 out_t[par(p)][parts, :, :]).then_inc(out_st[par(p)], 16)

            def both(p, b, n):
                if p is not None:
                    store(p)
                if n is not None:
                    residual(n)
                    if index_known(n) != B - 1:
                        loads(nxt(n))

            loads((0, 0))
            run(sp, both)
            for i in two:
                sp.wait_ge(out_st[i], 16 * NB * (B // 2))

        @block.gpsimd
        def _(pool):
            def masked_rest(n, m):
                pool.wait_ge(ah_ready, count(n, NB, m + 1))
                nc.gpsimd.tensor_tensor(al[m % 2][:, :], ex[m % 2][:, :], ah[m % 2][:, :].bitcast(F32), ALU.subtract)\
                    .then_inc(al_ready, 1)

            def out_add(b, f):
                t = out_t[par(b)][:, :, f::KD]
                arrived(pool, x_in, b, NB)
                pool.wait_ge(ot_ready, count(b, 2, f + 1))
                nc.gpsimd.tensor_tensor(t, turned[f][:, :].rearrange("p (b r) -> p b r", r=SQ), t, ALU.add)\
                    .then_inc(out_ready, 1)

            def both(p, b, n):
                if p is not None:
                    out_add(p, 1)
                if n is not None:
                    masked_rest(n, 0)
                    masked_rest(n, 1)
                if b is not None:
                    out_add(b, 0)
                if n is not None:
                    masked_rest(n, 2)
                    masked_rest(n, 3)

            run(pool, both)

        @block.scalar
        def _(act):
            A = nc.scalar.activation

            def tanh_n(b, f):
                act.wait_ge(v_ready, count(b, 2, f + 1))
                A(nn[:, :], nn[:, :], ACT.Tanh, bias=gate_bias[:, 4 + f:5 + f]).then_inc(n_ready, 1)

            def h_high(n):
                act.wait_ge(h_in, count(n, 16, 16))
                wait(act, gate_ready, count(nxt(n, -1), 8))
                A(hh[par(n)][:, :, :], h_next[:, :, :], ACT.Copy).then_inc(hh_ready, 1)

            def h_keep(n):
                wait(act, d_ready, count(nxt(n, -1), 2))
                A(hs[par(n)][:, :, :], h_next[:, :, :], ACT.Copy).then_inc(hs_ready, 1)

            def gate(b, k):
                f = 1 if k in (R1, HN1, Z1) else 0
                act.wait_ge(gate_ready, count(b, 8, k + 1))
                if k in (R0, R1):
                    wait(act, u_ready, count(b, 2, f))
                    A(rg[:, :], pg[BANK[k]][:, :], ACT.Tanh, bias=gate_bias[:, f:f + 1],
                      scale=gate_half[:, f:f + 1]).then_inc(act_gate, 1)
                elif k in (Z0, Z1):
                    wait(act, w_ready, count(nxt(b, -1), 2, f + 1))
                    A(zg[f][:, :], pg[BANK[k]][:, :], ACT.Tanh, bias=gate_bias[:, 2 + f:3 + f],
                      scale=gate_half[:, 2 + f:3 + f]).then_inc(act_gate, 1)
                else:
                    wait(act, v_ready, count(b, 2, f))
                    A(gh[:, :], pg[BANK[k]][:, :], ACT.Identity, bias=hn_bias[:, f:f + 1],
                      scale=gate_half[:, 4 + f:5 + f]).then_inc(act_gate, 1)

            def s_out(n):
                act.wait_ge(s_ready, count(n, 1, 1))
                wait(act, s_left_ready, count(n, 1))
                A(sf[0:64, :], pu[0][0:64, :], ACT.Identity, bias=s_bias[0:64, :], scale=s_inv[0:64, :])
                A(sf[64:128, :], pu[0][64:128, :], ACT.Square, bias=s_bias[64:128, :], scale=s_inv[64:128, :])\
                    .then_inc(sf_ready, 1)
                act.wait_ge(sf_ready, count(n, 1, 1))
                A(lin_right[:, :], sf[:, :], ACT.Identity, bias=rows[:, 2:3], scale=rows[:, 1:2]).then_inc(sr_lin, 1)
                A(lin_left[:, :], sf[:, :], ACT.Identity, bias=rows[:, 5:6], scale=rows[:, 4:5]).then_inc(sl_lin, 1)

            def messages(n):
                for m in range(2):
                    act.wait_ge(m_biased, count(n, 2, m + 1))
                    if m == 0:
                        wait(act, x_step, count(n, NB))
                    A(mh[:, 2 * m:2 * m + 2, :], mg[m][:, :, :], ACT.Relu).then_inc(mh_ready, 1)

            def exps(n, m):
                act.wait_ge(dist_ready, count(n, NB, m + 1))
                wait(act, al_ready, count(n, NB, m - 1))
                A(ex[m % 2][:, :], pu[m % 2][:, :], ACT.Exp).then_inc(ex_ready, 1)

            def mask_high(n, m):
                act.wait_ge(a_ready, count(n, NB, m + 1))
                wait(act, x_step, count(n, NB, m - 1))
                A(ah[m % 2][:, :], ex[m % 2][:, :], ACT.Copy).then_inc(ah_ready, 1)

            def conv_high(n):
                act.wait_ge(ct_ready, count(n, 1, 1))
                wait(act, gate_ready, count(nxt(n, -1), 8))
                A(ch[par(n)][:, :, :], xc_t[par(n)][:, :, :], ACT.Relu).then_inc(ch_ready, 1)

            def message_high(b):
                for c in range(KD):
                    act.wait_ge(x_step, count(b, NB, NB))
                    if c == 0:
                        wait(act, gate_ready, count(b, 8))
                    A(nh[:, c, :], px[c][:, :], ACT.Copy).then_inc(nmp_h, 1)

            def both(p, b, n):
                if b is not None:
                    message_high(b)
                if p is not None:
                    tanh_n(p, 1)
                if n is not None:
                    h_high(n)
                if b is not None:
                    gate(b, R0)
                if n is not None:
                    h_keep(n)
                if b is not None:
                    gate(b, HN0)
                    gate(b, Z0)
                if n is not None:
                    s_out(n)
                    messages(n)
                    exps(n, 0)
                if b is not None:
                    tanh_n(b, 0)
                if n is not None:
                    mask_high(n, 0)
                if b is not None:
                    gate(b, R1)
                if n is not None:
                    exps(n, 1)
                    mask_high(n, 1)
                if b is not None:
                    gate(b, HN1)
                if n is not None:
                    exps(n, 2)
                    mask_high(n, 2)
                if b is not None:
                    gate(b, Z1)
                if n is not None:
                    exps(n, 3)
                    mask_high(n, 3)
                    conv_high(n)

            run(act, both)

        @block.vector
        def _(dve):
            v = nc.vector

            def message_split(b):
                for c in range(KD):
                    dve.wait_ge(nmp_h, count(b, KD, c + 1))
                    v.tensor_tensor(nl[:, c, :], px[c][:, :], nh[:, c, :].bitcast(F32), ALU.subtract).then_inc(nmp_l, 1)

            def gate_mul(b, f):
                dve.wait_ge(act_gate, count(b, 6, 2 + 3 * f))
                v.scalar_tensor_tensor(out=gh[:, :], in0=rg[:, :], scalar=1.0, in1=gh[:, :],
                                       op0=ALU.add, op1=ALU.mult).then_inc(u_ready, 1)

            def gate_add(b, f):
                dve.wait_ge(gate_ready, count(b, 8, IN0 + 1 + 4 * f))
                dve.wait_ge(u_ready, count(b, 2, f + 1))
                v.scalar_tensor_tensor(out=nn[:, :], in0=pg[BANK[IN1 if f else IN0]][:, :],
                                       scalar=gate_inv[:, 4 + f:5 + f], in1=gh[:, :],
                                       op0=ALU.mult, op1=ALU.add).then_inc(v_ready, 1)

            def gate_end(b, f):
                o = oo[f][:, :]
                dve.wait_ge(n_ready, count(b, 2, f + 1))
                wait(dve, ot_ready, count(nxt(b, -1), 2, f + 1))
                v.scalar_tensor_tensor(out=o, in0=hs[par(b)][:, f, :], scalar=1.0 / H_SCALE, in1=nn[:, :],
                                       op0=ALU.mult, op1=ALU.subtract).then_inc(d_ready, 1)
                dve.wait_ge(act_gate, count(b, 6, 3 + 3 * f))
                dve.wait_ge(d_ready, count(b, 2, f + 1))
                v.scalar_tensor_tensor(out=o, in0=zg[f][:, :], scalar=1.0, in1=o, op0=ALU.add, op1=ALU.mult)\
                    .then_inc(w_ready, 1)
                dve.wait_ge(w_ready, count(b, 2, f + 1))
                v.scalar_tensor_tensor(out=o, in0=o, scalar=0.5, in1=nn[:, :], op0=ALU.mult, op1=ALU.add)\
                    .then_inc(o_ready, 1)

            def turn_out(b, f):
                dve.wait_ge(o_ready, count(b, 2, f + 1))
                wait(dve, out_ready, count(nxt(b, -1), 2, f + 1))
                v.transpose(turned[f][:, :], oo[f][:, :]).then_inc(ot_ready, 1)

            def h_rest(n):
                i = par(n)
                dve.wait_ge(hh_ready, count(n, 1, 1))
                v.tensor_tensor(hl[i][:, :, :], h_next[:, :, :], hh[i][:, :, :], ALU.subtract).then_inc(hl_ready, 1)

            def mask_turn(n, j):
                if j == 0:
                    arrived(dve, adj_in, n, NB)
                wait(dve, a_ready, count(n, NB, j + 1 - NB))
                v.transpose(mask_t[:, j, :], adj_t[par(n)][:, :, :, j]).then_inc(mask_ready, 1)

            def s_split(n):
                dve.wait_ge(sf_ready, count(n, 1, 1))
                v.tensor_copy(shi[:, :], sf[:, :]).then_inc(shi_ready, 1)
                dve.wait_ge(shi_ready, count(n, 1, 1))
                for dst, col, part, lin, done in ((s_right, 0, lin_right, sr_lin, s_right_ready),
                                                  (s_left, 3, lin_left, sl_lin, s_left_ready)):
                    dve.wait_ge(lin, count(n, 1, 1))
                    wait(dve, dist_ready, count(n, NB))
                    v.scalar_tensor_tensor(out=dst[:, :], in0=shi[:, :].bitcast(F32), scalar=rows[:, col:col + 1],
                                           in1=part[:, :], op0=ALU.mult, op1=ALU.add).then_inc(done, 1)

            def message_scale(n):
                for m in range(2):
                    dve.wait_ge(m_ready, count(n, 2, m + 1))
                    wait(dve, ml_ready, count(nxt(n, -1), 2, m + 1))
                    v.tensor_tensor(mg[m][:, :, :], pu[1 + m][:, :].rearrange("p (a d) -> p a d", d=D),
                                    msg_inv[:, :, :], ALU.mult).then_inc(m_scaled, 1)
                    dve.wait_ge(m_scaled, count(n, 2, m + 1))
                    v.tensor_tensor(mg[m][:, :, :], mg[m][:, :, :], msg_bias[:, :, :], ALU.add).then_inc(m_biased, 1)

            def message_rest(n, m):
                dve.wait_ge(mh_ready, count(n, 2, m + 1))
                v.scalar_tensor_tensor(out=ml[:, 2 * m:2 * m + 2, :].rearrange("p a d -> p (a d)"),
                                       in0=mg[m][:, :, :].rearrange("p a d -> p (a d)"), scalar=0.0,
                                       in1=mh[:, 2 * m:2 * m + 2, :].bitcast(F32).rearrange("p a d -> p (a d)"),
                                       op0=ALU.max, op1=ALU.subtract).then_inc(ml_ready, 1)

            def mask(n, m):
                dve.wait_ge(mask_ready, count(n, NB, m + 1))
                dve.wait_ge(ex_ready, count(n, NB, m + 1))
                v.tensor_tensor(ex[m % 2][:, :], ex[m % 2][:, :], mask_t[:, m, :], ALU.mult).then_inc(a_ready, 1)

            def conv_sum(n):
                i = par(n)
                arrived(dve, xc_in, n)
                dve.wait_ge(hs_ready, count(n, 1, 1))
                v.scalar_tensor_tensor(out=xc_t[i][:, :, :].rearrange("p k n -> p (k n)"),
                                       in0=hs[i][:, :, :].rearrange("p k n -> p (k n)"), scalar=1.0 / H_SCALE,
                                       in1=xc_t[i][:, :, :].rearrange("p k n -> p (k n)"),
                                       op0=ALU.mult, op1=ALU.add).then_inc(ct_ready, 1)

            def conv_rest(n):
                i = par(n)
                dve.wait_ge(ch_ready, count(n, 1, 1))
                v.scalar_tensor_tensor(out=cl[i][:, :, :].rearrange("p k n -> p (k n)"),
                                       in0=xc_t[i][:, :, :].rearrange("p k n -> p (k n)"), scalar=0.0,
                                       in1=ch[i][:, :, :].bitcast(F32).rearrange("p k n -> p (k n)"),
                                       op0=ALU.max, op1=ALU.subtract).then_inc(cl_ready, 1)

            def both(p, b, n):
                if b is not None:
                    conv_rest(b)
                    message_split(b)
                if p is not None:
                    gate_end(p, 1)
                if n is not None:
                    h_rest(n)
                if p is not None:
                    turn_out(p, 1)
                if n is not None:
                    for j in range(NB):
                        mask_turn(n, j)
                if b is not None:
                    gate_mul(b, 0)
                if n is not None:
                    s_split(n)
                    message_scale(n)
                if b is not None:
                    gate_add(b, 0)
                if n is not None:
                    message_rest(n, 0)
                    mask(n, 0)
                    message_rest(n, 1)
                if b is not None:
                    gate_end(b, 0)
                if n is not None:
                    mask(n, 1)
                if b is not None:
                    turn_out(b, 0)
                    gate_mul(b, 1)
                if n is not None:
                    conv_sum(n)
                    mask(n, 2)
                    mask(n, 3)
                if b is not None:
                    gate_add(b, 1)

            run(dve, both)

        @block.tensor
        def _(pe):
            mm = nc.tensor.matmul

            def of_block(t, j):
                return t[:, j::NB]

            def gate(b, k):
                i = par(b)
                f = 1 if k >= R1 else 0
                o = {R0: 0, R1: 1, Z0: 2, Z1: 3, HN0: 4, HN1: 5, IN0: 4, IN1: 5}[k]
                cols = slice(o * P, (o + 1) * P)
                bank = pg[BANK[k]][:, :]
                steps = []
                if k not in (IN0, IN1):
                    steps += [(w[:, c, cols], h[i][:, c, :]) for c in range(KD)
                              for w, h in ((whh, hh), (whh, hl), (whl, hh))]
                if k not in (HN0, HN1):
                    steps += [(w[:, c, cols], t[:, c, :]) for c in range(KD)
                              for w, t in ((wih, ch[i]), (wih, cl[i]), (wil, ch[i]))]
                    message = len(steps)
                    steps += [(w[:, KD + c, cols], t[:, c, :]) for c in range(KD)
                              for w, t in ((wih, nh), (wih, nl), (wil, nh))]
                bank_free(pe, b, k)
                for j, (w, t) in enumerate(steps):
                    if k == R0 and j == 3 * KD:
                        pe.wait_ge(cl_ready, count(b, 1, 1))
                    if k == R0 and j >= message and (j - message) % 3 == 0:
                        pe.wait_ge(nmp_l, count(b, KD, (j - message) // 3 + 1))
                    last = mm(bank, w, t, start=(j == 0), stop=(j == len(steps) - 1))
                last.then_inc(gate_ready, 1)

            def distance_rows_mm(n):
                i = par(n)
                pe.wait_ge(hl_ready, count(n, 1, 1))
                wait(pe, ex_ready, count(n, NB))
                steps = [(w[:, c, :], h[i][:, c, :]) for c in range(KD) for w, h in ((wsh, hh), (wsh, hl), (wsl, hh))]
                for j, (w, t) in enumerate(steps):
                    last = mm(pu[0][:, :], w, t, start=(j == 0), stop=(j == len(steps) - 1))
                last.then_inc(s_ready, 1)

            def messages(n):
                i = par(n)
                for m in range(NB):
                    steps = [(of_block(h[i][:, c, :], m), w[:, c, :]) for c in range(KD)
                             for h, w in ((hh, wmh), (hh, wml), (hl, wmh))]
                    for j, (h, w) in enumerate(steps):
                        last = mm(pu[1 + m // 2][:, (m % 2) * D:(m % 2 + 1) * D], h, w,
                                  start=(j == 0), stop=(j == len(steps) - 1))
                    if m % 2:
                        last.then_inc(m_ready, 1)

            def distance(n, m):
                if m == 0:
                    pe.wait_ge(s_left_ready, count(n, 1, 1))
                elif m == 1:
                    pe.wait_ge(m_scaled, count(n, 2, 1))
                else:
                    pe.wait_ge(ex_ready, count(n, NB, m - 1))
                mm(pu[m % 2][:, :], of_block(s_left, m), s_right[:, :], start=True, stop=True).then_inc(dist_ready, 1)

            def aggregate(n, m):
                if m == 0:
                    pe.wait_ge(ml_ready, count(n, 2, 2))
                    wait(pe, nmp_l, count(n, KD))
                pe.wait_ge(al_ready, count(n, NB, m + 1))
                for c in range(KD):
                    cols = slice(c * P, (c + 1) * P)
                    for j, (w, t) in enumerate(((mh, ah), (mh, al), (ml, ah))):
                        last = mm(px[c][:, :], w[:, m, cols], t[m % 2][:, :],
                                  start=(m == 0 and j == 0), stop=(m == NB - 1 and j == 2))
                last.then_inc(x_step, 1)

            def both(p, b, n):
                if b is not None:
                    gate(b, R0)
                if b is not None:
                    gate(b, HN0)
                if b is not None:
                    gate(b, Z0)
                if n is not None:
                    distance_rows_mm(n)
                    messages(n)
                if b is not None:
                    gate(b, IN0)
                if n is not None:
                    distance(n, 0)
                if b is not None:
                    gate(b, R1)
                if n is not None:
                    distance(n, 1)
                if b is not None:
                    gate(b, HN1)
                if n is not None:
                    distance(n, 2)
                    aggregate(n, 0)
                if b is not None:
                    gate(b, Z1)
                if n is not None:
                    aggregate(n, 1)
                    distance(n, 3)
                if b is not None:
                    gate(b, IN1)
                if n is not None:
                    aggregate(n, 2)
                    aggregate(n, 3)

            run(pe, both)


_NAMES = {
    "x": "x", "adj": "adj", "L0_gnn_w_se": "w_se", "L0_gnn_b_se": "b_se", "L0_gnn_conv1_w": "conv1_w",
    "L0_gnn_bn1_g": "bn1_g", "L0_gnn_bn1_b": "bn1_b", "L0_gnn_bn1_m": "bn1_m", "L0_gnn_bn1_v": "bn1_v",
    "L0_gnn_conv2_w": "conv2_w", "L0_gnn_bn2_g": "bn2_g", "L0_gnn_bn2_b": "bn2_b", "L0_gnn_bn2_m": "bn2_m",
    "L0_gnn_bn2_v": "bn2_v", "L0_gnn_w_msg": "w_msg", "L0_gnn_b_msg": "b_msg", "L0_gnn_w_ih": "w_ih",
    "L0_gnn_b_ih": "b_ih", "L0_gnn_w_hh": "w_hh", "L0_gnn_b_hh": "b_hh",
}


def build(nc, io, out):
    scratch = nc.dram_tensor("conv_scratch", (B, KD, P, N), F32, kind="Internal").ap()
    with ExitStack() as ctx:
        shared = {
            "ident": ctx.enter_context(nc.sbuf_tensor("ident", [P, P], F32)),
            "h_scratch": nc.dram_tensor("h_scratch", (B, KD, P, N), F32, kind="Internal").ap(),
        }
        with ExitStack() as early:
            shared["input_side"] = allocate(nc, early, INPUT_SIDE)
        shared["gates"] = gate_constants(nc, ctx)
        convolution_phase(nc, io, scratch, shared)
        gate_phase(nc, io, scratch, shared, out)


def kernel(**inputs):
    import concourse.bacc as bacc
    from concourse.bass_utils import run_bass_kernel_spmd

    nc = bacc.Bacc("TRN2", target_bir_lowering=False, num_devices=1)
    arrays = {f"in_{short}": np.ascontiguousarray(inputs[name]) for name, short in _NAMES.items()}
    arrays["in_ident"] = np.eye(P, dtype=np.float32)
    arrays["in_rows"] = distance_rows()
    io = {name[3:]: nc.dram_tensor(name, a.shape, mybir.dt.from_np(a.dtype), kind="ExternalInput").ap()
          for name, a in arrays.items()}
    out = nc.dram_tensor("out_y", (B, N, D), F32, kind="ExternalOutput").ap()
    build(nc, io, out)
    result = run_bass_kernel_spmd(nc, [arrays], core_ids=[0])
    return result.results[0]["out_y"]
```

```python
from contextlib import ExitStack

import concourse.bass as bass
import numpy as np
from concourse import mybir

DT = mybir.dt
F32, F16, F32R, I32 = DT.float32, DT.float16, DT.float32r, DT.int32
ALU = mybir.AluOpType
ACT = mybir.ActivationFunctionType
AX = mybir.AxisListType

P = 128
B, N, D = 32, 512, 256
KD = D // P
NB = N // P
EPS = 1e-5
H_TOP = 11
H_SCALE = float(2 ** H_TOP)
TAPS, PAD = 17, 8
G = 4
NGROUP = B // G
Q = N // 4
QW = (N + 2 * PAD) // 4
CW = KD * G * QW
W_TOP = 14
W2_TOP = 12
Y_TOP = 12
TINY = 1e-18
EXPO = 0x7F800000
PTAPS = [5, 5, 4, 5, 5, 4] + 9 * [2]
NPROD = len(PTAPS)
C1, C2, C3 = (range(c, c + 3) for c in (6, 9, 12))
TAP0 = [sum(PTAPS[:p]) for p in range(NPROD)]
NTAP = sum(PTAPS)
E = Q // 2
EW = QW // 2
BANK0 = [KD * p if p < C1[0] else KD * C1[0] + p - C1[0] for p in range(NPROD + 1)]
EV = BANK0[NPROD]
SUMS = 16
RAW_AFTER = 3
S_ROWS = [0, 3, 6, 64, 67, 70, 73]
KI = 2 * KD
NHH = 3 * D // P
SQ = 32
CHUNK = KD * SQ


def distance_rows():
    t = np.zeros((P, 6), np.float32)
    ar, br, cr, al, bl, cl = range(6)
    t[0:3, ar] = 1
    t[3:6, ar], t[3:6, br] = -1, 1
    t[6:9, ar] = 1
    t[0:6, al] = 2
    t[6:9, al], t[6:9, bl] = -2, 2
    t[64:67, ar] = 1
    t[67:70, ar], t[67:70, br] = -1, 1
    t[64:70, cl] = -1
    t[70:73, al] = -1
    t[73:76, al], t[73:76, bl] = 1, -1
    t[70:76, cr] = 1
    return t


def carve(room, start, shape, dtype=F32):
    size = int(np.prod(shape)) // (2 if dtype == F16 else 1)
    names = "abcde"[:len(shape)]
    flat = room[:, start:start + size]
    if dtype != F32:
        flat = flat.bitcast(dtype)
    form = f"p ({' '.join(names)}) -> p {' '.join(names)}"
    return flat.rearrange(form, **dict(zip(names, shape))), start + size


def paired(t, k):
    return t[k, :, :, :].rearrange("k q n -> (k q) n").rearrange("(p f) n -> p f n", f=KD)


def load_adjacency(sp, io, k, tile, done):
    for a in range(NB):
        sp.dma_start(tile[a * SQ:(a + 1) * SQ, :, :, :],
                     io["adj"][k, :, a * P:(a + 1) * P].rearrange("(b c) (r j) -> c b r j", c=SQ, r=SQ))\
            .then_inc(done, 16)


def allocate(nc, ctx, parts):
    return {name: ctx.enter_context(nc.sbuf_tensor(name, [P, *shape], dtype)) for name, shape, dtype in parts}


INPUT_SIDE = [
    ("y1", (4, KD, G, QW), F32),
    ("mix", (CW,), F32),
    ("da", (CW,), F32), ("db", (CW,), F32),
    ("xa0", (NB, D), F32), ("xa1", (NB, D), F32),
    ("h32", (KD, N), F32), ("hh", (KD, N), F16), ("hl", (KD, N), F16),
    ("w1h", (KD, D), F16), ("w1l", (KD, D), F16),
]
GATE_WEIGHTS = [
    ("wih", (KI, 3 * D), F32R), ("wil", (KI, 3 * D), F32R),
    ("whh", (KD, 3 * D), F16), ("whl", (KD, 3 * D), F16),
    ("wmh", (KD, D), F16), ("wml", (KD, D), F16),
    ("wsh", (KD, P), F16), ("wsl", (KD, P), F16),
    ("raw_ih", (NHH, 2 * D), F32),
]
RAW_WORDS = (NHH + KD + 1) * D + 2 * P
FIRST = [("behind_raw", (RAW_WORDS,), F32), ("h_next", (KD, N), F32), ("hs0", (KD, N), F32),
         ("hh20", (KD, N), F16), ("hl20", (KD, N), F16), ("adj0", (N // SQ, SQ, NB), F32)]
words = lambda parts: sum(int(np.prod(shape)) // (2 if dtype == F16 else 1) for _, shape, dtype in parts)
ROOM_LEFT = words(INPUT_SIDE) - words(GATE_WEIGHTS)
assert ROOM_LEFT >= 0


def count(index, per, k=0):
    base, off = index
    return base * per + (off * per + k)


def wait(eng, sem, value):
    if isinstance(value, int) and value <= 0:
        return
    eng.wait_ge(sem, value)


def tap_sums(raw, fa, b1, c1):
    w, f, b, c = ((lambda t, v=v: v[:, :, t]) for v in (raw, fa, b1, c1))
    last = [[w(TAPS - 1)]]
    four = range(4)

    def third_level(tap):
        return [[[tap(0), tap(1)], [tap(2), tap(3)]], [[tap(0)], [tap(2)]], [[tap(1)], [tap(3)]]]

    products = [[[f(2 * t), f(2 * t + 1)] for t in four] + last,
                [[f(2 * t)] for t in four] + last,
                [[f(2 * t + 1)] for t in four],
                [[b(t)] for t in four] + last,
                [[w(4 * t)] for t in four] + last,
                [[w(4 * t + 2)] for t in four]]
    return products + third_level(c) + third_level(lambda t: w(4 * t + 1)) + third_level(lambda t: w(4 * t + 3))


def rsqrt_step(eng, link, out, root, value, tmp):
    link(eng.reciprocal(out, root))
    link(eng.tensor_tensor(tmp, out, out, ALU.mult))
    link(eng.tensor_tensor(tmp, tmp, value, ALU.mult))
    link(eng.tensor_scalar(tmp, tmp, -0.5, 1.5, ALU.mult, ALU.add))
    link(eng.tensor_tensor(out, out, tmp, ALU.mult))


def power_scale(eng, link, biggest, power, scale, inverse, top):
    link(eng.tensor_scalar(biggest, biggest, TINY, None, ALU.max))
    link(eng.tensor_scalar(power.bitcast(I32), biggest.bitcast(I32), EXPO, None, ALU.bitwise_and))
    link(eng.reciprocal(scale, power))
    link(eng.tensor_scalar(scale, scale, float(2.0 ** top), None, ALU.mult))
    link(eng.tensor_scalar(inverse, power, float(2.0 ** -top), None, ALU.mult))


def convolution_phase(nc, io, scratch, shared):
    ident, h_scratch = shared["ident"], shared["h_scratch"]
    by_group = scratch.rearrange("(r g) k p n -> r k p g n", g=G)
    h_by_batch = h_scratch.rearrange("b k p n -> b p k n")
    ctx = ExitStack()
    with ctx:
        sb = lambda name, shape, dt=F32: ctx.enter_context(nc.sbuf_tensor(name, shape, dt))
        sem = lambda name: ctx.enter_context(nc.semaphore(name))
        w2_room = sb("w2_room", [P, NTAP * KD * D // 2])
        w2h, _ = carve(w2_room, 0, (NTAP, KD, D), F16)
        w2l = sb("w2l", [P, NTAP, KD, D], F16)
        side = shared["input_side"]
        y1, mix, da, db, h32, hh, hl, w1h, w1l = (side[n] for n in "y1 mix da db h32 hh hl w1h w1l".split())
        xa = [side["xa0"], side["xa1"]]
        conv1_scale = sb("conv1_scale", [P, KD])
        conv1_bias = sb("conv1_bias", [P, KD])
        conv2_scale = sb("conv2_scale", [P, KD])
        conv2_bias = sb("conv2_bias", [P, KD])

        bst = sb("bst", [P, NB, 6])
        mv = sb("mv", [P, NB, 2])
        ve = sb("ve", [P, NB])
        rt = sb("rt", [P, NB])
        r0 = sb("r0", [P, NB])
        nt = sb("nt", [P, NB])
        ln = [sb(f"ln{i}", [P, 2, NB]) for i in range(2)]
        turn = [ctx.enter_context(nc.psum_tensor(f"turn{i}", [P, NB, P], F32)) for i in range(KD)]
        c1p = [ctx.enter_context(nc.psum_tensor(f"c1p{i}", [P, Q, 4], F32)) for i in range(KD)]
        x_in = [sem(f"x_in{i}") for i in range(2)]
        loading, aggregating = sem("loading"), sem("aggregating")
        pad_ready, bst_ready, mv_ready, ve_ready, rt_ready, ln_step, ln_ready = map(sem, (
            "pad_ready", "bst_ready", "mv_ready", "ve_ready", "rt_ready", "ln_step", "ln_ready"))
        hrow_ready, turn_ready, h32_ready, hh_ready, hl_ready = map(sem, (
            "hrow_ready", "turn_ready", "h32_ready", "hh_ready", "hl_ready"))
        c1_ready, y1_ready, diff_ready, ch_ready, cl_ready = map(sem, (
            "c1_ready", "y1_ready", "diff_ready", "ch_ready", "cl_ready"))
        h_stored = sem("h_stored")

        def sp_load(sp, n, q):
            wait(sp, turn_ready, count(n, KD * G, KD * (q - 1)))
            sp.sem_inc(loading, 1)
            base, off = n
            sp.dma_start(xa[q % 2][:, :, :],
                         io["x"][base * G + (off * G + q), :, :].rearrange("(j p) d -> p j d", p=P))\
                .then_inc(x_in[q % 2], 16)

        def act_layernorm(act, n, q):
            act.wait_ge(ve_ready, count(n, G, q + 1))
            nc.scalar.activation(rt[:, :], ve[:, :], ACT.Sqrt).then_inc(rt_ready, 1)
            act.wait_ge(ln_ready, count(n, G, q + 1))
            for j in range(NB):
                nc.scalar.activation(xa[q % 2][:, j, :], xa[q % 2][:, j, :], ACT.Relu,
                                     bias=ln[q % 2][:, 1, j:j + 1], scale=ln[q % 2][:, 0, j:j + 1])\
                    .then_inc(hrow_ready, 1)

        def act_h_out(act, n, q):
            wait(act, hl_ready, count(n, G, q))
            wait(act, h_stored, count(n, 16 * G, 16 * q))
            for c in range(KD):
                act.wait_ge(turn_ready, count(n, KD * G, KD * q + c + 1))
                nc.scalar.activation(h32[:, c, :], turn[c][:, :, :].rearrange("p j r -> p (j r)"), ACT.Copy)\
                    .then_inc(h32_ready, 1)
            act.wait_ge(h32_ready, count(n, KD * G, KD * (q + 1)))
            base, off = n
            act.dma_start(h_by_batch[base * G + (off * G + q), :, :, :], h32[:, :, :]).then_inc(h_stored, 16)

        def act_y_out(act, n, q):
            if q == 0:
                wait(act, diff_ready, count(n, SUMS))
                wait(act, cl_ready, count(n, NPROD))
            for ob in range(KD):
                act.wait_ge(c1_ready, count(n, KD * G, KD * q + ob + 1))
                nc.scalar.activation(y1[:, :, ob, q, 2:2 + Q], c1p[ob][:, :, :].rearrange("p r c -> p c r"),
                                     ACT.Relu, bias=conv1_bias[:, ob:ob + 1], scale=conv1_scale[:, ob:ob + 1])\
                    .then_inc(y1_ready, 1)

        LN_STEPS = 6

        def dve_layernorm(dve, n, q):
            dve.wait_ge(x_in[q % 2], count(n, 2 * 16, 16 * (q // 2 + 1)))
            for j in range(NB):
                nc.vector.bn_stats(bst[:, j, :], xa[q % 2][:, j, :]).then_inc(bst_ready, 1)
            dve.wait_ge(bst_ready, count(n, NB * G, NB * (q + 1)))
            dve.sem_inc(aggregating, 1)
            for j in range(NB):
                nc.vector.bn_aggr(mv[:, j, :], bst[:, j, :]).then_inc(mv_ready, 1)
            dve.wait_ge(mv_ready, count(n, NB * G, NB * (q + 1)))
            nc.vector.tensor_scalar(ve[:, :], mv[:, :, 1], EPS, None, ALU.add).then_inc(ve_ready, 1)
            dve.wait_ge(rt_ready, count(n, G, q + 1))
            wait(dve, hrow_ready, count(n, NB * G, NB * (q - 1)))
            k = [0]

            def step(ins):
                k[0] += 1
                ins.then_inc(ln_step, 1)
                dve.wait_ge(ln_step, count(n, LN_STEPS * G, LN_STEPS * q + k[0]))
            rsqrt_step(nc.vector, step, r0[:, :], rt[:, :], ve[:, :], nt[:, :])
            step(nc.vector.tensor_scalar(ln[q % 2][:, 0, :], r0[:, :], H_SCALE, None, ALU.mult))
            nc.vector.scalar_tensor_tensor(out=ln[q % 2][:, 1, :], in0=mv[:, :, 0], scalar=-1.0,
                                           in1=ln[q % 2][:, 0, :], op0=ALU.mult, op1=ALU.mult).then_inc(ln_ready, 1)

        def dve_split(dve, n, q):
            dve.wait_ge(h32_ready, count(n, KD * G, KD * (q + 1)))
            wait(dve, c1_ready, count(n, KD * G, KD * q))
            nc.vector.tensor_copy(hh[:, :, :], h32[:, :, :]).then_inc(hh_ready, 1)
            dve.wait_ge(hh_ready, count(n, G, q + 1))
            nc.vector.tensor_tensor(hl[:, :, :], h32[:, :, :], hh[:, :, :], ALU.subtract).then_inc(hl_ready, 1)

        def pe_turn(pe, n, q):
            pe.wait_ge(hrow_ready, count(n, NB * G, NB * (q + 1)))
            for c in range(KD):
                wait(pe, h32_ready, count(n, KD * G, KD * (q - 1) + c + 1))
                for j in range(NB):
                    last = nc.tensor.transpose(turn[c][:, j, :], xa[q % 2][:, j, c * P:(c + 1) * P], ident[:, :])
                last.then_inc(turn_ready, 1)

        def pe_conv1(pe, n, q):
            pe.wait_ge(hl_ready, count(n, G, q + 1))
            for ob in range(KD):
                wait(pe, y1_ready, count(n, KD * G, KD * (q - 1) + ob + 1))
                pairs = [(w, h, k) for k in range(KD) for w, h in ((w1h, hh), (w1h, hl), (w1l, hh))]
                for i, (w, h, k) in enumerate(pairs):
                    last = nc.tensor.matmul(c1p[ob][:, :, :].rearrange("p r c -> p (r c)"),
                                            w[:, k, ob * P:(ob + 1) * P], h[:, k, :],
                                            start=(i == 0), stop=(i == len(pairs) - 1))
                last.then_inc(c1_ready, 1)

        with ExitStack() as tmp:
            tb = lambda name, shape, dt=F32: tmp.enter_context(nc.sbuf_tensor(name, shape, dt))
            raw2 = [tb(f"raw2_{o}", [P, D, TAPS]) for o in range(KD)]
            fa = [carve(shared["co_room"], o * D * 8, (D, 8))[0] for o in range(KD)]
            s4 = [[tb(f"sums{i}", [P, D, 4])[:, :, :] for i in range(2)],
                  [t[:, 0:4 * D].rearrange("p (o t) -> p o t", t=4) for t in (mix, da)]]
            raw1 = tb("raw1", [P, KD, D])
            sq_junk = tb("sq_junk", [P, D])
            vec = tb("vec", [P, 8, KD])
            ones = tb("ones", [P, P])
            diag = tb("diag", [P, P])
            names = "work1 norm2 norm w1max w1pow w1scale w1inv w2max w2pow w2scale w2inv bound"
            small = {n: tb(n, [P, KD]) for n in names.split()}
            veps = tb("veps2", [P, 2, KD])
            root = tb("root2", [P, 2, KD])
            bn = tb("bn2", [P, 2, KD])
            work = tb("work2", [P, 2, KD])
            ymax, ypow, yscale, yinv = (tb(n, [P, 1]) for n in ("ymax", "ypow", "yscale", "yinv"))
            bank = [tmp.enter_context(nc.psum_tensor(f"wt{i}", [P, 4, P], F32)) for i in range(4)]
            bound_row = c1p[1][:, :, :].rearrange("p r c -> p (r c)").rearrange("p (k c) -> p k c", c=P)[:, 0:KD, :]
            names = ("ones_ready vec_in raw1_in raw2_in0 raw2_in1 id_in dve_step act_step veps_ready root_ready "
                     "w1_scaled w2_power w2_scaled sums_ready0 sums_ready1 norm_ready "
                     "diag_ready row_ready turned high_ready rest_ready")
            s = {n: tmp.enter_context(nc.semaphore(n)) for n in names.split()}
            chunks = []
            for ob in range(KD):
                taps = tap_sums(raw2[ob], fa[ob], *s4[ob])
                for runs, summed in (([(4, 5), (*C2, *C3)], False), ([(0, 1, 2, 3), C1], True)):
                    for ib in range(KD):
                        for run in runs:
                            sources = [[v[:, ib * P:(ib + 1) * P] for v in tap] for p in run for tap in taps[p]]
                            for t in range(0, len(sources), 4):
                                chunks.append((ob, ib, TAP0[run[0]] + t, sources[t:t + 4], summed))
            beside = KD + len(chunks) * 3 // 4
            cut = [KD + (beside - KD) * q // G for q in range(G + 1)]
            every = KD + len(chunks)

            def sums(g, ob):
                r2 = raw2[ob]
                g.tensor_tensor(fa[ob], r2[:, :, 0:15:2], r2[:, :, 1:16:2], ALU.add)
                g.tensor_tensor(s4[ob][0], r2[:, :, 0:13:4], r2[:, :, 2:15:4], ALU.add)
                return g.tensor_tensor(s4[ob][1], r2[:, :, 1:14:4], r2[:, :, 3:16:4], ALU.add)

            block = tmp.enter_context(nc.Block())

            @block.sync
            def _(sp):
                sp.dma_start(ident[:, :], io["ident"]).then_inc(s["id_in"], 16)
                sp.dma_start(raw1[:, :, :], io["conv1_w"].rearrange("(ob p) i k -> p ob (i k)", p=P)).then_inc(s["raw1_in"], 16)
                sp_load(sp, (0, 0), 0)
                sp_load(sp, (0, 0), 1)
                for ob in range(KD):
                    src = io["conv2_w"][ob * P:(ob + 1) * P, :, :]
                    sp.dma_start(raw2[ob][:, :, :], src).then_inc(s[f"raw2_in{ob}"], 16)
                sp_load(sp, (0, 0), 2)
                sp_load(sp, (0, 0), 3)

            @block.gpsimd
            def _(pool):
                with nc.allow_non_contiguous_dma(reason="256-element vectors"):
                    for j, n in enumerate(("bn1_g", "bn1_b", "bn1_m", "bn1_v", "bn2_g", "bn2_b", "bn2_m", "bn2_v")):
                        pool.dma_start(vec[:, j, :], io[n].rearrange("(k p) -> p k", p=P)).then_inc(s["vec_in"], 16)

                for ob in range(KD):
                    pool.wait_ge(s["w2_scaled"], ob + 1)
                    sums(nc.gpsimd, ob).then_inc(s[f"sums_ready{ob}"], 1)

            @block.scalar
            def _(act):
                act.wait_ge(s["raw1_in"], 16)
                act.wait_ge(s["w1_scaled"], 1)
                for ob in range(KD):
                    if ob:
                        act.wait_ge(s["act_step"], ob)
                    nc.scalar.activation(sq_junk[:, :], raw1[:, ob, :], ACT.Square,
                                         accum_out=small["norm2"][:, ob:ob + 1]).then_inc(s["act_step"], 1)
                act.wait_ge(s["act_step"], KD)
                nc.scalar.activation(small["norm"][:, :], small["norm2"][:, :], ACT.Sqrt).then_inc(s["norm_ready"], 1)

                def highs(lo, hi):
                    for u in range(lo, hi):
                        act.wait_ge(s["turned"], u + 1)
                        if u < KD:
                            n, high = KD, w1h[:, :, u * P:(u + 1) * P]
                        else:
                            ob, ib, tap, sources, _ = chunks[u - KD]
                            n = len(sources)
                            high = w2h[:, tap:tap + n, ib, ob * P:(ob + 1) * P]
                        nc.scalar.activation(high, bank[u % 4][:, 0:n, :], ACT.Copy).then_inc(s["high_ready"], 1)

                def scale_rows(ob):
                    act.wait_ge(s["w2_power"], ob + 1)
                    nc.scalar.activation(raw2[ob][:, :, :], raw2[ob][:, :, :], ACT.Copy,
                                         scale=small["w2scale"][:, ob:ob + 1]).then_inc(s["w2_scaled"], 1)

                g0 = (0, 0)
                highs(0, KD)
                act_layernorm(act, g0, 0)
                act_layernorm(act, g0, 1)
                scale_rows(0)
                act.wait_ge(s["veps_ready"], 1)
                nc.scalar.activation(root[:, :, :], veps[:, :, :], ACT.Sqrt).then_inc(s["root_ready"], 1)
                act_h_out(act, g0, 0)
                highs(cut[0], cut[1])
                act_h_out(act, g0, 1)
                scale_rows(1)
                act_layernorm(act, g0, 2)
                act_y_out(act, g0, 0)
                highs(cut[1], cut[2])
                act_h_out(act, g0, 2)
                act_layernorm(act, g0, 3)
                act_y_out(act, g0, 1)
                highs(cut[2], cut[3])
                act_h_out(act, g0, 3)
                act_y_out(act, g0, 2)
                highs(cut[3], cut[4])
                act_y_out(act, g0, 3)
                highs(beside, every)

            @block.vector
            def _(dve):
                steps = [0]

                def link(ins):
                    steps[0] += 1
                    ins.then_inc(s["dve_step"], 1)
                    dve.wait_ge(s["dve_step"], steps[0])

                v = nc.vector
                v.memset(ones[:, :], 1.0).then_inc(s["ones_ready"], 1)
                v.memset(y1[:, :, :, :, :], 0.0).then_inc(pad_ready, 1)
                dve.wait_ge(pad_ready, 1)
                dve.wait_ge(s["raw1_in"], 16)
                link(v.tensor_reduce(small["w1max"][:, :], raw1[:, :, :], AX.X, ALU.max, apply_absolute_value=True))
                power_scale(v, link, small["w1max"][:, :], small["w1pow"][:, :], small["w1scale"][:, :],
                            small["w1inv"][:, :], W_TOP)
                for ob in range(KD):
                    ins = v.tensor_scalar(raw1[:, ob, :], raw1[:, ob, :], small["w1scale"][:, ob:ob + 1], None, ALU.mult)
                    if ob < KD - 1:
                        link(ins)
                    else:
                        ins.then_inc(s["w1_scaled"], 1)
                def rests(lo, hi):
                    for u in range(lo, hi):
                        dve.wait_ge(s["high_ready"], u + 1)
                        if u < KD:
                            o, h = w1l[:, :, u * P:(u + 1) * P], w1h[:, :, u * P:(u + 1) * P]
                            n = KD
                        else:
                            ob, ib, tap, sources, _ = chunks[u - KD]
                            n = len(sources)
                            o = w2l[:, tap:tap + n, ib, ob * P:(ob + 1) * P]
                            h = w2h[:, tap:tap + n, ib, ob * P:(ob + 1) * P]
                        v.tensor_tensor(o, bank[u % 4][:, 0:n, :], h, ALU.subtract).then_inc(s["rest_ready"], 1)

                def row_power(ob):
                    dve.wait_ge(s[f"raw2_in{ob}"], 16)
                    m = small["w2max"][:, ob:ob + 1]
                    link(v.tensor_reduce(m, raw2[ob][:, :, :], AX.XY, ALU.max, apply_absolute_value=True))
                    power_scale(v, link, m, small["w2pow"][:, ob:ob + 1], small["w2scale"][:, ob:ob + 1],
                                small["w2inv"][:, ob:ob + 1], W2_TOP)
                    dve.sem_inc(s["w2_power"], 1)

                g0 = (0, 0)
                dve_layernorm(dve, g0, 0)
                dve_layernorm(dve, g0, 1)
                row_power(0)
                dve.wait_ge(s["vec_in"], 8 * 16)
                vt = vec[:, :, :].rearrange("p (a c) k -> p a c k", a=2)
                link(v.tensor_scalar(veps[:, :, :], vt[:, :, 3, :], EPS, None, ALU.add))
                v.tensor_copy(work[:, :, :], veps[:, :, :]).then_inc(s["veps_ready"], 1)
                dve.wait_ge(s["root_ready"], 1)
                rsqrt_step(v, link, bn[:, :, :], root[:, :, :], veps[:, :, :], work[:, :, :])
                link(v.tensor_tensor(bn[:, :, :], bn[:, :, :], vt[:, :, 0, :], ALU.mult))
                link(v.tensor_tensor(work[:, :, :], vt[:, :, 2, :], bn[:, :, :], ALU.mult))
                link(v.tensor_tensor(veps[:, :, :], vt[:, :, 1, :], work[:, :, :], ALU.subtract))
                link(v.tensor_copy(conv2_bias[:, :], veps[:, 1, :]))
                dve.wait_ge(s["norm_ready"], 1)
                bound, t1 = small["bound"], small["work1"]
                link(v.tensor_tensor(bound[:, :], small["norm"][:, :], small["w1inv"][:, :], ALU.mult))
                link(v.scalar_tensor_tensor(out=t1[:, :], in0=bn[:, 0, :], scalar=-1.0, in1=bn[:, 0, :],
                                            op0=ALU.mult, op1=ALU.max))
                link(v.scalar_tensor_tensor(out=bound[:, :], in0=bound[:, :], scalar=16.25, in1=t1[:, :],
                                            op0=ALU.mult, op1=ALU.mult))
                link(v.scalar_tensor_tensor(out=t1[:, :], in0=veps[:, 0, :], scalar=-1.0, in1=veps[:, 0, :],
                                            op0=ALU.mult, op1=ALU.max))
                link(v.tensor_tensor(bound[:, :], bound[:, :], t1[:, :], ALU.add))
                for ob in range(KD):
                    if ob:
                        dve.wait_ge(s["row_ready"], ob)
                    v.tensor_scalar(diag[:, :], ident[:, :], bound[:, ob:ob + 1], None, ALU.mult)\
                        .then_inc(s["diag_ready"], 1)
                dve.wait_ge(s["row_ready"], KD)
                link(v.tensor_reduce(ymax[:, :], bound_row[:, :, :], AX.XY, ALU.max))
                power_scale(v, link, ymax[:, :], ypow[:, :], yscale[:, :], yinv[:, :], Y_TOP)
                link(v.tensor_scalar(conv1_bias[:, :], veps[:, 0, :], yscale[:, 0:1], None, ALU.mult))
                link(v.tensor_tensor(t1[:, :], bn[:, 0, :], small["w1inv"][:, :], ALU.mult))
                link(v.tensor_scalar(conv1_scale[:, :], t1[:, :], yscale[:, 0:1], float(2.0 ** -H_TOP),
                                     ALU.mult, ALU.mult))

                rests(0, KD)
                dve_split(dve, g0, 0)
                row_power(1)
                rests(cut[0], cut[1])
                dve_layernorm(dve, g0, 2)
                dve_split(dve, g0, 1)
                rests(cut[1], cut[2])
                dve_layernorm(dve, g0, 3)
                dve_split(dve, g0, 2)
                rests(cut[2], cut[3])
                dve_split(dve, g0, 3)
                rests(cut[3], every)
                link(v.tensor_tensor(t1[:, :], bn[:, 1, :], small["w2inv"][:, :], ALU.mult))
                link(v.tensor_scalar(conv2_scale[:, :], t1[:, :], yinv[:, 0:1], None, ALU.mult))

            @block.tensor
            def _(pe):
                def room(u):
                    if u >= 4:
                        pe.wait_ge(s["rest_ready"], u - 3)

                pe.wait_ge(s["id_in"], 16)
                pe.wait_ge(s["ones_ready"], 1)
                pe.wait_ge(s["w1_scaled"], 1)
                for ob in range(KD):
                    for ib in range(KD):
                        last = nc.tensor.transpose(bank[ob][:, ib, :], raw1[:, ob, ib * P:(ib + 1) * P], ident[:, :])
                    last.then_inc(s["turned"], 1)
                for ob in range(KD):
                    pe.wait_ge(s["diag_ready"], ob + 1)
                    nc.tensor.matmul(bound_row[:, ob, :], ones[:, :], diag[:, :], start=True, stop=True)\
                        .then_inc(s["row_ready"], 1)

                def turns(lo, hi):
                    for u in range(lo, hi):
                        ob, ib, tap, sources, summed = chunks[u - KD]
                        pe.wait_ge(s["w2_scaled"], ob + 1)
                        if summed:
                            pe.wait_ge(s[f"sums_ready{ob}"], 1)
                        room(u)
                        for j, views in enumerate(sources):
                            to = bank[u % 4][:, j, :]
                            if len(views) == 1:
                                last = nc.tensor.transpose(to, views[0], ident[:, :])
                            else:
                                for i, view in enumerate(views):
                                    last = nc.tensor.matmul(to, view, ident[:, :], start=(i == 0),
                                                            stop=(i == len(views) - 1))
                        last.then_inc(s["turned"], 1)

                g0 = (0, 0)
                pe_turn(pe, g0, 0)
                for q in range(G):
                    turns(cut[q], cut[q] + 4)
                    if q + 1 < G:
                        pe_turn(pe, g0, q + 1)
                    turns(cut[q] + 4, cut[q + 1])
                    pe_conv1(pe, g0, q)
                turns(beside, every)

        area = lambda name: [sb(f"{name}{i}", [P, 3 * CW // 2 if i < 3 else CW], F16) for i in range(6)]
        ch, cl = area("ch"), area("cl")

        def part(t, p):
            if p < C1[0]:
                return t[p][:, 0:CW].rearrange("p (r w) -> p r w", w=QW)
            c, j = divmod(p - C1[0], 3)
            return t[c][:, j * CW // 2:(j + 1) * CW // 2].rearrange("p (r w) -> p r w", w=EW)

        raw_hh, end = carve(w2_room, 0, (NHH, D))
        raw_m, end = carve(w2_room, end, (KD, D))
        raw_s, end = carve(w2_room, end, (D,))
        g_ones, end = carve(w2_room, end, (P,))
        g_diag, end = carve(w2_room, end, (P,))
        assert end == RAW_WORDS <= TAP0[RAW_AFTER] * KD * D // 2 and words(FIRST) <= TAP0[C2[0]] * KD * D // 2
        ga2, ga3, ha, hb = (sb(n, [P, KD, G, Q]) for n in ("ga2", "ga3", "ha", "hb"))
        sa = ha
        co, _ = carve(shared["co_room"], 0, (KD, G, N))
        kp = [ctx.enter_context(nc.psum_tensor(f"kp{i}", [P, G, Q], F32)) for i in range(3)]
        prod_ready, taken, fin_ready = map(sem, ("prod_ready", "taken", "fin_ready"))
        stored = shared["stored"]
        flat = lambda c: y1[:, c, :, :, :].rearrange("p k g w -> p (k g w)")
        whole, here, shifted = slice(0, CW), slice(0, CW - 1), slice(1, CW)
        rows_of = lambda t: t[:, :].rearrange("p (r w) -> p r w", w=QW)
        even, odd, even_next = slice(0, QW - 2, 2), slice(1, QW - 1, 2), slice(2, QW, 2)
        third = [y1[:, c, :, :, 2:2 + EW - 1].rearrange("p k g w -> p (k g) w") for c in range(4)]
        D_OF = {1: 0, 2: 3, 3: 2, 4: 4, 5: 5, 6: 7, 7: 8, 8: 9, 9: 10, 10: 11, 11: 12, 12: 13, 13: 14, 14: 15}
        SRC = {1: mix, 2: mix, 3: db, 4: mix, 5: mix}
        THIRD = {6: rows_of(db)[:, :, odd], 7: third[0], 8: third[1], 9: rows_of(mix)[:, :, odd], 10: third[2],
                 11: third[3], 12: rows_of(mix)[:, :, odd], 13: third[0], 14: third[1]}
        SHORT = {2, 5}
        span = lambda p: here if p in SHORT else whole
        src_of = lambda p: THIRD[p] if p in THIRD else (flat(3) if p == 0 else SRC[p][:, :])[:, span(p)]
        dst_of = lambda t, p: part(t, p)[:, :, 0:EW - 1] if p in THIRD else t[p][:, 0:CW][:, span(p)]

        gw = shared["gates"]
        raw_ih = gw["raw_ih"]
        vih, vhh = sb("vih", [P, NHH]), sb("vhh", [P, NHH])
        NS = NHH + KD + 1
        wmax, wpow, wscale, winv = (sb(n, [P, NS]) for n in ("wmax", "wpow", "wscale", "winv"))
        kscale = sb("kscale", [P, NHH])
        (small_in, big_in, s_cleared, s_in, v_in, g_step, g_scaled, g_turned, g_high, g_rest, g_diag_ready,
         g_row_ready) = map(sem, ("small_in", "big_in", "s_cleared", "s_in", "v_in", "g_step", "g_scaled",
                                  "g_turned", "g_high", "g_rest", "g_diag_ready", "g_row_ready"))
        chunks = []
        pairwise = [slice(k, D, KD) for k in range(KD)]
        plain = [slice(D + k * P, D + (k + 1) * P) for k in range(KD)]
        for raw, blocks, inputs, high, rest in ((raw_hh, NHH, pairwise, gw["whh"], gw["whl"]),
                                                (raw_m, KD, pairwise, gw["wmh"], gw["wml"]),
                                                (raw_ih, NHH, pairwise + plain, gw["wih"], gw["wil"])):
            for o in range(blocks):
                cols = slice(o * P, (o + 1) * P)
                chunks.append(([raw[:, o, i] for i in inputs], high[:, :, cols], rest[:, :, cols]))
        chunks.append(([raw_s[:, i] for i in pairwise], gw["wsh"][:, :, :], gw["wsl"][:, :, :]))
        cut = [0, 4, 8, 12, len(chunks)]
        c1_rows = [b[:, :, :].rearrange("p r c -> p (r c)").rearrange("p (k c) -> p k c", c=P) for b in c1p]
        g_bank = [turn[0][:, :, :], turn[1][:, :, :]] + c1_rows
        inv_row = g_bank[3]
        GATE_STEPS = 11

        block = ctx.enter_context(nc.Block())

        @block.sync
        def _(sp):
            def gate_loads():
                pairs = lambda w: w.rearrange("(g p f) i -> p g (f i)", p=P, f=KD)
                sp.wait_ge(prod_ready, EV * (NGROUP - 1) + BANK0[RAW_AFTER])
                sp.dma_start(raw_hh[:, :, :].rearrange("p (g f) i -> p g (f i)", f=KD), pairs(io["w_hh"])).then_inc(small_in, 16)
                sp.dma_start(raw_m[:, :, :], io["w_msg"].rearrange("(o p) i -> p o i", p=P)).then_inc(small_in, 16)
                sp.dma_start(gw["rows"][:, :], io["rows"]).then_inc(small_in, 16)
                sp.wait_ge(s_cleared, 2)
                for r in S_ROWS:
                    sp.dma_start(raw_s[r:r + 3, :], io["w_se"]).then_inc(s_in, 16)
                sp.wait_ge(cl_ready, NPROD * NGROUP)
                sp.wait_ge(h_stored, 16 * B)
                sp.dma_start(raw_ih[:, :, :].rearrange("p (g f) i -> p g (f i)", f=KD), pairs(io["w_ih"])).then_inc(big_in, 16)
                sp.wait_ge(prod_ready, EV * (NGROUP - 1) + BANK0[C2[0]])
                sp.dma_start(shared["first"]["h_next"][:, :, :], paired(h_scratch, 0)).then_inc(shared["h_in"], 16)
                load_adjacency(sp, io, 0, shared["first"]["adj0"], shared["adj_in0"])

            def loads(n):
                for q in range(G):
                    sp_load(sp, n, q)
            loads((0, 1))
            with sp.Fori(1, NGROUP - 1) as g:
                loads((g, 1))
            gate_loads()

        @block.gpsimd
        def _(pool):
            def rest(n, p):
                pool.wait_ge(ch_ready, count(n, NPROD, p + 1))
                nc.gpsimd.tensor_tensor(dst_of(cl, p), src_of(p), dst_of(ch, p), ALU.subtract)\
                    .then_inc(cl_ready, 1)

            def group(n):
                for p in range(NPROD):
                    rest(n, p)
            group((0, 0))
            group((0, 1))
            with pool.Fori(1, NGROUP - 1) as g:
                group((g, 1))
            with nc.allow_non_contiguous_dma(reason="small vectors"):
                for vector, name in ((vih, "b_ih"), (vhh, "b_hh")):
                    pool.dma_start(vector[:, :].rearrange("p (g f) -> p g f", f=KD),
                                   io[name].rearrange("(g p f) -> p g f", p=P, f=KD)).then_inc(v_in, 16)
                for c in range(2):
                    pool.dma_start(gw["msg_bias"][:, c, :], io["b_msg"].partition_broadcast(P)).then_inc(v_in, 16)
                pool.wait_ge(s_cleared, 2)
                for r in S_ROWS:
                    pool.dma_start(gw["s_bias"][r:r + 3, :], io["b_se"].rearrange("(p a) -> p a", a=1)).then_inc(v_in, 16)

        @block.scalar
        def _(act):
            def high(n, p):
                if p < 3:
                    wait(act, prod_ready, count(n, EV, -EV + BANK0[C1[0] + 3 * p + 3]))
                elif p < C1[0]:
                    wait(act, prod_ready, count(n, EV, -EV + BANK0[p + 1]))
                else:
                    act.wait_ge(prod_ready, count(n, EV, BANK0[(p - C1[0]) // 3 + 1]))
                if p == 0:
                    act.wait_ge(y1_ready, count(n, KD * G, KD * G))
                else:
                    act.wait_ge(diff_ready, count(n, SUMS, D_OF[p] + 1))
                nc.scalar.activation(dst_of(ch, p), src_of(p), ACT.Copy).then_inc(ch_ready, 1)

            def finish(g):
                act.wait_ge(taken, count(g, EV, EV))
                for ob in range(KD):
                    nc.scalar.activation(co[:, ob, :, :], co[:, ob, :, :], ACT.Identity,
                                         bias=conv2_bias[:, ob:ob + 1], scale=conv2_scale[:, ob:ob + 1])\
                        .then_inc(fin_ready, 1)
                base, off = g
                for ob in range(KD):
                    act.wait_ge(fin_ready, count(g, KD, ob + 1))
                    act.dma_start(by_group[base + off, ob, :, :, :], co[:, ob, :, :]).then_inc(stored[ob], 16)

            def highs(n, products):
                for p in products:
                    high(n, p)

            def gate_highs(lo, hi):
                for u in range(lo, hi):
                    sources, high_part, _ = chunks[u]
                    act.wait_ge(g_turned, u + 1)
                    nc.scalar.activation(high_part, g_bank[u % 4][:, 0:len(sources), :], ACT.Copy).then_inc(g_high, 1)

            highs((0, 0), range(C1[0]))

            def both(g, n):
                highs(g, C1)
                act_layernorm(act, n, 0)
                act_layernorm(act, n, 1)
                highs(g, C2)
                act_h_out(act, n, 0)
                highs(g, C3)
                act_y_out(act, n, 0)
                act_h_out(act, n, 1)
                act_layernorm(act, n, 2)
                act_y_out(act, n, 1)
                act_h_out(act, n, 2)
                act_layernorm(act, n, 3)
                act_y_out(act, n, 2)
                act_h_out(act, n, 3)
                act_y_out(act, n, 3)
                highs(n, range(3))
                finish(g)
                highs(n, range(3, C1[0]))
            both((0, 0), (0, 1))
            with act.Fori(1, NGROUP - 1) as g:
                both((g, 0), (g, 1))
            highs((0, NGROUP - 1), range(C1[0], NPROD))
            for part in range(len(cut) - 1):
                gate_highs(cut[part], cut[part + 1])
            first = shared["first"]
            act.wait_ge(shared["h_in"], 16)
            nc.scalar.activation(first["hh20"][:, :, :], first["h_next"][:, :, :], ACT.Copy).then_inc(shared["hh_ready"], 1)
            nc.scalar.activation(first["hs0"][:, :, :], first["h_next"][:, :, :], ACT.Copy).then_inc(shared["hs_ready"], 1)
            finish((0, NGROUP - 1))
            act.wait_ge(h_stored, 16 * B)

        @block.vector
        def _(dve):
            v = nc.vector
            def take(g, m):
                dve.wait_ge(prod_ready, count(g, EV, m + 1))
                if m >= BANK0[C1[0]]:
                    take_third(g, m)
                    return
                p, ob = divmod(m, KD)
                wait(dve, taken, count(g, EV, m - 1))
                if p == 4:
                    wait(dve, stored[ob], count(g, 16))
                bank = kp[m % 3][:, :, :]
                o4 = co[:, ob, :, :].rearrange("p g (r c) -> p c g r", c=4)
                if p == 0:
                    last = v.tensor_copy(sa[:, ob, :, :], bank)
                elif p == 1:
                    last = v.tensor_tensor(ga2[:, ob, :, :], bank, sa[:, ob, :, :], ALU.add)
                elif p == 2:
                    last = v.tensor_tensor(ga3[:, ob, :, :], bank, sa[:, ob, :, :], ALU.add)
                elif p == 3:
                    v.tensor_tensor(ha[:, ob, :, :], bank, ga2[:, ob, :, :], ALU.add)
                    last = v.tensor_tensor(hb[:, ob, :, :], bank, ga3[:, ob, :, :], ALU.add)
                else:
                    phase, addend = {4: (0, ha), 5: (2, hb)}[p]
                    last = v.tensor_tensor(o4[:, phase, :, :], bank, addend[:, ob, :, :], ALU.add)
                last.then_inc(taken, 1)

            def take_third(g, m):
                c, j = divmod(m - BANK0[C1[0]], 3)
                bank = kp[m % 3][:, :, :].rearrange("p g q -> p (g q)").rearrange("p (k g r) -> p k g r", k=KD, g=G)
                dve.wait_ge(taken, count(g, EV, m))
                halves = [lambda t, i=i: t[:, :, :, i::2] for i in range(2)]
                phase = lambda i: co[:, :, :, (1, 3)[c - 1] + 4 * i::8]
                for i in (range(2) if j == 0 else [j - 1]):
                    if c == 0:
                        for out, first in ((ha, ga2), (hb, ga3)):
                            to = halves[i](out)
                            last = v.tensor_tensor(to, bank, halves[i](first) if j == 0 else to, ALU.add)
                    else:
                        first = halves[i](ha if c == 1 else hb)
                        last = v.tensor_tensor(phase(i), bank, first if j == 0 else phase(i), ALU.add)
                last.then_inc(taken, 1)

            def difference(n, d):
                q0, q1, q2, q3 = (flat(c) for c in range(4))
                a, b = da[:, :], db[:, :]
                if d == 0:
                    dve.wait_ge(y1_ready, count(n, KD * G, KD * G))
                else:
                    dve.wait_ge(diff_ready, count(n, SUMS, d))
                free = {0: 12 - NPROD, 2: 6 - NPROD, 3: 1, 4: 2, 5: 4, 7: 3, 10: 5, 12: 0, 13: 9, 14: 7, 15: 8}
                if d in free:
                    wait(dve, cl_ready, count(n, NPROD, free[d] + 1))
                w, h, f = whole, here, shifted
                rm, rb = rows_of(mix), rows_of(db)
                out, x, y = [
                    (mix[:, w], q1[:, w], q3[:, w]),
                    (da[:, w], q0[:, w], q1[:, w]),
                    (db[:, w], q2[:, w], q3[:, w]),
                    (mix[:, h], q1[:, f], q3[:, h]),
                    (mix[:, w], a[:, w], b[:, w]),
                    (mix[:, h], a[:, f], b[:, h]),
                    (da[:, w], q2[:, w], q1[:, w]),
                    (db[:, h], q0[:, f], q3[:, h]),
                    (third[0], rb[:, :, even], rb[:, :, odd]),
                    (third[1], rb[:, :, even_next], rb[:, :, odd]),
                    (mix[:, h], a[:, h], b[:, h]),
                    (third[2], rm[:, :, even], rm[:, :, odd]),
                    (third[3], rm[:, :, even_next], rm[:, :, odd]),
                    (mix[:, h], a[:, f], b[:, h]),
                    (third[0], rm[:, :, even], rm[:, :, odd]),
                    (third[1], rm[:, :, even_next], rm[:, :, odd]),
                ][d]
                v.tensor_tensor(out, x, y, ALU.subtract).then_inc(diff_ready, 1)

            steps = [0]

            def link(ins):
                steps[0] += 1
                ins.then_inc(g_step, 1)
                dve.wait_ge(g_step, steps[0])

            def gate_clear():
                v.memset(raw_s[:, :], 0.0).then_inc(s_cleared, 1)
                v.memset(gw["s_bias"][:, :], 0.0).then_inc(s_cleared, 1)
                link(v.memset(g_ones[:, :], 1.0))

            def gate_scales():
                dve.wait_ge(small_in, 3 * 16)
                dve.wait_ge(s_in, 16 * len(S_ROWS))
                v.tensor_reduce(wmax[:, 0:NHH], raw_hh[:, :, :], AX.X, ALU.max, apply_absolute_value=True)
                v.tensor_reduce(wmax[:, NHH:NHH + KD], raw_m[:, :, :], AX.X, ALU.max, apply_absolute_value=True)
                link(v.tensor_reduce(wmax[:, NS - 1:NS], raw_s[:, :], AX.X, ALU.max, apply_absolute_value=True))
                power_scale(v, link, wmax[:, :], wpow[:, :], wscale[:, :], winv[:, :], W_TOP)
                v.tensor_scalar(kscale[:, :], wscale[:, 0:NHH], H_SCALE, None, ALU.mult)
                link(v.tensor_scalar(winv[:, :], winv[:, :], 1.0 / H_SCALE, None, ALU.mult))
                v.tensor_copy(gw["gate_inv"][:, :], winv[:, 0:NHH])
                v.tensor_scalar(gw["gate_half"][:, :], winv[:, 0:NHH], 0.5, None, ALU.mult)
                link(v.tensor_copy(gw["s_inv"][:, :], winv[:, NS - 1:NS]))

            def gate_scaled():
                for o in range(NHH):
                    v.tensor_scalar(raw_hh[:, o, :], raw_hh[:, o, :], wscale[:, o:o + 1], None, ALU.mult)
                for o in range(KD):
                    v.tensor_scalar(raw_m[:, o, :], raw_m[:, o, :], wscale[:, NHH + o:NHH + o + 1], None, ALU.mult)
                v.tensor_scalar(raw_s[:, :], raw_s[:, :], wscale[:, NS - 1:NS], None, ALU.mult).then_inc(g_scaled, 1)
                dve.wait_ge(big_in, 16)
                for o in range(NHH):
                    last = v.tensor_scalar(raw_ih[:, o, :], raw_ih[:, o, :], kscale[:, o:o + 1], None, ALU.mult)
                last.then_inc(g_scaled, 1)

            def gate_biases():
                gate_bias, hn_bias = gw["gate_bias"], gw["hn_bias"]
                dve.wait_ge(v_in, 16 * (4 + len(S_ROWS)))
                link(v.tensor_tensor(gate_bias[:, 0:4], vih[:, 0:4], vhh[:, 0:4], ALU.add))
                v.tensor_scalar(gate_bias[:, 0:4], gate_bias[:, 0:4], 0.5, None, ALU.mult)
                v.tensor_copy(gate_bias[:, 4:6], vih[:, 4:6])
                v.tensor_scalar(hn_bias[:, :], vhh[:, 4:6], 0.5, None, ALU.mult)
                for o in range(KD):
                    if o:
                        dve.wait_ge(g_row_ready, o)
                    v.tensor_scalar(g_diag[:, :], ident[:, :], winv[:, NHH + o:NHH + o + 1], None, ALU.mult)\
                        .then_inc(g_diag_ready, 1)
                dve.wait_ge(g_row_ready, KD)
                for c in range(2):
                    last = v.tensor_copy(gw["msg_inv"][:, c, :], inv_row[:, 0:KD, :].rearrange("p k o -> p (k o)"))
                link(last)

            def gate_rests(lo, hi):
                for u in range(lo, hi):
                    sources, high_part, rest_part = chunks[u]
                    if high_part.dtype == F32R:
                        high_part = high_part.bitcast(F32)
                    dve.wait_ge(g_high, u + 1)
                    v.tensor_tensor(rest_part, g_bank[u % 4][:, 0:len(sources), :], high_part, ALU.subtract)\
                        .then_inc(g_rest, 1)

            def both(g, n):
                def banks(*products):
                    for p in products:
                        for m in range(BANK0[p], BANK0[p + 1]):
                            take(g, m)

                def differences(n, lo, hi):
                    for d in range(lo, hi):
                        difference(n, d)

                take(g, 0)
                differences(g, 5, 8)
                take(g, 1)
                differences(g, 8, 13)
                if n is None:
                    banks(1, 2)
                    differences(g, 13, SUMS)
                    gate_clear()
                    gate_scales()
                    banks(3)
                    gate_scaled()
                    banks(4)
                    gate_biases()
                    for part, products in enumerate(([5], C1, C2, C3)):
                        gate_rests(cut[part], cut[part + 1])
                        if part == 3:
                            first = shared["first"]
                            dve.wait_ge(shared["hh_ready"], 1)
                            v.tensor_tensor(first["hl20"][:, :, :], first["h_next"][:, :, :], first["hh20"][:, :, :],
                                            ALU.subtract).then_inc(shared["hl_ready"], 1)
                        banks(*products)
                    return
                dve_layernorm(dve, n, 0)
                dve_layernorm(dve, n, 1)
                banks(1)
                banks(2)
                dve_split(dve, n, 0)
                differences(g, 13, SUMS)
                banks(3)
                dve_layernorm(dve, n, 2)
                dve_split(dve, n, 1)
                banks(4)
                dve_layernorm(dve, n, 3)
                dve_split(dve, n, 2)
                banks(5)
                dve_split(dve, n, 3)
                banks(*C1)
                differences(n, 0, 3)
                banks(*C2)
                differences(n, 3, 4)
                banks(*C3)
                differences(n, 4, 5)

            for d in range(5):
                difference((0, 0), d)
            both((0, 0), (0, 1))
            with dve.Fori(1, NGROUP - 1) as g:
                both((g, 0), (g, 1))
            both((0, NGROUP - 1), None)

        @block.tensor
        def _(pe):
            def product(g, p):
                pe.wait_ge(cl_ready, count(g, NPROD, p + 1))
                width, out_blocks = (Q, 1) if p < C1[0] else (E, KD)
                views = [part(t, p).rearrange("p (k g) w -> p k g w", g=G) for t in (ch, cl)]
                for ob in range(KD):
                    m = BANK0[p] + ob // out_blocks
                    if ob % out_blocks == 0:
                        wait(pe, taken, count(g, EV, m - 2))
                    bank = kp[m % 3][:, :, :]
                    if out_blocks > 1:
                        bank = bank.rearrange("p g q -> p (g q)").rearrange("p (k g r) -> p k g r", k=KD, g=G)[:, ob, :, :]
                    steps = [(w, c, t, k) for t in range(PTAPS[p]) for k in range(KD)
                             for w, c in ((w2h, views[0]), (w2h, views[1]), (w2l, views[0]))]
                    for i, (w, c, t, k) in enumerate(steps):
                        last = nc.tensor.matmul(bank, w[:, TAP0[p] + t, k, ob * P:(ob + 1) * P],
                                                c[:, k, :, t:t + width], start=(i == 0), stop=(i == len(steps) - 1))
                    if ob % out_blocks == out_blocks - 1:
                        last.then_inc(prod_ready, 1)

            def gate_rows():
                pe.wait_ge(y1_ready, KD * G * NGROUP)
                for o in range(KD):
                    pe.wait_ge(g_diag_ready, o + 1)
                    nc.tensor.matmul(inv_row[:, o, :], g_ones[:, :], g_diag[:, :], start=True, stop=True)\
                        .then_inc(g_row_ready, 1)

            def gate_turns(lo, hi):
                if lo == 0:
                    pe.wait_ge(g_scaled, 2)
                    pe.wait_ge(h32_ready, KD * G * NGROUP)
                for u in range(lo, hi):
                    if u == 3:
                        pe.wait_ge(g_step, GATE_STEPS)
                    if u >= 4:
                        pe.wait_ge(g_rest, u - 3)
                    for j, source in enumerate(chunks[u][0]):
                        last = nc.tensor.transpose(g_bank[u % 4][:, j, :], source, ident[:, :])
                    last.then_inc(g_turned, 1)

            def both(g, n):
                def products(*which):
                    for p in which:
                        product(g, p)
                if n is None:
                    products(0, 1, 2, 3, 4)
                    gate_rows()
                    for part, which in enumerate(([5], C1, C2, C3)):
                        gate_turns(cut[part], cut[part + 1])
                        products(*which)
                    return
                products(0, 1, 2)
                pe_turn(pe, n, 0)
                for q, which in enumerate(([3], [4], [5], C1)):
                    products(*which)
                    pe_conv1(pe, n, q)
                    if q + 1 < G:
                        pe_turn(pe, n, q + 1)
                products(*C2)
                products(*C3)

            both((0, 0), (0, 1))
            with pe.Fori(1, NGROUP - 1) as g:
                both((g, 0), (g, 1))
            both((0, NGROUP - 1), None)


def gate_constants(nc, ctx):
    sb = lambda name, shape, dt=F32: ctx.enter_context(nc.sbuf_tensor(name, shape, dt))
    g = allocate(nc, ctx, GATE_WEIGHTS)
    sb("room_left", [P, ROOM_LEFT])
    g.update({
        "gate_inv": sb("gate_inv", [P, NHH]),
        "gate_half": sb("gate_half", [P, NHH]),
        "gate_bias": sb("gate_bias", [P, NHH]),
        "hn_bias": sb("hn_bias", [P, KD]),
        "s_inv": sb("s_inv", [P, 1]),
        "s_bias": sb("s_bias", [P, 1]),
        "msg_inv": sb("msg_inv", [P, 2, D]),
        "msg_bias": sb("msg_bias", [P, 2, D]),
        "rows": sb("rows", [P, 6]),
    })
    return g


def gate_phase(nc, io, scratch, shared, out):
    ident, h_scratch = shared["ident"], shared["h_scratch"]
    ctx = ExitStack()
    with ctx:
        sb = lambda name, shape, dt=F32: ctx.enter_context(nc.sbuf_tensor(name, shape, dt))
        sem = lambda name: ctx.enter_context(nc.semaphore(name))
        mask_t = sb("mask_t", [P, NB, N])
        zg1 = sb("zg1", [P, RAW_WORDS - NB * N])
        first = shared["first"]
        sb("first_place", [P, words(FIRST) - RAW_WORDS])
        h_next = first["h_next"]
        g = shared["gates"]
        whh, whl, wih, wil, wmh, wml, wsh, wsl, gate_inv, gate_half, gate_bias, hn_bias, s_inv, s_bias, msg_inv, \
            msg_bias, rows = (g[n] for n in "whh whl wih wil wmh wml wsh wsl gate_inv gate_half gate_bias hn_bias "
                              "s_inv s_bias msg_inv msg_bias rows".split())
        two = range(2)
        adj_t = [first["adj0"], sb("adj_t1", [P, N // SQ, SQ, NB])]
        xc_t = [sb(f"xc_t{i}", [P, KD, N]) for i in two]
        out_t = [sb(f"out_t{i}", [P, N // SQ, CHUNK]) for i in two]
        turned = [sb(f"turned{i}", [P, N]) for i in two]
        hs = [first["hs0"], sb("hs1", [P, KD, N])]
        hh = [first["hh20"], sb("hh21", [P, KD, N], F16)]
        hl = [first["hl20"], sb("hl21", [P, KD, N], F16)]
        sf, lin_right, lin_left = sb("sf", [P, N]), sb("lin_right", [P, N]), sb("lin_left", [P, N])
        shi = sb("shi", [P, N], F32R)
        s_right, s_left = sb("s_right", [P, N], F32R), sb("s_left", [P, N], F32R)
        mg = [sb(f"mg{i}", [P, 2, D]) for i in two]
        mh = sb("mh", [P, NB, D], F32R)
        ml = sb("ml", [P, NB, D], F32R)
        ex = [sb(f"ex{i}", [P, N]) for i in two]
        ah = [sb(f"ah{i}", [P, N], F32R) for i in two]
        al = [sb(f"al{i}", [P, N], F32R) for i in two]
        ch = [sb(f"ch2{i}", [P, KD, N], F32R) for i in two]
        cl = [sb(f"cl2{i}", [P, KD, N], F32R) for i in two]
        nh = sb("nh", [P, KD, N], F32R)
        nl = sb("nl", [P, KD, N], F32R)
        rg, zg, gh, nn = (sb(n, [P, N]) for n in ("rg", "zg", "gh", "nn"))
        zg = [zg, zg1]
        oo = [sb(f"oo{i}", [P, N]) for i in two]
        pg = [ctx.enter_context(nc.psum_tensor(f"pg{i}", [P, N], F32)) for i in range(3)]
        px = [ctx.enter_context(nc.psum_tensor(f"px{i}", [P, N], F32)) for i in range(KD)]
        pu = [ctx.enter_context(nc.psum_tensor(f"pu{i}", [P, N], F32)) for i in range(3)]
        x_in, xc_in, out_st = ([sem(f"{n}{i}") for i in two] for n in ("xt_in", "xc_in", "out_st"))
        adj_in = [shared["adj_in0"], sem("adj_in1")]
        moving = sem("moving")
        h_in, hs_ready, hh_ready, hl_ready, stored = (shared[n] for n in "h_in hs_ready hh_ready hl_ready stored".split())
        (s_ready, sf_ready, shi_ready, sr_lin, s_right_ready, sl_lin, s_left_ready) = map(sem, (
            "s_ready", "sf_ready", "shi_ready", "sr_lin", "s_right_ready", "sl_lin", "s_left_ready"))
        (m_ready, m_scaled, m_biased, mh_ready, ml_ready) = map(sem, (
            "m_ready", "m_scaled", "m_biased", "mh_ready", "ml_ready"))
        (dist_ready, ex_ready, mask_ready, a_ready, ah_ready, al_ready, x_step) = map(sem, (
            "dist_ready", "ex_ready", "mask_ready", "a_ready", "ah_ready", "al_ready", "x_step"))
        (nmp_h, nmp_l, ct_ready, ch_ready, cl_ready) = map(sem, ("nmp_h", "nmp_l", "ct_ready", "ch2_ready", "cl2_ready"))
        (gate_ready, act_gate, u_ready, v_ready, n_ready, d_ready, w_ready, o_ready, ot_ready, out_ready) = map(sem, (
            "gate_ready", "act_gate", "u_ready", "v_ready", "n_ready", "d_ready", "w_ready", "o_ready",
            "ot_ready", "out_ready"))
        R0, HN0, Z0, IN0, R1, HN1, Z1, IN1 = range(8)
        BANK = {R0: 0, HN0: 1, Z0: 2, IN0: 0, R1: 1, HN1: 2, Z1: 0, IN1: 1}
        block = ctx.enter_context(nc.Block())
        nxt = lambda b, k=1: (b[0], b[1] + k)
        par = lambda b: b[1] % 2

        def index(b):
            return b[0] + b[1]

        def index_known(b):
            return b[0] + b[1] if isinstance(b[0], int) else None

        PREV = {R0: (Z1, -1), HN0: (IN1, -1), Z0: (HN1, -1), IN0: (R0, 0), R1: (HN0, 0), HN1: (Z0, 0),
                Z1: (IN0, 0), IN1: (R1, 0)}
        ACT_ORDER = {R0: 1, HN0: 2, Z0: 3, R1: 4, HN1: 5, Z1: 6}

        def bank_free(eng, b, k):
            prev, back = PREV[k]
            if prev in ACT_ORDER:
                wait(eng, act_gate, count(nxt(b, back), 6, ACT_ORDER[prev]))
            else:
                wait(eng, v_ready, count(nxt(b, back), 2, 1 if prev == IN0 else 2))

        def run(eng, both):
            both(None, None, (0, 0))
            both(None, (0, 0), (0, 1))
            both((0, 0), (0, 1), (0, 2))
            with eng.Fori(1, B // 2 - 1) as pair:
                b = pair * 2
                both((b, -1), (b, 0), (b, 1))
                both((b, 0), (b, 1), (b, 2))
            both((0, B - 3), (0, B - 2), (0, B - 1))
            both((0, B - 2), (0, B - 1), None)
            both((0, B - 1), None, None)

        def arrived(eng, sems, b, parts=1):
            base, off = b
            if isinstance(base, int):
                eng.wait_ge(sems[par(b)], 16 * parts * ((base + off) // 2 + 1))
            else:
                eng.wait_ge(sems[par(b)], base * (8 * parts) + 16 * parts * (off // 2 + 1))

        @block.sync
        def _(sp):
            groups = [(slice(a * SQ, (a + 1) * SQ), slice(a * CHUNK, (a + 1) * CHUNK)) for a in range(NB)]

            def loads(b):
                i, k = par(b), index(b)
                if index_known(b) != 0:
                    wait(sp, hl_ready, count(b, 1))
                    sp.sem_inc(moving, 1)
                    wait(sp, hs_ready, count(b, 1))
                    sp.sem_inc(moving, 1)
                    sp.dma_start(h_next[:, :, :], paired(h_scratch, k)).then_inc(h_in, 16)
                if index_known(b) != 0:
                    wait(sp, mask_ready, count(nxt(b, -1), NB))
                    sp.sem_inc(moving, 1)
                    load_adjacency(sp, io, k, adj_t[i], adj_in[i])
                wait(sp, cl_ready, count(nxt(b, -1), 1))
                sp.sem_inc(moving, 1)
                if index_known(b) == 0:
                    for ob in range(KD):
                        sp.wait_ge(stored[ob], 16 * NGROUP)
                sp.dma_start(xc_t[i][:, :, :], paired(scratch, k)).then_inc(xc_in[i], 16)

            def residual(b):
                if index_known(b) is None or index_known(b) >= 2:
                    arrived(sp, out_st, nxt(b, -2), NB)
                    sp.sem_inc(moving, 1)
                for parts, features in groups:
                    sp.dma_start(out_t[par(b)][parts, :, :],
                                 io["x"][index(b), :, features].rearrange("(b c) w -> c b w", c=SQ))\
                        .then_inc(x_in[par(b)], 16)

            def store(p):
                sp.wait_ge(out_ready, count(p, 2, 2))
                sp.sem_inc(moving, 1)
                for parts, features in groups:
                    sp.dma_start(out[index(p), :, features].rearrange("(b c) w -> c b w", c=SQ),
                                 out_t[par(p)][parts, :, :]).then_inc(out_st[par(p)], 16)

            def both(p, b, n):
                if p is not None:
                    store(p)
                if n is not None:
                    if index_known(n) != 0:
                        residual(n)
                    if index_known(n) != B - 1:
                        loads(nxt(n))

            residual((0, 0))
            loads((0, 0))
            run(sp, both)
            for i in two:
                sp.wait_ge(out_st[i], 16 * NB * (B // 2))

        @block.gpsimd
        def _(pool):
            def masked_rest(n, m):
                pool.wait_ge(ah_ready, count(n, NB, m + 1))
                nc.gpsimd.tensor_tensor(al[m % 2][:, :], ex[m % 2][:, :], ah[m % 2][:, :].bitcast(F32), ALU.subtract)\
                    .then_inc(al_ready, 1)

            def out_add(b, f):
                t = out_t[par(b)][:, :, f::KD]
                arrived(pool, x_in, b, NB)
                pool.wait_ge(ot_ready, count(b, 2, f + 1))
                nc.gpsimd.tensor_tensor(t, turned[f][:, :].rearrange("p (b r) -> p b r", r=SQ), t, ALU.add)\
                    .then_inc(out_ready, 1)

            def both(p, b, n):
                if p is not None:
                    out_add(p, 1)
                if n is not None:
                    masked_rest(n, 0)
                    masked_rest(n, 1)
                if b is not None:
                    out_add(b, 0)
                if n is not None:
                    masked_rest(n, 2)
                    masked_rest(n, 3)

            run(pool, both)

        @block.scalar
        def _(act):
            A = nc.scalar.activation

            def tanh_n(b, f):
                act.wait_ge(v_ready, count(b, 2, f + 1))
                A(nn[:, :], nn[:, :], ACT.Tanh, bias=gate_bias[:, 4 + f:5 + f]).then_inc(n_ready, 1)

            def h_high(n):
                if index_known(n) == 0:
                    return
                act.wait_ge(h_in, count(n, 16, 16))
                wait(act, gate_ready, count(nxt(n, -1), 8))
                A(hh[par(n)][:, :, :], h_next[:, :, :], ACT.Copy).then_inc(hh_ready, 1)

            def h_keep(n):
                if index_known(n) == 0:
                    return
                wait(act, d_ready, count(nxt(n, -1), 2))
                A(hs[par(n)][:, :, :], h_next[:, :, :], ACT.Copy).then_inc(hs_ready, 1)

            def gate(b, k):
                f = 1 if k in (R1, HN1, Z1) else 0
                act.wait_ge(gate_ready, count(b, 8, k + 1))
                if k in (R0, R1):
                    wait(act, u_ready, count(b, 2, f))
                    A(rg[:, :], pg[BANK[k]][:, :], ACT.Tanh, bias=gate_bias[:, f:f + 1],
                      scale=gate_half[:, f:f + 1]).then_inc(act_gate, 1)
                elif k in (Z0, Z1):
                    wait(act, w_ready, count(nxt(b, -1), 2, f + 1))
                    A(zg[f][:, :], pg[BANK[k]][:, :], ACT.Tanh, bias=gate_bias[:, 2 + f:3 + f],
                      scale=gate_half[:, 2 + f:3 + f]).then_inc(act_gate, 1)
                else:
                    wait(act, v_ready, count(b, 2, f))
                    A(gh[:, :], pg[BANK[k]][:, :], ACT.Identity, bias=hn_bias[:, f:f + 1],
                      scale=gate_half[:, 4 + f:5 + f]).then_inc(act_gate, 1)

            def s_out(n):
                act.wait_ge(s_ready, count(n, 1, 1))
                wait(act, s_left_ready, count(n, 1))
                A(sf[0:64, :], pu[0][0:64, :], ACT.Identity, bias=s_bias[0:64, :], scale=s_inv[0:64, :])
                A(sf[64:128, :], pu[0][64:128, :], ACT.Square, bias=s_bias[64:128, :], scale=s_inv[64:128, :])\
                    .then_inc(sf_ready, 1)
                act.wait_ge(sf_ready, count(n, 1, 1))
                A(lin_right[:, :], sf[:, :], ACT.Identity, bias=rows[:, 2:3], scale=rows[:, 1:2]).then_inc(sr_lin, 1)
                A(lin_left[:, :], sf[:, :], ACT.Identity, bias=rows[:, 5:6], scale=rows[:, 4:5]).then_inc(sl_lin, 1)

            def messages(n):
                for m in range(2):
                    act.wait_ge(m_biased, count(n, 2, m + 1))
                    if m == 0:
                        wait(act, x_step, count(n, NB))
                    A(mh[:, 2 * m:2 * m + 2, :], mg[m][:, :, :], ACT.Relu).then_inc(mh_ready, 1)

            def exps(n, m):
                act.wait_ge(dist_ready, count(n, NB, m + 1))
                wait(act, al_ready, count(n, NB, m - 1))
                A(ex[m % 2][:, :], pu[m % 2][:, :], ACT.Exp).then_inc(ex_ready, 1)

            def mask_high(n, m):
                act.wait_ge(a_ready, count(n, NB, m + 1))
                wait(act, x_step, count(n, NB, m - 1))
                A(ah[m % 2][:, :], ex[m % 2][:, :], ACT.Copy).then_inc(ah_ready, 1)

            def conv_high(n):
                act.wait_ge(ct_ready, count(n, 1, 1))
                wait(act, gate_ready, count(nxt(n, -1), 8))
                A(ch[par(n)][:, :, :], xc_t[par(n)][:, :, :], ACT.Relu).then_inc(ch_ready, 1)

            def message_high(b):
                for c in range(KD):
                    act.wait_ge(x_step, count(b, NB, NB))
                    if c == 0:
                        wait(act, gate_ready, count(b, 8))
                    A(nh[:, c, :], px[c][:, :], ACT.Copy).then_inc(nmp_h, 1)

            def both(p, b, n):
                if b is not None:
                    message_high(b)
                if p is not None:
                    tanh_n(p, 1)
                if n is not None:
                    h_high(n)
                if b is not None:
                    gate(b, R0)
                if n is not None:
                    h_keep(n)
                if b is not None:
                    gate(b, HN0)
                    gate(b, Z0)
                if n is not None:
                    s_out(n)
                    messages(n)
                    exps(n, 0)
                if b is not None:
                    tanh_n(b, 0)
                if n is not None:
                    mask_high(n, 0)
                if b is not None:
                    gate(b, R1)
                if n is not None:
                    exps(n, 1)
                    mask_high(n, 1)
                if b is not None:
                    gate(b, HN1)
                if n is not None:
                    exps(n, 2)
                    mask_high(n, 2)
                if b is not None:
                    gate(b, Z1)
                if n is not None:
                    exps(n, 3)
                    mask_high(n, 3)
                    conv_high(n)

            run(act, both)

        @block.vector
        def _(dve):
            v = nc.vector

            def message_split(b):
                for c in range(KD):
                    dve.wait_ge(nmp_h, count(b, KD, c + 1))
                    v.tensor_tensor(nl[:, c, :], px[c][:, :], nh[:, c, :].bitcast(F32), ALU.subtract).then_inc(nmp_l, 1)

            def gate_mul(b, f):
                dve.wait_ge(act_gate, count(b, 6, 2 + 3 * f))
                v.scalar_tensor_tensor(out=gh[:, :], in0=rg[:, :], scalar=1.0, in1=gh[:, :],
                                       op0=ALU.add, op1=ALU.mult).then_inc(u_ready, 1)

            def gate_add(b, f):
                dve.wait_ge(gate_ready, count(b, 8, IN0 + 1 + 4 * f))
                dve.wait_ge(u_ready, count(b, 2, f + 1))
                v.scalar_tensor_tensor(out=nn[:, :], in0=pg[BANK[IN1 if f else IN0]][:, :],
                                       scalar=gate_inv[:, 4 + f:5 + f], in1=gh[:, :],
                                       op0=ALU.mult, op1=ALU.add).then_inc(v_ready, 1)

            def gate_end(b, f):
                o = oo[f][:, :]
                dve.wait_ge(n_ready, count(b, 2, f + 1))
                wait(dve, ot_ready, count(nxt(b, -1), 2, f + 1))
                v.scalar_tensor_tensor(out=o, in0=hs[par(b)][:, f, :], scalar=1.0 / H_SCALE, in1=nn[:, :],
                                       op0=ALU.mult, op1=ALU.subtract).then_inc(d_ready, 1)
                dve.wait_ge(act_gate, count(b, 6, 3 + 3 * f))
                dve.wait_ge(d_ready, count(b, 2, f + 1))
                v.scalar_tensor_tensor(out=o, in0=zg[f][:, :], scalar=1.0, in1=o, op0=ALU.add, op1=ALU.mult)\
                    .then_inc(w_ready, 1)
                dve.wait_ge(w_ready, count(b, 2, f + 1))
                v.scalar_tensor_tensor(out=o, in0=o, scalar=0.5, in1=nn[:, :], op0=ALU.mult, op1=ALU.add)\
                    .then_inc(o_ready, 1)

            def turn_out(b, f):
                dve.wait_ge(o_ready, count(b, 2, f + 1))
                wait(dve, out_ready, count(nxt(b, -1), 2, f + 1))
                v.transpose(turned[f][:, :], oo[f][:, :]).then_inc(ot_ready, 1)

            def h_rest(n):
                i = par(n)
                if index_known(n) == 0:
                    return
                dve.wait_ge(hh_ready, count(n, 1, 1))
                v.tensor_tensor(hl[i][:, :, :], h_next[:, :, :], hh[i][:, :, :], ALU.subtract).then_inc(hl_ready, 1)

            def mask_turn(n, j):
                if j == 0:
                    arrived(dve, adj_in, n, NB)
                wait(dve, a_ready, count(n, NB, j + 1 - NB))
                v.transpose(mask_t[:, j, :], adj_t[par(n)][:, :, :, j]).then_inc(mask_ready, 1)

            def s_split(n):
                dve.wait_ge(sf_ready, count(n, 1, 1))
                v.tensor_copy(shi[:, :], sf[:, :]).then_inc(shi_ready, 1)
                dve.wait_ge(shi_ready, count(n, 1, 1))
                for dst, col, part, lin, done in ((s_right, 0, lin_right, sr_lin, s_right_ready),
                                                  (s_left, 3, lin_left, sl_lin, s_left_ready)):
                    dve.wait_ge(lin, count(n, 1, 1))
                    wait(dve, dist_ready, count(n, NB))
                    v.scalar_tensor_tensor(out=dst[:, :], in0=shi[:, :].bitcast(F32), scalar=rows[:, col:col + 1],
                                           in1=part[:, :], op0=ALU.mult, op1=ALU.add).then_inc(done, 1)

            def message_scale(n):
                for m in range(2):
                    dve.wait_ge(m_ready, count(n, 2, m + 1))
                    wait(dve, ml_ready, count(nxt(n, -1), 2, m + 1))
                    v.tensor_tensor(mg[m][:, :, :], pu[1 + m][:, :].rearrange("p (a d) -> p a d", d=D),
                                    msg_inv[:, :, :], ALU.mult).then_inc(m_scaled, 1)
                    dve.wait_ge(m_scaled, count(n, 2, m + 1))
                    v.tensor_tensor(mg[m][:, :, :], mg[m][:, :, :], msg_bias[:, :, :], ALU.add).then_inc(m_biased, 1)

            def message_rest(n, m):
                dve.wait_ge(mh_ready, count(n, 2, m + 1))
                v.scalar_tensor_tensor(out=ml[:, 2 * m:2 * m + 2, :].rearrange("p a d -> p (a d)"),
                                       in0=mg[m][:, :, :].rearrange("p a d -> p (a d)"), scalar=0.0,
                                       in1=mh[:, 2 * m:2 * m + 2, :].bitcast(F32).rearrange("p a d -> p (a d)"),
                                       op0=ALU.max, op1=ALU.subtract).then_inc(ml_ready, 1)

            def mask(n, m):
                dve.wait_ge(mask_ready, count(n, NB, m + 1))
                dve.wait_ge(ex_ready, count(n, NB, m + 1))
                v.tensor_tensor(ex[m % 2][:, :], ex[m % 2][:, :], mask_t[:, m, :], ALU.mult).then_inc(a_ready, 1)

            def conv_sum(n):
                i = par(n)
                arrived(dve, xc_in, n)
                dve.wait_ge(hs_ready, count(n, 1, 1))
                v.scalar_tensor_tensor(out=xc_t[i][:, :, :].rearrange("p k n -> p (k n)"),
                                       in0=hs[i][:, :, :].rearrange("p k n -> p (k n)"), scalar=1.0 / H_SCALE,
                                       in1=xc_t[i][:, :, :].rearrange("p k n -> p (k n)"),
                                       op0=ALU.mult, op1=ALU.add).then_inc(ct_ready, 1)

            def conv_rest(n):
                i = par(n)
                dve.wait_ge(ch_ready, count(n, 1, 1))
                v.scalar_tensor_tensor(out=cl[i][:, :, :].rearrange("p k n -> p (k n)"),
                                       in0=xc_t[i][:, :, :].rearrange("p k n -> p (k n)"), scalar=0.0,
                                       in1=ch[i][:, :, :].bitcast(F32).rearrange("p k n -> p (k n)"),
                                       op0=ALU.max, op1=ALU.subtract).then_inc(cl_ready, 1)

            def both(p, b, n):
                if b is not None:
                    conv_rest(b)
                    message_split(b)
                if p is not None:
                    gate_end(p, 1)
                if n is not None:
                    h_rest(n)
                if p is not None:
                    turn_out(p, 1)
                if n is not None:
                    for j in range(NB):
                        mask_turn(n, j)
                if b is not None:
                    gate_mul(b, 0)
                if n is not None:
                    s_split(n)
                    message_scale(n)
                if b is not None:
                    gate_add(b, 0)
                if n is not None:
                    message_rest(n, 0)
                    mask(n, 0)
                    message_rest(n, 1)
                if b is not None:
                    gate_end(b, 0)
                if n is not None:
                    mask(n, 1)
                if b is not None:
                    turn_out(b, 0)
                    gate_mul(b, 1)
                if n is not None:
                    conv_sum(n)
                    mask(n, 2)
                    mask(n, 3)
                if b is not None:
                    gate_add(b, 1)

            run(dve, both)

        @block.tensor
        def _(pe):
            mm = nc.tensor.matmul

            def of_block(t, j):
                return t[:, j::NB]

            def gate(b, k):
                i = par(b)
                f = 1 if k >= R1 else 0
                o = {R0: 0, R1: 1, Z0: 2, Z1: 3, HN0: 4, HN1: 5, IN0: 4, IN1: 5}[k]
                cols = slice(o * P, (o + 1) * P)
                bank = pg[BANK[k]][:, :]
                steps = []
                if k not in (IN0, IN1):
                    steps += [(w[:, c, cols], h[i][:, c, :]) for c in range(KD)
                              for w, h in ((whh, hh), (whh, hl), (whl, hh))]
                if k not in (HN0, HN1):
                    steps += [(w[:, c, cols], t[:, c, :]) for c in range(KD)
                              for w, t in ((wih, ch[i]), (wih, cl[i]), (wil, ch[i]))]
                    message = len(steps)
                    steps += [(w[:, KD + c, cols], t[:, c, :]) for c in range(KD)
                              for w, t in ((wih, nh), (wih, nl), (wil, nh))]
                bank_free(pe, b, k)
                for j, (w, t) in enumerate(steps):
                    if k == R0 and j == 3 * KD:
                        pe.wait_ge(cl_ready, count(b, 1, 1))
                    if k == R0 and j >= message and (j - message) % 3 == 0:
                        pe.wait_ge(nmp_l, count(b, KD, (j - message) // 3 + 1))
                    last = mm(bank, w, t, start=(j == 0), stop=(j == len(steps) - 1))
                last.then_inc(gate_ready, 1)

            def distance_rows_mm(n):
                i = par(n)
                pe.wait_ge(hl_ready, count(n, 1, 1))
                wait(pe, ex_ready, count(n, NB))
                steps = [(w[:, c, :], h[i][:, c, :]) for c in range(KD) for w, h in ((wsh, hh), (wsh, hl), (wsl, hh))]
                for j, (w, t) in enumerate(steps):
                    last = mm(pu[0][:, :], w, t, start=(j == 0), stop=(j == len(steps) - 1))
                last.then_inc(s_ready, 1)

            def messages(n):
                i = par(n)
                for m in range(NB):
                    steps = [(of_block(h[i][:, c, :], m), w[:, c, :]) for c in range(KD)
                             for h, w in ((hh, wmh), (hh, wml), (hl, wmh))]
                    for j, (h, w) in enumerate(steps):
                        last = mm(pu[1 + m // 2][:, (m % 2) * D:(m % 2 + 1) * D], h, w,
                                  start=(j == 0), stop=(j == len(steps) - 1))
                    if m % 2:
                        last.then_inc(m_ready, 1)

            def distance(n, m):
                if m == 0:
                    pe.wait_ge(s_left_ready, count(n, 1, 1))
                elif m == 1:
                    pe.wait_ge(m_scaled, count(n, 2, 1))
                else:
                    pe.wait_ge(ex_ready, count(n, NB, m - 1))
                mm(pu[m % 2][:, :], of_block(s_left, m), s_right[:, :], start=True, stop=True).then_inc(dist_ready, 1)

            def aggregate(n, m):
                if m == 0:
                    pe.wait_ge(ml_ready, count(n, 2, 2))
                    wait(pe, nmp_l, count(n, KD))
                pe.wait_ge(al_ready, count(n, NB, m + 1))
                for c in range(KD):
                    cols = slice(c * P, (c + 1) * P)
                    for j, (w, t) in enumerate(((mh, ah), (mh, al), (ml, ah))):
                        last = mm(px[c][:, :], w[:, m, cols], t[m % 2][:, :],
                                  start=(m == 0 and j == 0), stop=(m == NB - 1 and j == 2))
                last.then_inc(x_step, 1)

            def both(p, b, n):
                if b is not None:
                    gate(b, R0)
                if b is not None:
                    gate(b, HN0)
                if b is not None:
                    gate(b, Z0)
                if n is not None:
                    distance_rows_mm(n)
                    messages(n)
                if b is not None:
                    gate(b, IN0)
                if n is not None:
                    distance(n, 0)
                if b is not None:
                    gate(b, R1)
                if n is not None:
                    distance(n, 1)
                if b is not None:
                    gate(b, HN1)
                if n is not None:
                    distance(n, 2)
                    aggregate(n, 0)
                if b is not None:
                    gate(b, Z1)
                if n is not None:
                    aggregate(n, 1)
                    distance(n, 3)
                if b is not None:
                    gate(b, IN1)
                if n is not None:
                    aggregate(n, 2)
                    aggregate(n, 3)

            run(pe, both)


_NAMES = {
    "x": "x", "adj": "adj", "L0_gnn_w_se": "w_se", "L0_gnn_b_se": "b_se", "L0_gnn_conv1_w": "conv1_w",
    "L0_gnn_bn1_g": "bn1_g", "L0_gnn_bn1_b": "bn1_b", "L0_gnn_bn1_m": "bn1_m", "L0_gnn_bn1_v": "bn1_v",
    "L0_gnn_conv2_w": "conv2_w", "L0_gnn_bn2_g": "bn2_g", "L0_gnn_bn2_b": "bn2_b", "L0_gnn_bn2_m": "bn2_m",
    "L0_gnn_bn2_v": "bn2_v", "L0_gnn_w_msg": "w_msg", "L0_gnn_b_msg": "b_msg", "L0_gnn_w_ih": "w_ih",
    "L0_gnn_b_ih": "b_ih", "L0_gnn_w_hh": "w_hh", "L0_gnn_b_hh": "b_hh",
}


def build(nc, io, out):
    scratch = nc.dram_tensor("conv_scratch", (B, KD, P, N), F32, kind="Internal").ap()
    with ExitStack() as ctx:
        shared = {
            "ident": ctx.enter_context(nc.sbuf_tensor("ident", [P, P], F32)),
            "h_scratch": nc.dram_tensor("h_scratch", (B, KD, P, N), F32, kind="Internal").ap(),
        }
        with ExitStack() as early:
            shared["input_side"] = allocate(nc, early, INPUT_SIDE)
        shared["gates"] = gate_constants(nc, ctx)
        shared["co_room"] = ctx.enter_context(nc.sbuf_tensor("co_room", [P, KD * G * N], F32))
        for name in ("h_in", "adj_in0", "hs_ready", "hh_ready", "hl_ready"):
            shared[name] = ctx.enter_context(nc.semaphore("gate_" + name))
        shared["stored"] = [ctx.enter_context(nc.semaphore(f"stored{i}")) for i in range(KD)]
        with ExitStack() as early:
            shared["first"] = allocate(nc, early, FIRST)
        convolution_phase(nc, io, scratch, shared)
        gate_phase(nc, io, scratch, shared, out)


def kernel(**inputs):
    import concourse.bacc as bacc
    from concourse.bass_utils import run_bass_kernel_spmd

    nc = bacc.Bacc("TRN2", target_bir_lowering=False, num_devices=1)
    arrays = {f"in_{short}": np.ascontiguousarray(inputs[name]) for name, short in _NAMES.items()}
    arrays["in_ident"] = np.eye(P, dtype=np.float32)
    arrays["in_rows"] = distance_rows()
    io = {name[3:]: nc.dram_tensor(name, a.shape, mybir.dt.from_np(a.dtype), kind="ExternalInput").ap()
          for name, a in arrays.items()}
    out = nc.dram_tensor("out_y", (B, N, D), F32, kind="ExternalOutput").ap()
    build(nc, io, out)
    result = run_bass_kernel_spmd(nc, [arrays], core_ids=[0])
    return result.results[0]["out_y"]
```
